# Optimizing a Trainium2 kernel written in Bass

```python
import numpy as np
import jax
import jax.numpy as jnp

def _softmax(x, axis=-1):
    return jax.nn.softmax(x, axis=axis)
def _gelu(x):
    return jax.nn.gelu(x, approximate=True)
def _silu(x):
    return jax.nn.silu(x)
def _sigmoid(x):
    return jax.nn.sigmoid(x)
def _layernorm(x, axis=-1, eps=1e-5):
    m = jnp.mean(x, axis=axis, keepdims=True)
    v = jnp.var(x, axis=axis, keepdims=True)
    return (x - m) / jnp.sqrt(v + eps)
def _scatter_add(tgt, idx, src, axis=0):
    return tgt.at[idx].add(src)
def _segment_sum(src, seg, n):
    return jax.ops.segment_sum(src, seg, n)

kernel_name = 'mk_vit_tower_d1_tok_img768_9ef5e4'

def setup_inputs(seed: int = 0):
    np.random.seed(seed)
    _w = jnp.asarray
    def _rec_inputs():
        import jax
        import jax.numpy as jnp
        _rk = jax.random.key(seed)
        x = (-0.00117387 + 1.00025 * jax.random.normal(jax.random.fold_in(_rk, 1), (4, 3, 224, 224), jnp.float32))
        return x
    x = _rec_inputs()
    def _L0_tok_setup():
        import jax, jax.numpy as jnp
        import numpy as np
        import math
        LN_EPS = 1e-05
        EPS = 1e-08

        def _unfold3(x, stride):
            B, C, H, W = x.shape
            xp = jnp.pad(x, ((0, 0), (0, 0), (1, 1), (1, 1)))
            Ho = (H + 2 - 3) // stride + 1
            Wo = (W + 2 - 3) // stride + 1
            pats = [xp[:, :, i:i + stride * (Ho - 1) + 1:stride, j:j + stride * (Wo - 1) + 1:stride] for i in range(3) for j in range(3)]
            out = jnp.stack(pats, axis=2)
            return out.reshape(B, C * 9, Ho * Wo)

        def _ln(x, g, b):
            mu = jnp.mean(x, axis=-1, keepdims=True)
            var = jnp.mean((x - mu) ** 2, axis=-1, keepdims=True)
            return (x - mu) * jax.lax.rsqrt(var + LN_EPS) * g + b

        def _prm_exp(x, w):
            m = w.shape[0]
            xd = jnp.sum(x * x, axis=-1, keepdims=True) / 2.0
            wtx = jnp.einsum('bte,me->btm', x, w)
            return jnp.exp(wtx - xd) / math.sqrt(m)

        def _performer(x, kqv_w, kqv_b, pw, pb, g1, b1, g2, b2, m1w, m1b, m2w, m2b, w):
            h = _ln(x, g1, b1)
            kqv = h @ kqv_w.T + kqv_b
            k, q, v = jnp.split(kqv, 3, axis=-1)
            kp = _prm_exp(k, w)
            qp = _prm_exp(q, w)
            D = jnp.einsum('btm,bm->bt', qp, kp.sum(axis=1))[..., None]
            kptv = jnp.einsum('btn,btm->bnm', v, kp)
            y = jnp.einsum('btm,bnm->btn', qp, kptv) / (D + EPS)
            y = v + (y @ pw.T + pb)
            h2 = _ln(y, g2, b2)
            mlp = jax.nn.gelu(h2 @ m1w.T + m1b, approximate=False) @ m2w.T + m2b
            return y + mlp

        def _forward(x, p1_kqv_w, p1_kqv_b, p1_proj_w, p1_proj_b, p1_n1_g, p1_n1_b, p1_n2_g, p1_n2_b, p1_m1_w, p1_m1_b, p1_m2_w, p1_m2_b, p1_w, p2_kqv_w, p2_kqv_b, p2_proj_w, p2_proj_b, p2_n1_g, p2_n1_b, p2_n2_g, p2_n2_b, p2_m1_w, p2_m1_b, p2_m2_w, p2_m2_b, p2_w, proj_w, proj_b):
            t = _unfold3(x, 1).transpose(0, 2, 1)
            t = _performer(t, p1_kqv_w, p1_kqv_b, p1_proj_w, p1_proj_b, p1_n1_g, p1_n1_b, p1_n2_g, p1_n2_b, p1_m1_w, p1_m1_b, p1_m2_w, p1_m2_b, p1_w)
            B, N, C = t.shape
            s = int(math.isqrt(N))
            t = t.transpose(0, 2, 1).reshape(B, C, s, s)
            t = _unfold3(t, 2).transpose(0, 2, 1)
            t = _performer(t, p2_kqv_w, p2_kqv_b, p2_proj_w, p2_proj_b, p2_n1_g, p2_n1_b, p2_n2_g, p2_n2_b, p2_m1_w, p2_m1_b, p2_m2_w, p2_m2_b, p2_w)
            B, N, C = t.shape
            s = int(math.isqrt(N))
            t = t.transpose(0, 2, 1).reshape(B, C, s, s)
            t = _unfold3(t, 2).transpose(0, 2, 1)
            return t @ proj_w.T + proj_b
        key = jax.random.key(seed)
        ks = iter(jax.random.split(key, 40))

        def rn(shape, scale=0.02):
            return jax.random.normal(next(ks), shape, dtype=jnp.float32) * scale
        EMB, M = (64, 32)
        inp = {'x': jax.random.normal(next(ks), (8, 3, 224, 224), dtype=jnp.float32)}
        for pfx, dim in (('p1', 27), ('p2', 576)):
            inp[f'{pfx}_kqv_w'] = rn((3 * EMB, dim))
            inp[f'{pfx}_kqv_b'] = jnp.zeros((3 * EMB,), jnp.float32)
            inp[f'{pfx}_proj_w'] = rn((EMB, EMB))
            inp[f'{pfx}_proj_b'] = jnp.zeros((EMB,), jnp.float32)
            inp[f'{pfx}_n1_g'] = jnp.ones((dim,), jnp.float32)
            inp[f'{pfx}_n1_b'] = jnp.zeros((dim,), jnp.float32)
            inp[f'{pfx}_n2_g'] = jnp.ones((EMB,), jnp.float32)
            inp[f'{pfx}_n2_b'] = jnp.zeros((EMB,), jnp.float32)
            inp[f'{pfx}_m1_w'] = rn((EMB, EMB))
            inp[f'{pfx}_m1_b'] = jnp.zeros((EMB,), jnp.float32)
            inp[f'{pfx}_m2_w'] = rn((EMB, EMB))
            inp[f'{pfx}_m2_b'] = jnp.zeros((EMB,), jnp.float32)
            inp[f'{pfx}_w'] = jax.random.normal(next(ks), (M, EMB), dtype=jnp.float32)
        inp['proj_w'] = rn((768, 576))
        inp['proj_b'] = jnp.zeros((768,), jnp.float32)
        return inp
    _L0_tok_all = _L0_tok_setup()
    _L0_tok_in = {k: v for k, v in _L0_tok_all.items() if k in ('p1_kqv_w', 'p1_kqv_b', 'p1_proj_w', 'p1_proj_b', 'p1_n1_g', 'p1_n1_b', 'p1_n2_g', 'p1_n2_b', 'p1_m1_w', 'p1_m1_b', 'p1_m2_w', 'p1_m2_b', 'p1_w', 'p2_kqv_w', 'p2_kqv_b', 'p2_proj_w', 'p2_proj_b', 'p2_n1_g', 'p2_n1_b', 'p2_n2_g', 'p2_n2_b', 'p2_m1_w', 'p2_m1_b', 'p2_m2_w', 'p2_m2_b', 'p2_w', 'proj_w', 'proj_b', )}
    del _L0_tok_all

    def _L0_attn_setup():
        import jax, jax.numpy as jnp
        import numpy as np
        from jax import lax
        BATCH, L, D, N = (2, 4096, 768, 16)

        def _ssm_forward(x, A, W_B, b_B, W_C, b_C, W_D, b_D, p_Delta):
            Bproj = x @ W_B + b_B
            Cproj = x @ W_C + b_C
            delta = jax.nn.softplus(x @ W_D + b_D + p_Delta)
            dA = delta[..., None] * A
            A_bar = jnp.exp(dA)
            B_bar = (A_bar - A) / dA * delta[..., None] * Bproj[:, :, None, :]

            def step(h, inp):
                a, b, c, xl = inp
                h = a * h + b * xl[..., None]
                y = jnp.einsum('bn,bdn->bd', c, h)
                return (h, y)
            h0 = jnp.zeros((x.shape[0], D, N), dtype=x.dtype)
            xs = (jnp.moveaxis(A_bar, 1, 0), jnp.moveaxis(B_bar, 1, 0), jnp.moveaxis(Cproj, 1, 0), jnp.moveaxis(x, 1, 0))
            _, ys = lax.scan(step, h0, xs)
            return jnp.moveaxis(ys, 0, 1)
        key = jax.random.key(seed)
        ks = jax.random.split(key, 8)
        x = jax.random.normal(ks[0], (BATCH, L, D), dtype=jnp.float32)
        A = -jnp.tile((jnp.arange(N, dtype=jnp.float32) + 1.0)[None, :], (D, 1))
        s = 0.02
        W_B = jax.random.normal(ks[1], (D, N), dtype=jnp.float32) * s
        b_B = jnp.zeros((N,), dtype=jnp.float32)
        W_C = jax.random.normal(ks[2], (D, N), dtype=jnp.float32) * s
        b_C = jnp.zeros((N,), dtype=jnp.float32)
        W_D = jax.random.normal(ks[3], (D, 1), dtype=jnp.float32) * s
        b_D = jnp.zeros((1,), dtype=jnp.float32)
        p_Delta = jax.random.normal(ks[4], (D,), dtype=jnp.float32) * 0.1
        return {'x': x, 'A': A, 'W_B': W_B, 'b_B': b_B, 'W_C': W_C, 'b_C': b_C, 'W_D': W_D, 'b_D': b_D, 'p_Delta': p_Delta}
    _L0_attn_all = _L0_attn_setup()
    _L0_attn_in = {k: v for k, v in _L0_attn_all.items() if k in ('A', 'W_B', 'b_B', 'W_C', 'b_C', 'W_D', 'b_D', 'p_Delta', )}
    del _L0_attn_all

    def _L0_ffn_setup():
        import jax, jax.numpy as jnp
        import numpy as np
        H = 768
        R = 64
        E = 8
        B, S = (8, 2048)
        key = jax.random.key(seed)
        ks = jax.random.split(key, 10)
        s_in = 1.0 / np.sqrt(H)
        s_r = 1.0 / np.sqrt(R)
        return {'x': jax.random.normal(ks[0], (B, S, H), dtype=jnp.float32), 'enc_w': jax.random.uniform(ks[1], (H, R), jnp.float32, -s_in, s_in), 'enc_b': jax.random.uniform(ks[2], (R,), jnp.float32, -s_in, s_in), 'sw_w': jax.random.uniform(ks[3], (R, E), jnp.float32, -s_r, s_r), 'sw_b': jax.random.uniform(ks[4], (E,), jnp.float32, -s_r, s_r), 'w1': jax.random.uniform(ks[5], (E, H, R), jnp.float32, -s_in, s_in), 'b1': jax.random.uniform(ks[6], (E, R), jnp.float32, -s_in, s_in), 'w2': jax.random.uniform(ks[7], (E, R, H), jnp.float32, -s_r, s_r), 'b2': jax.random.uniform(ks[8], (E, H), jnp.float32, -s_r, s_r)}
    _L0_ffn_all = _L0_ffn_setup()
    _L0_ffn_in = {k: v for k, v in _L0_ffn_all.items() if k in ('enc_w', 'enc_b', 'sw_w', 'sw_b', 'w1', 'b1', 'w2', 'b2', )}
    del _L0_ffn_all

    return {
        "x": x,
        "L0_tok_p1_kqv_w": _L0_tok_in["p1_kqv_w"],
        "L0_tok_p1_kqv_b": _L0_tok_in["p1_kqv_b"],
        "L0_tok_p1_proj_w": _L0_tok_in["p1_proj_w"],
        "L0_tok_p1_proj_b": _L0_tok_in["p1_proj_b"],
        "L0_tok_p1_n1_g": _L0_tok_in["p1_n1_g"],
        "L0_tok_p1_n1_b": _L0_tok_in["p1_n1_b"],
        "L0_tok_p1_n2_g": _L0_tok_in["p1_n2_g"],
        "L0_tok_p1_n2_b": _L0_tok_in["p1_n2_b"],
        "L0_tok_p1_m1_w": _L0_tok_in["p1_m1_w"],
        "L0_tok_p1_m1_b": _L0_tok_in["p1_m1_b"],
        "L0_tok_p1_m2_w": _L0_tok_in["p1_m2_w"],
        "L0_tok_p1_m2_b": _L0_tok_in["p1_m2_b"],
        "L0_tok_p1_w": _L0_tok_in["p1_w"],
        "L0_tok_p2_kqv_w": _L0_tok_in["p2_kqv_w"],
        "L0_tok_p2_kqv_b": _L0_tok_in["p2_kqv_b"],
        "L0_tok_p2_proj_w": _L0_tok_in["p2_proj_w"],
        "L0_tok_p2_proj_b": _L0_tok_in["p2_proj_b"],
        "L0_tok_p2_n1_g": _L0_tok_in["p2_n1_g"],
        "L0_tok_p2_n1_b": _L0_tok_in["p2_n1_b"],
        "L0_tok_p2_n2_g": _L0_tok_in["p2_n2_g"],
        "L0_tok_p2_n2_b": _L0_tok_in["p2_n2_b"],
        "L0_tok_p2_m1_w": _L0_tok_in["p2_m1_w"],
        "L0_tok_p2_m1_b": _L0_tok_in["p2_m1_b"],
        "L0_tok_p2_m2_w": _L0_tok_in["p2_m2_w"],
        "L0_tok_p2_m2_b": _L0_tok_in["p2_m2_b"],
        "L0_tok_p2_w": _L0_tok_in["p2_w"],
        "L0_tok_proj_w": _L0_tok_in["proj_w"],
        "L0_tok_proj_b": _L0_tok_in["proj_b"],
        "L0_attn_A": _L0_attn_in["A"],
        "L0_attn_W_B": _L0_attn_in["W_B"],
        "L0_attn_b_B": _L0_attn_in["b_B"],
        "L0_attn_W_C": _L0_attn_in["W_C"],
        "L0_attn_b_C": _L0_attn_in["b_C"],
        "L0_attn_W_D": _L0_attn_in["W_D"],
        "L0_attn_b_D": _L0_attn_in["b_D"],
        "L0_attn_p_Delta": _L0_attn_in["p_Delta"],
        "L0_ffn_enc_w": _L0_ffn_in["enc_w"],
        "L0_ffn_enc_b": _L0_ffn_in["enc_b"],
        "L0_ffn_sw_w": _L0_ffn_in["sw_w"],
        "L0_ffn_sw_b": _L0_ffn_in["sw_b"],
        "L0_ffn_w1": _L0_ffn_in["w1"],
        "L0_ffn_b1": _L0_ffn_in["b1"],
        "L0_ffn_w2": _L0_ffn_in["w2"],
        "L0_ffn_b2": _L0_ffn_in["b2"],
    }

def reference(x, L0_tok_p1_kqv_w, L0_tok_p1_kqv_b, L0_tok_p1_proj_w, L0_tok_p1_proj_b, L0_tok_p1_n1_g, L0_tok_p1_n1_b, L0_tok_p1_n2_g, L0_tok_p1_n2_b, L0_tok_p1_m1_w, L0_tok_p1_m1_b, L0_tok_p1_m2_w, L0_tok_p1_m2_b, L0_tok_p1_w, L0_tok_p2_kqv_w, L0_tok_p2_kqv_b, L0_tok_p2_proj_w, L0_tok_p2_proj_b, L0_tok_p2_n1_g, L0_tok_p2_n1_b, L0_tok_p2_n2_g, L0_tok_p2_n2_b, L0_tok_p2_m1_w, L0_tok_p2_m1_b, L0_tok_p2_m2_w, L0_tok_p2_m2_b, L0_tok_p2_w, L0_tok_proj_w, L0_tok_proj_b, L0_attn_A, L0_attn_W_B, L0_attn_b_B, L0_attn_W_C, L0_attn_b_C, L0_attn_W_D, L0_attn_b_D, L0_attn_p_Delta, L0_ffn_enc_w, L0_ffn_enc_b, L0_ffn_sw_w, L0_ffn_sw_b, L0_ffn_w1, L0_ffn_b1, L0_ffn_w2, L0_ffn_b2):
    import jax
    import jax.numpy as jnp
    def _L0_tok_ref(x, p1_kqv_w, p1_kqv_b, p1_proj_w, p1_proj_b, p1_n1_g, p1_n1_b, p1_n2_g, p1_n2_b, p1_m1_w, p1_m1_b, p1_m2_w, p1_m2_b, p1_w, p2_kqv_w, p2_kqv_b, p2_proj_w, p2_proj_b, p2_n1_g, p2_n1_b, p2_n2_g, p2_n2_b, p2_m1_w, p2_m1_b, p2_m2_w, p2_m2_b, p2_w, proj_w, proj_b):
        import jax, jax.numpy as jnp
        import numpy as np
        import math
        LN_EPS = 1e-05
        EPS = 1e-08

        def _unfold3(x, stride):
            B, C, H, W = x.shape
            xp = jnp.pad(x, ((0, 0), (0, 0), (1, 1), (1, 1)))
            Ho = (H + 2 - 3) // stride + 1
            Wo = (W + 2 - 3) // stride + 1
            pats = [xp[:, :, i:i + stride * (Ho - 1) + 1:stride, j:j + stride * (Wo - 1) + 1:stride] for i in range(3) for j in range(3)]
            out = jnp.stack(pats, axis=2)
            return out.reshape(B, C * 9, Ho * Wo)

        def _ln(x, g, b):
            mu = jnp.mean(x, axis=-1, keepdims=True)
            var = jnp.mean((x - mu) ** 2, axis=-1, keepdims=True)
            return (x - mu) * jax.lax.rsqrt(var + LN_EPS) * g + b

        def _prm_exp(x, w):
            m = w.shape[0]
            xd = jnp.sum(x * x, axis=-1, keepdims=True) / 2.0
            wtx = jnp.einsum('bte,me->btm', x, w)
            return jnp.exp(wtx - xd) / math.sqrt(m)

        def _performer(x, kqv_w, kqv_b, pw, pb, g1, b1, g2, b2, m1w, m1b, m2w, m2b, w):
            h = _ln(x, g1, b1)
            kqv = h @ kqv_w.T + kqv_b
            k, q, v = jnp.split(kqv, 3, axis=-1)
            kp = _prm_exp(k, w)
            qp = _prm_exp(q, w)
            D = jnp.einsum('btm,bm->bt', qp, kp.sum(axis=1))[..., None]
            kptv = jnp.einsum('btn,btm->bnm', v, kp)
            y = jnp.einsum('btm,bnm->btn', qp, kptv) / (D + EPS)
            y = v + (y @ pw.T + pb)
            h2 = _ln(y, g2, b2)
            mlp = jax.nn.gelu(h2 @ m1w.T + m1b, approximate=False) @ m2w.T + m2b
            return y + mlp

        def _forward(x, p1_kqv_w, p1_kqv_b, p1_proj_w, p1_proj_b, p1_n1_g, p1_n1_b, p1_n2_g, p1_n2_b, p1_m1_w, p1_m1_b, p1_m2_w, p1_m2_b, p1_w, p2_kqv_w, p2_kqv_b, p2_proj_w, p2_proj_b, p2_n1_g, p2_n1_b, p2_n2_g, p2_n2_b, p2_m1_w, p2_m1_b, p2_m2_w, p2_m2_b, p2_w, proj_w, proj_b):
            t = _unfold3(x, 1).transpose(0, 2, 1)
            t = _performer(t, p1_kqv_w, p1_kqv_b, p1_proj_w, p1_proj_b, p1_n1_g, p1_n1_b, p1_n2_g, p1_n2_b, p1_m1_w, p1_m1_b, p1_m2_w, p1_m2_b, p1_w)
            B, N, C = t.shape
            s = int(math.isqrt(N))
            t = t.transpose(0, 2, 1).reshape(B, C, s, s)
            t = _unfold3(t, 2).transpose(0, 2, 1)
            t = _performer(t, p2_kqv_w, p2_kqv_b, p2_proj_w, p2_proj_b, p2_n1_g, p2_n1_b, p2_n2_g, p2_n2_b, p2_m1_w, p2_m1_b, p2_m2_w, p2_m2_b, p2_w)
            B, N, C = t.shape
            s = int(math.isqrt(N))
            t = t.transpose(0, 2, 1).reshape(B, C, s, s)
            t = _unfold3(t, 2).transpose(0, 2, 1)
            return t @ proj_w.T + proj_b
        return _forward(x, p1_kqv_w, p1_kqv_b, p1_proj_w, p1_proj_b, p1_n1_g, p1_n1_b, p1_n2_g, p1_n2_b, p1_m1_w, p1_m1_b, p1_m2_w, p1_m2_b, p1_w, p2_kqv_w, p2_kqv_b, p2_proj_w, p2_proj_b, p2_n1_g, p2_n1_b, p2_n2_g, p2_n2_b, p2_m1_w, p2_m1_b, p2_m2_w, p2_m2_b, p2_w, proj_w, proj_b)

    def _L0_attn_ref(x, A, W_B, b_B, W_C, b_C, W_D, b_D, p_Delta):
        import jax, jax.numpy as jnp
        import numpy as np
        from jax import lax
        BATCH, L, D, N = (2, 4096, 768, 16)

        def _ssm_forward(x, A, W_B, b_B, W_C, b_C, W_D, b_D, p_Delta):
            Bproj = x @ W_B + b_B
            Cproj = x @ W_C + b_C
            delta = jax.nn.softplus(x @ W_D + b_D + p_Delta)
            dA = delta[..., None] * A
            A_bar = jnp.exp(dA)
            B_bar = (A_bar - A) / dA * delta[..., None] * Bproj[:, :, None, :]

            def step(h, inp):
                a, b, c, xl = inp
                h = a * h + b * xl[..., None]
                y = jnp.einsum('bn,bdn->bd', c, h)
                return (h, y)
            h0 = jnp.zeros((x.shape[0], D, N), dtype=x.dtype)
            xs = (jnp.moveaxis(A_bar, 1, 0), jnp.moveaxis(B_bar, 1, 0), jnp.moveaxis(Cproj, 1, 0), jnp.moveaxis(x, 1, 0))
            _, ys = lax.scan(step, h0, xs)
            return jnp.moveaxis(ys, 0, 1)
        return _ssm_forward(x, A, W_B, b_B, W_C, b_C, W_D, b_D, p_Delta)

    def _L0_ffn_ref(x, enc_w, enc_b, sw_w, sw_b, w1, b1, w2, b2):
        import jax, jax.numpy as jnp
        import numpy as np
        H = 768
        R = 64
        E = 8
        B, S = (8, 2048)
        b, s, d = x.shape
        xt = x.reshape(-1, d)
        x_enc = xt @ enc_w + enc_b
        route_prob = jax.nn.softmax(x_enc @ sw_w + sw_b, axis=-1)
        route_prob_max = jnp.max(route_prob, axis=-1)
        routes = jnp.argmax(route_prob, axis=-1)
        onehot = jax.nn.one_hot(routes, E, dtype=xt.dtype)
        h = jnp.einsum('td,edr->ter', xt, w1) + b1[None]
        h = jax.nn.gelu(h, approximate=False)
        h = h * onehot[..., None]
        out = jnp.einsum('ter,erd->td', h, w2) + onehot @ b2
        out = out * route_prob_max[:, None]
        return out.reshape(b, s, d)

    h = _L0_tok_ref(x, L0_tok_p1_kqv_w, L0_tok_p1_kqv_b, L0_tok_p1_proj_w, L0_tok_p1_proj_b, L0_tok_p1_n1_g, L0_tok_p1_n1_b, L0_tok_p1_n2_g, L0_tok_p1_n2_b, L0_tok_p1_m1_w, L0_tok_p1_m1_b, L0_tok_p1_m2_w, L0_tok_p1_m2_b, L0_tok_p1_w, L0_tok_p2_kqv_w, L0_tok_p2_kqv_b, L0_tok_p2_proj_w, L0_tok_p2_proj_b, L0_tok_p2_n1_g, L0_tok_p2_n1_b, L0_tok_p2_n2_g, L0_tok_p2_n2_b, L0_tok_p2_m1_w, L0_tok_p2_m1_b, L0_tok_p2_m2_w, L0_tok_p2_m2_b, L0_tok_p2_w, L0_tok_proj_w, L0_tok_proj_b)
    h = h + _L0_attn_ref(_layernorm(h, axis=-1), L0_attn_A, L0_attn_W_B, L0_attn_b_B, L0_attn_W_C, L0_attn_b_C, L0_attn_W_D, L0_attn_b_D, L0_attn_p_Delta)
    h = h + _L0_ffn_ref(_layernorm(h, axis=-1), L0_ffn_enc_w, L0_ffn_enc_b, L0_ffn_sw_w, L0_ffn_sw_b, L0_ffn_w1, L0_ffn_b1, L0_ffn_w2, L0_ffn_b2)
    return h


_drawn_inputs = setup_inputs


def setup_inputs(seed=0):
    import zlib

    import numpy as np

    out = dict(_drawn_inputs(seed))
    spreads = {'L0_tok_p1_kqv_b': (0.0, 0.1),
     'L0_tok_p1_proj_b': (0.0, 0.1),
     'L0_tok_p1_n1_g': (1.0, 0.2),
     'L0_tok_p1_n1_b': (0.0, 0.1),
     'L0_tok_p1_n2_g': (1.0, 0.6),
     'L0_tok_p1_n2_b': (0.0, 0.8),
     'L0_tok_p1_m1_b': (0.0, 0.1),
     'L0_tok_p1_m2_b': (0.0, 0.1),
     'L0_tok_p2_kqv_b': (0.0, 0.1),
     'L0_tok_p2_proj_b': (0.0, 0.1),
     'L0_tok_p2_n1_g': (1.0, 0.2),
     'L0_tok_p2_n1_b': (0.0, 0.1),
     'L0_tok_p2_n2_g': (1.0, 0.6),
     'L0_tok_p2_n2_b': (0.0, 0.8),
     'L0_tok_p2_m1_b': (0.0, 0.1),
     'L0_tok_p2_m2_b': (0.0, 0.1),
     'L0_tok_proj_b': (0.0, 0.1),
     'L0_attn_b_B': (0.0, 0.1),
     'L0_attn_b_C': (0.0, 0.1)}
    factors = {'L0_tok_p1_w': 8.0,
     'L0_attn_p_Delta': 6.249,
     'L0_ffn_enc_b': 8.0,
     'L0_ffn_sw_b': 5.036,
     'L0_ffn_b1': 44.136,
     'L0_ffn_b2': 5.852}
    for name, (base, spread) in spreads.items():
        noise = np.random.default_rng([zlib.crc32(name.encode()), seed]).standard_normal(out[name].shape)
        drawn = base * np.exp(spread * noise) if base else spread * noise
        out[name] = jnp.asarray(drawn.astype(out[name].dtype))
    for name, factor in factors.items():
        out[name] = (out[name] * factor).astype(out[name].dtype)
    return out
```

```python
from contextlib import ExitStack

import numpy as np

import concourse.bass as bass
from concourse import mybir

F32 = mybir.dt.float32
ALU = mybir.AluOpType
ACT = mybir.ActivationFunctionType

B = 4
IMG = 224
G = 4
F1 = 27
E = 64
M = 32
XP = IMG + 2
XROWS = XP + 1
T = 448
CH = 112
NCH = T // CH
U = 4
R1 = T // IMG
GROWS = IMG // G
J1 = GROWS // (R1 * U)
LN_EPS = 1e-5
D_EPS = 1e-8
T1ROWS = IMG + 2


def one_pass(it, u=0):
    return it * U + u + 1 + U


def last_turn(it, u=0):
    return it * U + u + 1


def before(it, per=U):
    return it * per + U


def lead(eng, *sems):
    for s in sems:
        eng.sem_inc(s, U)


def performer1(nc, sem, x, w, c, t1, h_spill):
    with ExitStack() as ctx:
        def sb(name, shape):
            return ctx.enter_context(nc.sbuf_tensor(name, shape, F32))

        ps = ctx.enter_context(nc.psum_tensor("ps1", [128, 8, 512], F32))

        def bank(k, n=T, rows=128):
            return ps[0:rows, k, 0:n]

        def banks(k):
            return ps[:, k:k + 2, 0:T]

        ident = sb("ident", [128, 128])
        bd32 = sb("bd32", [128, 128])
        srep = sb("srep", [128, 128])
        cen1 = sb("cen1", [128, 128])
        mean27 = sb("mean27", [128, 128])
        jb64 = sb("jb64", [128, 128])
        pmask = sb("pmask", [128, 2, 2, 64])
        nh = sb("nh", [128, 2, 128])
        eps1 = sb("eps1", [128, 1])
        eps64 = sb("eps64", [128, 1])
        ic64 = sb("ic64", [64, 128])
        e27 = sb("e27", [1, 128])
        gain1 = sb("gain1", [32, 128])
        wt1 = sb("wt1", [32, 192])
        pb1 = sb("pb1", [1, 64])
        pw1 = sb("pw1", [64, 64])
        pwr1 = sb("pwr1", [64, 128])
        wfeat = sb("wfeat", [64, 32])
        m1bd = sb("m1bd", [128, 128])
        m2bd = sb("m2bd", [128, 128])
        g2 = sb("g2", [128, 1])
        b2 = sb("b2", [128, 1])
        m1b = sb("m1b", [128, 1])
        m2b = sb("m2b", [128, 1])
        w1r = sb("w1r", [128, 192])
        w1t = sb("w1t", [64, 3, 128])
        wvyt = sb("wvyt", [64, 128])
        wkb = sb("wkb", [128, 2, 2, 64])
        wqb = sb("wqb", [128, 2, 2, 64])
        wvyb = sb("wvyb", [128, 2, 2, 64])
        wvycb = sb("wvycb", [128, 2, 2, 64])
        wwk = sb("wwk", [128, 4, 32])
        wwq = sb("wwq", [128, 4, 32])
        p1x = sb("p1x", [128, 129])
        m1g = sb("m1g", [128, 128])
        m1bias = sb("m1bias", [128, 1])
        khacc = sb("khacc", [128, 128])
        khm = sb("khm", [128, 128])
        t1s = sb("t1s", [128, 128])
        t2s = sb("t2s", [128, 129])
        myb = sb("myb", [128, 2, 2, 64])
        mycb = sb("mycb", [128, 2, 2, 64])
        dwb = sb("dwb", [128, 128])
        zero = sb("zero", [128, B * E // 128, IMG])
        xt = sb("xt", [128, R1 * U * XP])
        sq = sb("sq", [128, U, T])
        rs = sb("rs", [128, U, T])
        h = sb("h", [128, U, T])
        ksq = sb("ksq", [128, U, 2, T])
        kp = sb("kp", [CH, U, NCH, 128])
        ht = sb("ht", [CH, U, NCH, 128])
        hb = sb("hb", [128, U, T])
        qsq = sb("qsq", [128, U, 2, T])
        qp = sb("qp", [128, U, T])
        qpn = sb("qpn", [128, U, T])
        yc = sb("yc", [128, U, 2, T])
        ycs = sb("ycs", [128, U, 2, T])
        rs2 = sb("rs2", [128, U, 2, T])
        gl = sb("gl", [128, U, 2, T])
        ob = sb("ob", [128, U, 2, T])

        loads = [(ident, c["ident"]), (bd32, c["bd32"]), (srep, c["srep"]), (cen1, c["cen1"]),
                 (mean27, c["mean27"]), (jb64, c["jb64"]), (pmask, c["pmask"]), (nh, c["nh"]),
                 (eps1, c["eps1"]), (eps64, c["eps64"]), (ic64, c["ic64"]), (e27, c["e27"]),
                 (gain1, w["gain1"]), (wt1, w["wt1"]), (pb1, w["pb1"]), (pw1, w["pw1"]),
                 (pwr1[:, 0:64], w["pwt1"]), (wfeat, w["wfeat1"]), (m1bd, w["m1bd1"]),
                 (m2bd, w["m2bd1"]), (g2, w["g21"]), (b2, w["b21"]), (m1b, w["m1b1"]),
                 (m2b, w["m2b1"]), (p1x[:, 128:129], c["e27col"])]

        s_w = sem("p1_weights_loaded")
        s_ones = sem("p1_ones_set")
        s_prep_mm = sem("p1_prep_products")
        s_prep = sem("p1_prep_copied")
        s_x = sem("p1_x_loaded")
        s_cen = sem("p1_centred")
        s_sq = sem("p1_squared")
        s_var = sem("p1_variance")
        s_ln = sem("p1_log_variance")
        s_rs = sem("p1_inverse_deviation")
        s_h = sem("p1_h_written")
        s_hst = sem("p1_h_stored")
        s_k = sem("p1_k_product")
        s_ksq = sem("p1_k_squared")
        s_tok = sem("p1_token_major")
        s_kp = sem("p1_kp_written")
        s_ht = sem("p1_ht_written")
        s_kh = sem("p1_kh_summed")
        s_khadd = sem("p1_kh_added")
        s_khm = sem("p1_kh_masked")
        s_khz = sem("p1_kh_cleared")
        s_t1 = sem("p1_t1_product")
        s_t1s = sem("p1_t1_copied")
        s_t2 = sem("p1_t2_product")
        s_t2s = sem("p1_t2_scaled")
        s_yw = sem("p1_y_weights")
        s_hl = [sem(f"p1_h_loaded_{u}") for u in range(U)]
        s_q = sem("p1_q_product")
        s_qsq = sem("p1_q_squared")
        s_lq = sem("p1_q_logits")
        s_qp = sem("p1_qp_written")
        s_d = sem("p1_denominator")
        s_de = sem("p1_denominator_guarded")
        s_dr = sem("p1_denominator_inverse")
        s_qpn = sem("p1_qp_normalised")
        s_yc = sem("p1_y_centred")
        s_ycb = sem("p1_y_copied")
        s_ycs = sem("p1_y_squared")
        s_var2 = sem("p1_y_variance")
        s_ln2 = sem("p1_y_log_variance")
        s_rs2 = sem("p1_y_inverse_deviation")
        s_h2 = sem("p1_h2_written")
        s_m1 = sem("p1_mlp_in")
        s_gl = sem("p1_gelu_written")
        s_o = sem("p1_out_product")
        s_ob = sem("p1_out_written")
        s_t1st = sem("p1_out_stored")
        s_zero = sem("p1_zero_set")

        block = ctx.enter_context(nc.Block())

        @block.sync
        def _(sp):
            lead(sp, s_hst)
            for dst, src in loads:
                sp.dma_start(dst[...] if not isinstance(dst, bass.AP) else dst, src).then_inc(s_w, 16)
            sp.wait_ge(s_ones, 1)
            with sp.Fori(0, B) as b:
                with sp.Fori(0, J1) as j:
                    it = b * J1 + j
                    sp.wait_ge(s_cen, before(it))
                    for g in range(G):
                        for ch in range(3):
                            row = GROWS * g + j * (R1 * U)
                            src = bass.AP(x.tensor, (b * 3 + ch) * (XROWS * XP) + row * XP,
                                          [[XP, 3], [1, 3], [1, R1 * U * XP]])
                            sp.dma_start(xt[32 * g + 9 * ch:32 * g + 9 * ch + 9, :], src).then_inc(s_x, 16)
                    for u in range(U):
                        sp.wait_ge(s_h, one_pass(it, u))
                        sp.dma_start(h_spill[it * U + u], h[:, u, :]).then_inc(s_hst, 16)
                with sp.Fori(0, J1) as j:
                    it = b * J1 + j
                    sp.wait_ge(s_hst, before(b + 1, J1 * U * 16))
                    for u in range(U):
                        sp.wait_ge(s_o, last_turn(it, u))
                        sp.dma_start(hb[:, u, :], h_spill[it * U + u]).then_inc(s_hl[u], 16)

        @block.gpsimd
        def _(pool):
            pool.memset(xt[:, :], 1.0).then_inc(s_ones, 1)
            pool.memset(zero[:, :, :], 0.0).then_inc(s_zero, 1)
            pool.wait_ge(s_zero, 1)
            pool.dma_start(bass.AP(t1.tensor, 0, [[T1ROWS * IMG, B * E], [1, IMG]]), zero[:, :, :]).then_inc(s_t1st, 16)
            with pool.Fori(0, B) as b:
                with pool.Fori(0, J1) as j:
                    it = b * J1 + j
                    for u in range(U):
                        pool.wait_ge(s_ob, one_pass(it, u))
                        for p in range(2):
                            for gl_ in range(2):
                                row = 1 + GROWS * (2 * p + gl_) + R1 * u + j * (R1 * U)
                                dst = bass.AP(t1.tensor, b * (E * T1ROWS * IMG) + row * IMG,
                                              [[T1ROWS * IMG, E], [1, T]])
                                pool.dma_start(dst, ob[64 * gl_:64 * gl_ + 64, u, p, :]).then_inc(s_t1st, 16)
            pool.wait_ge(s_t1st, 16 + B * J1 * U * 4 * 16)

        @block.tensor
        def _(pe):
            mm = nc.tensor.matmul
            lead(pe, s_cen, s_var, s_k, s_tok, s_q, s_lq, s_d, s_yc, s_var2, s_m1, s_o)
            pe.wait_ge(s_w, 16 * len(loads))
            mm(bank(0, 192), gain1[:, :], wt1[:, :], start=True, stop=True)
            for k in range(3):
                mm(ps[0:64, 1, 128 * k:128 * k + 128], wt1[:, 64 * k:64 * k + 64], gain1[:, :], start=True, stop=True)
            mm(bank(2, 128, 64), wt1[:, 128:192], gain1[:, :], start=True, stop=False)
            mm(bank(2, 128, 64), pb1[:, :], e27[:, :], start=False, stop=True)
            mm(bank(7, 1), m1bd[:, :], b2[:, :], start=True, stop=True)
            mm(bank(3, 64, 64), pw1[:, :], ic64[:, 64:128], start=True, stop=True).then_inc(s_prep_mm, 1)
            pe.wait_ge(s_prep, 4)
            mm(ps[:, 4, 0:32], w1t[:, 0, :], wfeat[:, :], start=True, stop=True)
            mm(ps[:, 4, 32:64], w1t[:, 1, :], wfeat[:, :], start=True, stop=True)
            mm(bank(5, 128), wvyt[:, :], ic64[:, :], start=True, stop=True)
            mm(bank(6, 128), w1t[:, 2, :], pwr1[:, :], start=True, stop=True).then_inc(s_prep_mm, 1)
            pe.wait_ge(s_prep, 17)
            with pe.Fori(0, B) as b:
                with pe.Fori(0, J1) as j:
                    it = b * J1 + j
                    pe.wait_ge(s_khadd, before(it, 1))
                    pe.wait_ge(s_ob, before(b, J1 * U))
                    pe.wait_ge(s_x, (it + 1) * (16 * G * 3))
                    for u in range(U):
                        rows = xt[:, u * R1 * XP:(u + 1) * R1 * XP].rearrange("p (r c) -> p r c", c=XP)
                        mm(ps[:, u, 0:T], cen1[:, :], rows[:, :, 0:IMG], start=True, stop=True).then_inc(s_cen, 1)
                    for u in range(U):
                        pe.wait_ge(s_sq, one_pass(it, u))
                        mm(bank(4 + u), mean27[:, :], sq[:, u, :], start=True, stop=True).then_inc(s_var, 1)
                    for u in range(U):
                        if u == 0:
                            pe.wait_ge(s_h, one_pass(it, U - 1))
                        for p in range(2):
                            last = mm(bank(2 * u + p), wkb[:, p], h[:, u, :], start=True, stop=True)
                        last.then_inc(s_k, 1)
                    for u in range(U):
                        pe.wait_ge(s_ksq, one_pass(it, u))
                        for ch in range(NCH):
                            cs = slice(ch * CH, ch * CH + CH)
                            o = ps[0:CH, 2 * u, 128 * ch:128 * ch + 128]
                            mm(o, h[:, u, cs], wwk[:, :, :], start=True, stop=False)
                            mm(o, ksq[:, u, 0, cs], nh[:, 0, :], start=False, stop=False)
                            mm(o, ksq[:, u, 1, cs], nh[:, 1, :], start=False, stop=True)
                        for ch in range(NCH):
                            cs = slice(ch * CH, ch * CH + CH)
                            last = mm(ps[0:CH, 2 * u + 1, 128 * ch:128 * ch + 128], h[:, u, cs], ident[:, :],
                                      start=True, stop=True)
                        last.then_inc(s_tok, 1)
                    for u in range(U):
                        pe.wait_ge(s_kp, one_pass(it, u))
                        pe.wait_ge(s_ht, one_pass(it, u))
                        for ch in range(NCH):
                            last = mm(bank(0, 128), kp[:, u, ch, :], ht[:, u, ch, :],
                                      start=(u == 0 and ch == 0), stop=(u == U - 1 and ch == NCH - 1))
                    last.then_inc(s_kh, 1)
                pe.wait_ge(s_khm, b + 1)
                mm(bank(1, 128), khm[:, :], srep[:, :], start=True, stop=True).then_inc(s_t1, 1)
                pe.wait_ge(s_t1s, b + 1)
                mm(bank(2, 129), t1s[:, :], p1x[:, :], start=True, stop=True).then_inc(s_t2, 1)
                with pe.Fori(0, J1) as j:
                    it = b * J1 + j
                    pe.wait_ge(s_yw, 5 * (b + 1))
                    for u in range(U):
                        pe.wait_ge(s_ob, last_turn(it, u))
                        pe.wait_ge(s_hl[u], (it + 1) * 16)
                        for p in range(2):
                            last = mm(bank(2 * u + p), wqb[:, p], hb[:, u, :], start=True, stop=True)
                        last.then_inc(s_q, 1)
                    for u in range(U):
                        pe.wait_ge(s_qsq, one_pass(it, u))
                        mm(bank(u), wwq[:, :, :], hb[:, u, :], start=True, stop=False)
                        mm(bank(u), nh[:, 0, :], qsq[:, u, 0, :], start=False, stop=False)
                        mm(bank(u), nh[:, 1, :], qsq[:, u, 1, :], start=False, stop=True).then_inc(s_lq, 1)
                    for u in range(U):
                        pe.wait_ge(s_qp, one_pass(it, u))
                        mm(bank(4 + u), dwb[:, :], qp[:, u, :], start=True, stop=True).then_inc(s_d, 1)
                    for u in range(U):
                        pe.wait_ge(s_qpn, one_pass(it, u if u < 2 else U - 1))
                        for p in range(2):
                            mm(bank(2 * u + p), mycb[:, p], qpn[:, u, :], start=True, stop=False)
                            last = mm(bank(2 * u + p), wvycb[:, p], hb[:, u, :], start=False, stop=True)
                        last.then_inc(s_yc, 1)
                    for u in range(U):
                        pe.wait_ge(s_ycs, one_pass(it, u))
                        for p in range(2):
                            last = mm(bank(2 * u + p), jb64[:, :], ycs[:, u, p, :], start=True, stop=True)
                        last.then_inc(s_var2, 1)
                    for u in range(U):
                        pe.wait_ge(s_h2, one_pass(it, u))
                        for p in range(2):
                            last = mm(bank(2 * u + p), m1g[:, :], yc[:, u, p, :], start=True, stop=True)
                        last.then_inc(s_m1, 1)
                    for u in range(U):
                        pe.wait_ge(s_gl, one_pass(it, u))
                        for p in range(2):
                            mm(bank(2 * u + p), myb[:, p], qpn[:, u, :], start=True, stop=False)
                            mm(bank(2 * u + p), wvyb[:, p], hb[:, u, :], start=False, stop=False)
                            last = mm(bank(2 * u + p), m2bd[:, :], gl[:, u, p, :], start=False, stop=True)
                        last.then_inc(s_o, 1)

        @block.scalar
        def _(act):
            fn = nc.scalar.activation
            lead(act, s_sq, s_ln, s_rs, s_ksq, s_kp, s_qsq, s_qp, s_ycs, s_ln2, s_rs2, s_gl)
            act.wait_ge(s_w, 16 * len(loads))
            act.wait_ge(s_prep, 17)
            with act.Fori(0, B) as b:
                with act.Fori(0, J1) as j:
                    it = b * J1 + j
                    for u in range(U):
                        act.wait_ge(s_cen, one_pass(it, u))
                        fn(sq[:, u, :], bank(u), ACT.Square).then_inc(s_sq, 1)
                    for u in range(U):
                        act.wait_ge(s_var, one_pass(it, u))
                        fn(rs[:, u, :], bank(4 + u), ACT.Ln, bias=eps1[:, :]).then_inc(s_ln, 1)
                    for u in range(U):
                        act.wait_ge(s_ln, one_pass(it, u))
                        fn(rs[:, u, :], rs[:, u, :], ACT.Exp, scale=-0.5).then_inc(s_rs, 1)
                    for u in range(U):
                        act.wait_ge(s_k, one_pass(it, u))
                        fn(ksq[:, u], banks(2 * u), ACT.Square).then_inc(s_ksq, 1)
                    for u in range(U):
                        act.wait_ge(s_tok, one_pass(it, u))
                        fn(kp[:, u], ps[0:CH, 2 * u, :], ACT.Exp).then_inc(s_kp, 1)
                with act.Fori(0, J1) as j:
                    it = b * J1 + j
                    for u in range(U):
                        act.wait_ge(s_q, one_pass(it, u))
                        fn(qsq[:, u], banks(2 * u), ACT.Square).then_inc(s_qsq, 1)
                    for u in range(U):
                        act.wait_ge(s_lq, one_pass(it, u))
                        fn(qp[:, u, :], bank(u), ACT.Exp).then_inc(s_qp, 1)
                    for u in range(U):
                        act.wait_ge(s_ycb, one_pass(it, u))
                        fn(ycs[:, u], yc[:, u], ACT.Square).then_inc(s_ycs, 1)
                    for u in range(U):
                        act.wait_ge(s_var2, one_pass(it, u))
                        fn(rs2[:, u], banks(2 * u), ACT.Ln, bias=eps64[:, :]).then_inc(s_ln2, 1)
                    for u in range(U):
                        act.wait_ge(s_ln2, one_pass(it, u))
                        fn(rs2[:, u], rs2[:, u], ACT.Exp, scale=-0.5).then_inc(s_rs2, 1)
                    for u in range(U):
                        act.wait_ge(s_m1, one_pass(it, u))
                        fn(gl[:, u], banks(2 * u), ACT.Gelu, bias=m1bias[:, :]).then_inc(s_gl, 1)

        @block.vector
        def _(dve):
            tt = nc.vector.tensor_tensor
            cp = nc.vector.tensor_copy

            def spread(a):
                return a.unsqueeze(1).to_broadcast([128, 2, 64])

            lead(dve, s_h, s_ht, s_khadd, s_de, s_dr, s_qpn, s_ycb, s_h2, s_ob)
            dve.memset(khacc[:, :], 0.0).then_inc(s_khz, 1)
            dve.wait_ge(s_w, 16 * len(loads))
            dve.wait_ge(s_prep_mm, 1)
            cp(w1r[:, :], bank(0, 192)).then_inc(s_prep, 1)
            cp(w1t[:, :, :], ps[0:64, 1, 0:384]).then_inc(s_prep, 1)
            cp(wvyt[:, :], bank(2, 128, 64)).then_inc(s_prep, 1)
            cp(pwr1[:, 64:128], bank(3, 64, 64)).then_inc(s_prep, 1)
            dve.wait_ge(s_prep, 4)
            for p in range(2):
                tt(wkb[:, p], spread(w1r[:, 0:64]), pmask[:, p], ALU.mult).then_inc(s_prep, 1)
                tt(wqb[:, p], spread(w1r[:, 64:128]), pmask[:, p], ALU.mult).then_inc(s_prep, 1)
            dve.wait_ge(s_prep_mm, 2)
            for p in range(2):
                tt(wvyb[:, p], spread(ps[:, 5, 0:64]), pmask[:, p], ALU.mult).then_inc(s_prep, 1)
                tt(wvycb[:, p], spread(ps[:, 5, 64:128]), pmask[:, p], ALU.mult).then_inc(s_prep, 1)
            for dst, lo in ((wwk, 0), (wwq, 32)):
                tt(dst[:, :, :], ps[:, 4, lo:lo + 32].unsqueeze(1).to_broadcast([128, 4, 32]),
                   bd32[:, :].rearrange("p (g m) -> p g m", g=4), ALU.mult).then_inc(s_prep, 1)
            cp(p1x[:, 0:128], bank(6, 128)).then_inc(s_prep, 1)
            nc.vector.tensor_scalar(m1g[:, :], m1bd[:, :], g2[:, :], None, ALU.mult).then_inc(s_prep, 1)
            tt(m1bias[:, :], bank(7, 1), m1b[:, :], ALU.add).then_inc(s_prep, 1)
            with dve.Fori(0, B) as b:
                with dve.Fori(0, J1) as j:
                    it = b * J1 + j
                    dve.wait_ge(s_khz, b + 1)
                    for u in range(U):
                        dve.wait_ge(s_rs, one_pass(it, u))
                        if u == 0:
                            dve.wait_ge(s_hst, before(it, U * 16))
                        tt(h[:, u, :], bank(u), rs[:, u, :], ALU.mult).then_inc(s_h, 1)
                    for u in range(U):
                        dve.wait_ge(s_tok, one_pass(it, u))
                        cp(ht[:, u], ps[0:CH, 2 * u + 1, :]).then_inc(s_ht, 1)
                    dve.wait_ge(s_kh, it + 1)
                    dve.wait_ge(s_khadd, before(it, 1))
                    tt(khacc[:, :], khacc[:, :], bank(0, 128), ALU.add).then_inc(s_khadd, 1)
                dve.wait_ge(s_khadd, before(b + 1, J1))
                tt(khm[:, :], khacc[:, :], bd32[:, :], ALU.mult).then_inc(s_khm, 1)
                dve.wait_ge(s_khm, b + 1)
                dve.memset(khacc[:, :], 0.0).then_inc(s_khz, 1)
                dve.wait_ge(s_t1, b + 1)
                cp(t1s[:, :], bank(1, 128)).then_inc(s_t1s, 1)
                dve.wait_ge(s_t2, b + 1)
                nc.vector.tensor_scalar(t2s[:, :], bank(2, 129), 1.0 / M, None, ALU.mult).then_inc(s_t2s, 1)
                dve.wait_ge(s_t2s, b + 1)
                for p in range(2):
                    tt(myb[:, p], spread(t2s[:, 0:64]), pmask[:, p], ALU.mult).then_inc(s_yw, 1)
                    tt(mycb[:, p], spread(t2s[:, 64:128]), pmask[:, p], ALU.mult).then_inc(s_yw, 1)
                nc.vector.tensor_scalar(dwb[:, :], bd32[:, :], t2s[:, 128:129], None, ALU.mult).then_inc(s_yw, 1)
                with dve.Fori(0, J1) as j:
                    it = b * J1 + j
                    for u in range(U):
                        dve.wait_ge(s_d, one_pass(it, u))
                        nc.vector.tensor_scalar(qpn[:, u, :], bank(4 + u), D_EPS, None, ALU.add).then_inc(s_de, 1)
                        dve.wait_ge(s_de, one_pass(it, u))
                        nc.vector.reciprocal(qpn[:, u, :], qpn[:, u, :]).then_inc(s_dr, 1)
                        dve.wait_ge(s_dr, one_pass(it, u))
                        tt(qpn[:, u, :], qp[:, u, :], qpn[:, u, :], ALU.mult).then_inc(s_qpn, 1)
                    for u in range(U):
                        dve.wait_ge(s_yc, one_pass(it, u))
                        cp(yc[:, u], banks(2 * u)).then_inc(s_ycb, 1)
                    for u in range(U):
                        dve.wait_ge(s_rs2, one_pass(it, u))
                        tt(yc[:, u], yc[:, u], rs2[:, u], ALU.mult).then_inc(s_h2, 1)
                    for u in range(U):
                        dve.wait_ge(s_o, one_pass(it, u))
                        if u == 0:
                            dve.wait_ge(s_t1st, it * (U * 4 * 16) + 16)
                        nc.vector.tensor_scalar(ob[:, u], banks(2 * u), m2b[:, :], None, ALU.add).then_inc(s_ob, 1)


S2 = IMG // 2
TR2 = T // S2
J2 = S2 // (TR2 * U)
T2ROWS = S2 + 2


def performer2(nc, sem, w, c, t1, vq_spill, t2):
    with ExitStack() as ctx:
        def sb(name, shape):
            return ctx.enter_context(nc.sbuf_tensor(name, shape, F32))

        ps = ctx.enter_context(nc.psum_tensor("ps2", [128, 8, 512], F32))

        def bank(k, n=T, rows=128):
            return ps[0:rows, k, 0:n]

        ident = sb("ident2", [128, 128])
        ones576 = sb("ones576", [128, 128])
        sel2 = sb("sel2", [128, 64])
        seli = sb("seli", [128, 64])
        selk = sb("selk", [64, 32])
        j64 = sb("j64", [64, 128])
        c64 = sb("c64", [64, 64])
        eps64 = sb("eps64b", [128, 1])
        wa = sb("wa", [128, 3, 256])
        wb = sb("wb", [64, 3, 256])
        wn = sb("wn", [64, 2, 576])
        ga = sb("ga", [128, 3])
        gb = sb("gb", [64, 3])
        ba = sb("ba", [128, 3])
        bb = sb("bb", [64, 3])
        wfeat = sb("wfeat2", [64, 32])
        wsel = sb("wsel2", [128, 64])
        kqb = sb("kqb2", [128, 1])
        vb = sb("vb2", [64, 1])
        pb = sb("pb2", [64, 1])
        pw = sb("pw2", [64, 64])
        prj = sb("prj2", [64, 128])
        m1 = sb("m1t2", [64, 128])
        m2 = sb("m2t2", [64, 128])
        g2 = sb("g22", [64, 1])
        b2 = sb("b22", [64, 1])
        m1b = sb("m1b2", [64, 1])
        m2b = sb("m2b2", [64, 1])
        bkq = sb("bkq", [128, 1])
        bvp = sb("bvp", [64, 1])
        iv = sb("iv", [64, 65])
        by = sb("by", [64, 1])
        bo = sb("bo", [64, 1])
        blq = sb("blq", [64, 1])
        rr = sb("rr", [65, 129])
        m1g = sb("m1g2", [64, 128])
        m1bias = sb("m1bias2", [64, 1])
        kvacc = sb("kvacc", [65, 96])
        dw = sb("dw2", [96, 96])
        ycw = sb("ycw", [96, 128])
        yw = sb("yw", [96, 128])
        ones32 = sb("ones32", [96, 32])
        kps = sb("kps", [96, 1])
        xt = sb("xt2", [128, U, TR2 + 1, XP])
        xs = sb("xs2", [128, U, TR2 + 1, XP])
        cs = sb("cs2", [128, U, TR2 + 1, S2])
        css = sb("css2", [128, U, TR2 + 1, S2])
        ms = sb("ms2", [128, U, T])
        rs = sb("rsa2", [128, U, T])
        kq = sb("kq2", [128, U, T])
        vl = sb("vl2", [128, U, T])
        kpq = sb("kpq2", [64, U, T])
        vt = sb("vt2", [CH, U, NCH, 97])
        vq = sb("vq2", [96, U, T])
        dn = sb("dn2", [96, U, T])
        yc = sb("yc2", [64, U, T])
        ycs = sb("ycs2", [64, U, T])
        rs2 = sb("rs22", [64, U, T])
        gl = sb("gl2", [64, U, T])
        ob = sb("ob2", [64, U, T])

        loads = [(ident, c["ident"]), (ones576, c["ones576"]), (sel2, c["sel2"]), (seli, c["seli"]),
                 (selk, c["selk"]), (j64, c["j64"]), (c64, c["c64"]), (eps64, c["eps64"]),
                 (wa[:, :, 0:192], w["wa2"]), (wb[:, :, 0:192], w["wb2"]), (wn, w["wn2"]), (ga, w["ga2"]),
                 (gb, w["gb2"]), (ba, w["ba2"]), (bb, w["bb2"]), (wfeat, w["wfeat2"]), (wsel, w["wsel2"]),
                 (kqb, w["kqb2"]), (vb, w["vb2"]), (pb, w["pb2"]), (pw, w["pw2"]), (prj[:, 0:64], w["pwt2"]),
                 (m1, w["m1t2"]), (m2, w["m2t2"]), (g2, w["g22"]), (b2, w["b22"]), (m1b, w["m1b2"]),
                 (m2b, w["m2b2"]), (iv[:, 0:64], c["ident"][0:64, 0:64]), (ycw[0:64, :], c["c64pad"]),
                 (yw[0:64, :], c["i64pad"]), (rr[0:65, 128:129], c["last65"])]

        s_w = sem("p2_weights_loaded")
        s_set = sem("p2_buffers_set")
        s_pm = sem("p2_prep_products")
        s_pd = sem("p2_prep_written")
        s_x = [sem(f"p2_x_loaded_{u}") for u in range(U)]
        s_xs = sem("p2_x_squared")
        s_cs = sem("p2_column_sums")
        s_css = sem("p2_column_sums_of_squares")
        s_c1 = sem("p2_column_pairs_added")
        s_st = sem("p2_statistics")
        s_kq = sem("p2_kq_product")
        s_vl = sem("p2_vl_product")
        s_ms = sem("p2_mean_squared")
        s_va = sem("p2_variance")
        s_lv = sem("p2_log_variance")
        s_rs = sem("p2_inverse_deviation")
        s_kqn = sem("p2_kq_normalised")
        s_kqs = sem("p2_kq_squared")
        s_vln = sem("p2_vl_normalised")
        s_lg = sem("p2_logits")
        s_kpq = sem("p2_kpq_written")
        s_tr = sem("p2_transposed")
        s_vt = sem("p2_vt_written")
        s_kv = sem("p2_kv_product")
        s_kva = sem("p2_kv_added")
        s_vst = sem("p2_v_and_q_stored")
        s_mp = sem("p2_matrix_product")
        s_yw = sem("p2_y_weights")
        s_kps = sem("p2_kp_sum_scaled")
        s_kvz = sem("p2_kv_cleared")
        s_vql = [sem(f"p2_v_and_q_loaded_{u}") for u in range(U)]
        s_d = sem("p2_denominator")
        s_de = sem("p2_denominator_guarded")
        s_dr = sem("p2_denominator_inverse")
        s_qn = sem("p2_qp_normalised")
        s_yc = sem("p2_y_centred")
        s_ycb = sem("p2_y_copied")
        s_ycs = sem("p2_y_squared")
        s_v2 = sem("p2_y_variance")
        s_l2 = sem("p2_y_log_variance")
        s_r2 = sem("p2_y_inverse_deviation")
        s_h2 = sem("p2_h2_written")
        s_m1 = sem("p2_mlp_in")
        s_gl = sem("p2_gelu_written")
        s_o = sem("p2_out_product")
        s_ob = sem("p2_out_written")
        s_t2 = sem("p2_out_stored")
        s_zero = sem("p2_zero_set")

        block = ctx.enter_context(nc.Block())

        @block.sync
        def _(sp):
            for dst, src in loads:
                sp.dma_start(dst[...] if not isinstance(dst, bass.AP) else dst, src).then_inc(s_w, 16)
            sp.wait_ge(s_set, 3)
            with sp.Fori(0, B) as b:
                with sp.Fori(0, J2) as j:
                    it = b * J2 + j
                    for u in range(U):
                        sp.wait_ge(s_vl, last_turn(it, u))
                        sp.wait_ge(s_css, last_turn(it, u))
                        for par in range(2):
                            rows = TR2 + 1 - par
                            src = bass.AP(t1.tensor, b * (E * T1ROWS * IMG) + j * (U * TR2 * 2 * IMG)
                                          + (u * TR2 * 2 + par) * IMG,
                                          [[T1ROWS * IMG, E], [2 * IMG, rows], [1, IMG]])
                            sp.dma_start(xt[64 * par:64 * par + 64, u, 0:rows, 1:IMG + 1], src).then_inc(s_x[u], 16)
                with sp.Fori(0, J2) as j:
                    it = b * J2 + j
                    sp.wait_ge(s_vst, before(b + 1, J2 * U * 32))
                    for u in range(U):
                        sp.wait_ge(s_o, last_turn(it, u))
                        sp.dma_start(vq[:, u, :], vq_spill[it * U + u]).then_inc(s_vql[u], 16)

        @block.gpsimd
        def _(pool):
            lead(pool, s_c1, s_cs, s_css)
            pool.memset(ob[:, 0, :], 0.0).then_inc(s_zero, 1)
            pool.wait_ge(s_zero, 1)
            for b in range(B):
                pool.dma_start(bass.AP(t2.tensor, b * E * T2ROWS * S2, [[T2ROWS * S2, E], [1, S2]]),
                               ob[:, 0, 0:S2]).then_inc(s_t2, 16)
            pool.memset(xt[:, :, :, :], 0.0).then_inc(s_set, 1)
            pool.memset(vt[:, :, :, :], 1.0).then_inc(s_set, 1)
            pool.memset(ones32[:, :], 1.0).then_inc(s_set, 1)
            add = nc.gpsimd.tensor_tensor
            with pool.Fori(0, B) as b:
                with pool.Fori(0, J2) as j:
                    it = b * J2 + j
                    for u in range(U):
                        for src, dst, s_src, s_dst, at in ((xt, cs, s_x[u], s_cs, (it + 1) * 32),
                                                           (xs, css, s_xs, s_css, one_pass(it, u))):
                            first = 1 if s_dst is s_cs else 2
                            pool.wait_ge(s_src, at)
                            a = src[:, u, :, 0:2 * S2].rearrange("p r (c two) -> p r c two", two=2)
                            add(dst[:, u], a[:, :, :, 0], a[:, :, :, 1], ALU.add).then_inc(s_c1, 1)
                            pool.wait_ge(s_c1, it * (2 * U) + 2 * u + first + U)
                            a = src[:, u, :, 2:2 * S2 + 2].rearrange("p r (c two) -> p r c two", two=2)
                            add(dst[:, u], dst[:, u], a[:, :, :, 0], ALU.add).then_inc(s_dst, 1)
                with pool.Fori(0, J2) as j:
                    it = b * J2 + j
                    for u in range(U):
                        pool.wait_ge(s_ob, one_pass(it, u))
                        dst = bass.AP(t2.tensor, b * (E * T2ROWS * S2) + j * (U * TR2 * S2) + (1 + u * TR2) * S2,
                                      [[T2ROWS * S2, E], [1, T]])
                        pool.dma_start(dst, ob[:, u, :]).then_inc(s_t2, 16)
            pool.wait_ge(s_t2, 16 * B + B * J2 * U * 16)

        @block.tensor
        def _(pe):
            mm = nc.tensor.matmul
            lead(pe, s_st, s_kq, s_vl, s_lg, s_tr, s_kv, s_d, s_yc, s_v2, s_m1, s_o)
            pe.wait_ge(s_w, 16 * len(loads))
            for j in range(3):
                for k, lo in ((1, 0), (0, 32)):
                    mm(ps[:, 0, 64 * j + lo:64 * j + lo + 32], wn[:, k, 192 * j:192 * j + 128], wfeat[:, :],
                       start=True, stop=True)
                    mm(ps[0:64, 1, 64 * j + lo:64 * j + lo + 32], wn[:, k, 192 * j + 128:192 * j + 192],
                       wfeat[:, :], start=True, stop=True)
            for j in range(3):
                mm(bank(2, 1), wa[:, j, 0:128], ba[:, j:j + 1], start=(j == 0), stop=False)
            for j in range(3):
                mm(bank(2, 1), wb[:, j, 0:128], bb[:, j:j + 1], start=False, stop=(j == 2))
            for j in range(3):
                mm(bank(3, 1, 64), wa[:, j, 128:192], ba[:, j:j + 1], start=(j == 0), stop=False)
            for j in range(3):
                mm(bank(3, 1, 64), wb[:, j, 128:192], bb[:, j:j + 1], start=False, stop=(j == 2))
            mm(bank(7, 1), m1[:, :], b2[:, :], start=True, stop=True)
            mm(bank(6, 64, 64), pw[:, :], c64[:, :], start=True, stop=True).then_inc(s_pm, 1)
            pe.wait_ge(s_pd, 11)
            for j in range(3):
                mm(bank(4, 256), ones576[:, :], wa[:, j, :], start=(j == 0), stop=False)
            for j in range(3):
                mm(bank(4, 256), ones576[0:64, :], wb[:, j, :], start=False, stop=(j == 2))
            mm(bank(5, 1, 64), wsel[:, :], bkq[:, :], start=True, stop=True)
            mm(bank(0, 1, 64), c64[:, :], bvp[:, :], start=True, stop=True)
            mm(bank(1, 128, 65), iv[:, :], prj[:, :], start=True, stop=True).then_inc(s_pm, 1)
            pe.wait_ge(s_pd, 19)

            def taps(o, view, cols):
                for j in range(3):
                    mm(o, wa[:, j, cols], view(0, 128, j), start=(j == 0), stop=False)
                for j in range(3):
                    last = mm(o, wb[:, j, cols], view(1, 64, j), start=False, stop=(j == 2))
                return last

            def pixels(u):
                return lambda r, n, j: xt[0:n, u, r:r + TR2, j:j + 2 * S2 - 1:2]

            def statistics(it, u):
                base = 4 * (u % 2)
                pe.wait_ge(s_css, one_pass(it, u))
                pe.wait_ge(s_cs, one_pass(it, u))
                for k, a in ((2, cs), (3, css)):
                    o = bank(base + k)
                    mm(o, ones576[:, :], a[:, u, 0:TR2, :], start=True, stop=False)
                    last = mm(o, ones576[0:64, :], a[0:64, u, 1:TR2 + 1, :], start=False, stop=True)
                last.then_inc(s_st, 1)

            def conv_kq(it, u):
                taps(bank(4 * (u % 2)), pixels(u), slice(0, 128)).then_inc(s_kq, 1)

            def conv_vl(it, u):
                if u < 2:
                    pe.wait_ge(s_kva, before(it))
                else:
                    pe.wait_ge(s_kva, one_pass(it, u - 2))
                taps(bank(4 * (u % 2) + 1), pixels(u), slice(128, 256)).then_inc(s_vl, 1)

            def logits(it, u):
                o = bank(4 * (u % 2) + 2, T, 64)
                pe.wait_ge(s_vln, one_pass(it, u))
                mm(o, seli[:, :], vl[:, u, :], start=True, stop=False)
                pe.wait_ge(s_kqs, one_pass(it, u))
                mm(o, sel2[:, :], kq[:, u, :], start=False, stop=True).then_inc(s_lg, 1)

            def transposes(it, u):
                pe.wait_ge(s_kpq, one_pass(it, u))
                for ch in range(NCH):
                    cols = slice(ch * CH, ch * CH + CH)
                    o = 4 * (u % 2) + 3
                    mm(ps[0:CH, o, 96 * ch:96 * ch + 32], kpq[:, u, cols], selk[:, :], start=True, stop=True)
                    last = mm(ps[0:CH, o, 96 * ch + 32:96 * ch + 96], vl[0:64, u, cols], ident[0:64, 0:64],
                              start=True, stop=True)
                last.then_inc(s_tr, 1)

            def keys_values(it, u):
                pe.wait_ge(s_vt, one_pass(it, u))
                for ch in range(NCH):
                    last = mm(bank(4 * (u % 2) + 1, 32, 65), vt[:, u, ch, 32:97], vt[:, u, ch, 0:32],
                              start=(ch == 0), stop=(ch == NCH - 1))
                last.then_inc(s_kv, 1)

            with pe.Fori(0, B) as b:
                with pe.Fori(0, J2) as j:
                    it = b * J2 + j
                    pe.wait_ge(s_kpq, before(it))
                    pe.wait_ge(s_vt, before(it))
                    pe.wait_ge(s_ob, before(b, J2 * U))
                    for u in range(U + 1):
                        if u < U:
                            statistics(it, u)
                        if u > 0:
                            logits(it, u - 1)
                        if u < U:
                            conv_kq(it, u)
                        if u > 0:
                            transposes(it, u - 1)
                        if u < U:
                            conv_vl(it, u)
                        if u > 0:
                            keys_values(it, u - 1)
                pe.wait_ge(s_kva, before(b + 1, J2 * U))
                mm(bank(0, 129, 96), kvacc[:, :], rr[:, :], start=True, stop=True).then_inc(s_mp, 1)
                with pe.Fori(0, J2) as j:
                    it = b * J2 + j
                    pe.wait_ge(s_yw, 3 * (b + 1))
                    for u in range(U):
                        pe.wait_ge(s_ob, last_turn(it, u))
                        pe.wait_ge(s_vql[u], (it + 1) * 16)
                        mm(bank(u, T, 96), dw[:, :], vq[:, u, :], start=True, stop=True).then_inc(s_d, 1)
                    for u in range(U):
                        pe.wait_ge(s_qn, one_pass(it, u))
                        mm(bank(4 + u), ycw[:, :], vq[:, u, :], start=True, stop=True).then_inc(s_yc, 1)
                    for u in range(U):
                        pe.wait_ge(s_ycs, one_pass(it, u))
                        mm(bank(u), j64[:, :], ycs[:, u, :], start=True, stop=True).then_inc(s_v2, 1)
                    for u in range(U):
                        pe.wait_ge(s_h2, one_pass(it, u))
                        mm(bank(4 + u), m1g[:, :], yc[:, u, :], start=True, stop=True).then_inc(s_m1, 1)
                    for u in range(U):
                        pe.wait_ge(s_gl, one_pass(it, u))
                        mm(bank(u), m2[:, :], gl[:, u, :], start=True, stop=False)
                        mm(bank(u), yw[:, :], vq[:, u, :], start=False, stop=True).then_inc(s_o, 1)

        @block.scalar
        def _(act):
            fn = nc.scalar.activation
            lead(act, s_xs, s_ms, s_lv, s_rs, s_kqs, s_kpq, s_ycs, s_l2, s_r2, s_gl, s_vst)
            act.wait_ge(s_w, 16 * len(loads))
            act.wait_ge(s_pd, 19)

            def squares(it, u):
                act.wait_ge(s_x[u], (it + 1) * 32)
                act.wait_ge(s_css, last_turn(it, u))
                fn(xs[:, u], xt[:, u], ACT.Square).then_inc(s_xs, 1)

            with act.Fori(0, B) as b:
                with act.Fori(0, J2) as j:
                    it = b * J2 + j
                    squares(it, 0)
                    for u in range(U):
                        base = 4 * (u % 2)
                        if u + 1 < U:
                            squares(it, u + 1)
                        act.wait_ge(s_st, one_pass(it, u))
                        fn(ms[:, u, :], bank(base + 2), ACT.Square).then_inc(s_ms, 1)
                        act.wait_ge(s_va, one_pass(it, u))
                        fn(rs[:, u, :], ms[:, u, :], ACT.Ln, bias=eps64[:, :]).then_inc(s_lv, 1)
                        act.wait_ge(s_lv, one_pass(it, u))
                        fn(rs[:, u, :], rs[:, u, :], ACT.Exp, scale=-0.5).then_inc(s_rs, 1)
                        act.wait_ge(s_kqn, one_pass(it, u))
                        fn(kq[:, u, :], kq[:, u, :], ACT.Square, bias=bkq[:, :]).then_inc(s_kqs, 1)
                        act.wait_ge(s_lg, one_pass(it, u))
                        fn(kpq[:, u, :], bank(base + 2, T, 64), ACT.Exp, bias=blq[:, :]).then_inc(s_kpq, 1)
                        act.wait_ge(s_kpq, one_pass(it, u))
                        act.dma_start(vq_spill[it * U + u, 0:64], vl[0:64, u, :]).then_inc(s_vst, 16)
                        act.dma_start(vq_spill[it * U + u, 64:96], kpq[0:32, u, :]).then_inc(s_vst, 16)
                with act.Fori(0, J2) as j:
                    it = b * J2 + j
                    for u in range(U):
                        act.wait_ge(s_ycb, one_pass(it, u))
                        fn(ycs[:, u, :], yc[:, u, :], ACT.Square).then_inc(s_ycs, 1)
                    for u in range(U):
                        act.wait_ge(s_v2, one_pass(it, u))
                        fn(rs2[:, u, :], bank(u, T, 64), ACT.Ln, bias=eps64[0:64, :]).then_inc(s_l2, 1)
                    for u in range(U):
                        act.wait_ge(s_l2, one_pass(it, u))
                        fn(rs2[:, u, :], rs2[:, u, :], ACT.Exp, scale=-0.5).then_inc(s_r2, 1)
                    for u in range(U):
                        act.wait_ge(s_m1, one_pass(it, u))
                        fn(gl[:, u, :], bank(4 + u, T, 64), ACT.Gelu, bias=m1bias[:, :]).then_inc(s_gl, 1)

        @block.vector
        def _(dve):
            tt = nc.vector.tensor_tensor
            ts = nc.vector.tensor_scalar
            cp = nc.vector.tensor_copy
            lead(dve, s_va, s_kqn, s_vln, s_vt, s_kva, s_de, s_dr, s_qn, s_ycb, s_h2, s_ob)
            dve.memset(kvacc[:, :], 0.0).then_inc(s_kvz, 1)
            dve.memset(ycw[64:96, 64:128], 0.0).then_inc(s_pd, 1)
            dve.memset(yw[64:96, 64:128], 0.0).then_inc(s_pd, 1)
            dve.memset(dw[:, :], 0.0).then_inc(s_pd, 1)
            dve.wait_ge(s_w, 16 * len(loads))
            dve.wait_ge(s_pm, 1)
            cp(wa[:, :, 192:256], ps[:, 0, 0:192].rearrange("p (j m) -> p j m", j=3)).then_inc(s_pd, 1)
            cp(wb[:, :, 192:256], ps[0:64, 1, 0:192].rearrange("p (j m) -> p j m", j=3)).then_inc(s_pd, 1)
            tt(bkq[:, :], bank(2, 1), kqb[:, :], ALU.add).then_inc(s_pd, 1)
            tt(iv[:, 64:65], bank(3, 1, 64), vb[:, :], ALU.add).then_inc(s_pd, 1)
            dve.wait_ge(s_pd, 7)
            tt(wa[:, :, :], wa[:, :, :], ga[:, :].unsqueeze(2).to_broadcast([128, 3, 256]), ALU.mult).then_inc(s_pd, 1)
            tt(wb[:, :, :], wb[:, :, :], gb[:, :].unsqueeze(2).to_broadcast([64, 3, 256]), ALU.mult).then_inc(s_pd, 1)
            tt(bvp[:, :], iv[:, 64:65], pb[:, :], ALU.add).then_inc(s_pd, 1)
            cp(prj[:, 64:128], bank(6, 64, 64)).then_inc(s_pd, 1)
            dve.wait_ge(s_pd, 11)
            dve.wait_ge(s_pm, 2)
            tt(wa[:, :, :], wa[:, :, :], bank(4, 256).unsqueeze(1).to_broadcast([128, 3, 256]),
               ALU.subtract).then_inc(s_pd, 1)
            tt(wb[:, :, :], wb[:, :, :], bank(4, 256, 64).unsqueeze(1).to_broadcast([64, 3, 256]),
               ALU.subtract).then_inc(s_pd, 1)
            cp(blq[:, :], bank(5, 1, 64)).then_inc(s_pd, 1)
            cp(by[:, :], bank(0, 1, 64)).then_inc(s_pd, 1)
            tt(bo[:, :], bvp[:, :], m2b[:, :], ALU.add).then_inc(s_pd, 1)
            cp(rr[:, 0:128], bank(1, 128, 65)).then_inc(s_pd, 1)
            ts(m1g[:, :], m1[:, :], g2[:, :], None, ALU.mult).then_inc(s_pd, 1)
            tt(m1bias[:, :], bank(7, 1, 64), m1b[:, :], ALU.add).then_inc(s_pd, 1)
            with dve.Fori(0, B) as b:
                with dve.Fori(0, J2) as j:
                    it = b * J2 + j
                    dve.wait_ge(s_kvz, b + 1)
                    for u in range(U):
                        base = 4 * (u % 2)
                        dve.wait_ge(s_ms, one_pass(it, u))
                        tt(ms[:, u, :], bank(base + 3), ms[:, u, :], ALU.subtract).then_inc(s_va, 1)
                        if u > 0:
                            dve.wait_ge(s_tr, one_pass(it, u - 1))
                            cp(vt[:, u - 1, :, 0:96], ps[0:CH, 4 * ((u - 1) % 2) + 3, 0:96 * NCH]
                               .rearrange("p (h n) -> p h n", h=NCH)).then_inc(s_vt, 1)
                        dve.wait_ge(s_rs, one_pass(it, u))
                        dve.wait_ge(s_kq, one_pass(it, u))
                        tt(kq[:, u, :], bank(base), rs[:, u, :], ALU.mult).then_inc(s_kqn, 1)
                        dve.wait_ge(s_vl, one_pass(it, u))
                        if u == 0:
                            dve.wait_ge(s_vst, before(it, U * 32))
                        tt(vl[:, u, :], bank(base + 1), rs[:, u, :], ALU.mult).then_inc(s_vln, 1)
                        if u > 0:
                            dve.wait_ge(s_kv, one_pass(it, u - 1))
                            dve.wait_ge(s_kva, one_pass(it, u - 1) - 1)
                            tt(kvacc[:, 64:96], kvacc[:, 64:96], bank(4 * ((u - 1) % 2) + 1, 32, 65),
                               ALU.add).then_inc(s_kva, 1)
                    u = U - 1
                    dve.wait_ge(s_tr, one_pass(it, u))
                    cp(vt[:, u, :, 0:96], ps[0:CH, 4 * (u % 2) + 3, 0:96 * NCH]
                       .rearrange("p (h n) -> p h n", h=NCH)).then_inc(s_vt, 1)
                    dve.wait_ge(s_kv, one_pass(it, u))
                    dve.wait_ge(s_kva, one_pass(it, u) - 1)
                    tt(kvacc[:, 64:96], kvacc[:, 64:96], bank(4 * (u % 2) + 1, 32, 65), ALU.add).then_inc(s_kva, 1)
                dve.wait_ge(s_mp, b + 1)
                ts(ycw[64:96, 0:64], ps[64:96, 0, 64:128], 1.0 / M, None, ALU.mult).then_inc(s_yw, 1)
                ts(yw[64:96, 0:64], ps[64:96, 0, 0:64], 1.0 / M, None, ALU.mult).then_inc(s_yw, 1)
                ts(kps[64:96, :], ps[64:96, 0, 128:129], 1.0 / M, None, ALU.mult).then_inc(s_kps, 1)
                dve.wait_ge(s_kps, b + 1)
                ts(dw[64:96, 64:96], ones32[64:96, :], kps[64:96, :], None, ALU.mult).then_inc(s_yw, 1)
                dve.memset(kvacc[:, 64:96], 0.0).then_inc(s_kvz, 1)
                with dve.Fori(0, J2) as j:
                    it = b * J2 + j
                    for u in range(U):
                        dve.wait_ge(s_d, one_pass(it, u))
                        ts(dn[64:96, u, :], ps[64:96, u, 0:T], D_EPS, None, ALU.add).then_inc(s_de, 1)
                        dve.wait_ge(s_de, one_pass(it, u))
                        nc.vector.reciprocal(dn[64:96, u, :], dn[64:96, u, :]).then_inc(s_dr, 1)
                        dve.wait_ge(s_dr, one_pass(it, u))
                        tt(vq[64:96, u, :], vq[64:96, u, :], dn[64:96, u, :], ALU.mult).then_inc(s_qn, 1)
                    for u in range(U):
                        dve.wait_ge(s_yc, one_pass(it, u))
                        ts(yc[:, u, :], bank(4 + u, T, 64), by[:, :], None, ALU.add).then_inc(s_ycb, 1)
                    for u in range(U):
                        dve.wait_ge(s_r2, one_pass(it, u))
                        tt(yc[:, u, :], yc[:, u, :], rs2[:, u, :], ALU.mult).then_inc(s_h2, 1)
                    for u in range(U):
                        dve.wait_ge(s_o, one_pass(it, u))
                        if u == 0:
                            dve.wait_ge(s_t2, it * (U * 16) + 16 * B)
                        ts(ob[:, u, :], bank(u, T, 64), bo[:, :], None, ALU.add).then_inc(s_ob, 1)


S3 = S2 // 2
L = S3 * S3
TR3 = T // S3
J3 = S3 // TR3
D = 768
DC = D // 128
N = 16
Q = N // 4
NX = 8
NR = 64
MT = NX * NR // 128


def mark(it, per, k):
    return it * per + (U + k)


def tail(nc, sem, w, c, t2, out):
    with ExitStack() as ctx:
        def sb(name, shape):
            return ctx.enter_context(nc.sbuf_tensor(name, shape, F32))

        ps = ctx.enter_context(nc.psum_tensor("ps3", [128, 8, 512], F32))

        def bank(k, n=T, rows=128):
            return ps[0:rows, k, 0:n]

        ident = sb("ident3", [128, 128])
        jm = sb("jm768", [128, 128])
        sel8 = sb("sel8", [NX, MT, 128])
        desc = sb("desc", [CH, NCH, NX])
        eps = sb("eps3", [128, 1])
        wpa = sb("wpa", [128, 3, D])
        wpb = sb("wpb", [64, 3, D])
        pbias = sb("pbias", [128, DC])
        wbc = sb("wbc", [128, DC, 2 * N])
        bbc = sb("bbc", [2 * N, 1])
        wd = sb("wd", [128, DC])
        pd = sb("pd", [128, DC + 1])
        bd = sb("bd", [128, 1])
        aa = sb("aa", [128, DC, N])
        ai = sb("ai", [128, DC, N])
        enc = sb("enc", [128, DC, NR])
        encb = sb("encb", [NR, 1])
        sw = sb("sw", [NR, NX])
        swb = sb("swb", [CH, NCH, NX])
        w1 = sb("w1", [128, DC, NX * NR])
        b1 = sb("b1", [128, MT])
        w2 = sb("w2", [128, MT, D])
        b2 = sb("b2x", [NX, D])
        x3 = sb("x3", [128, TR3 + 1, S2 + 2])
        h = sb("h3", [128, DC, T])
        xn = sb("xn3", [128, DC, T])
        rs = sb("rs3", [128, T])
        bcs = sb("bcs", [2 * N, T])
        zs = sb("zs", [128, T])
        mx = sb("mx", [128, T])
        sp_ = sb("sp", [128, T])
        delta = sb("delta", [128, T])
        bcb = sb("bcb", [128, 2 * N, T])
        v = sb("v3", [128, N, T])
        a = sb("a3", [128, 2, 4, T])
        dg = sb("dg3", [128, N, 128])
        st = sb("st3", [128, DC, N])
        xe = sb("xe", [NR, T])
        lg = sb("lg", [CH, NCH, NX])
        ex = sb("ex", [CH, NCH, NX])
        eq = sb("eq", [CH, NCH, NX])
        m1 = sb("mx8", [CH, NCH])
        sm = sb("sm8", [CH, NCH])
        oh8 = sb("oh8", [NX, T])
        ot = sb("ot", [CH, 2, D])
        sq = v
        gm = a[:, 0]

        loads = [(ident, c["ident"]), (jm, c["jm768"]), (sel8, c["sel8"]), (desc, c["desc"]), (eps, c["eps64"]),
                 (wpa, w["wpa"]), (wpb, w["wpb"]), (pbias, w["pbias"]), (wbc, w["wbc"]), (bbc, w["bbc"]),
                 (wd, w["wd"]), (pd, w["pd"]), (bd, w["bd"]), (aa, w["aa"]), (enc, w["enc"]), (encb, w["encb"]),
                 (sw, w["sw"]), (swb, w["swb"]), (w1, w["w1"]), (b1, w["b1"]), (w2, w["w2"]), (b2, w["b2"])]

        s_w = sem("t_weights_loaded")
        s_set = sem("t_buffers_set")
        s_pd = sem("t_delta_bias_added")
        s_x = sem("t_x_loaded")
        s_pj = sem("t_projected")
        s_hw = sem("t_h_written")
        s_mean = [sem("t_mean_1"), sem("t_mean_2")]
        s_xc = [sem("t_centred_1"), sem("t_centred_2")]
        s_sq = [sem("t_squared_1"), sem("t_squared_2")]
        s_var = [sem("t_variance_1"), sem("t_variance_2")]
        s_ln = [sem("t_log_variance_1"), sem("t_log_variance_2")]
        s_rs = [sem("t_inverse_deviation_1"), sem("t_inverse_deviation_2")]
        s_xn = [sem("t_normalised_1"), sem("t_normalised_2")]
        s_z = sem("t_z_product")
        s_bc = sem("t_bc_product")
        s_zs = sem("t_z_copied")
        s_bcs = sem("t_bc_written")
        s_bp = sem("t_bc_spread_product")
        s_ba = sem("t_bc_spread_by_scalar")
        s_bv = sem("t_bc_spread_by_vector")
        s_ab = sem("t_delta_magnitude")
        s_ea = sem("t_delta_exponential")
        s_l1 = sem("t_delta_logarithm")
        s_mx = sem("t_delta_positive_part")
        s_dl = sem("t_delta_written")
        s_v = sem("t_v_written")
        s_dg = sem("t_diagonals_written")
        s_a = sem("t_decay_written")
        s_wt = sem("t_v_weighted")
        s_sc = sem("t_states_scanned")
        s_st = sem("t_last_states_kept")
        s_stz = sem("t_first_states_cleared")
        s_cm = sem("t_states_times_c")
        s_ns = sem("t_states_summed")
        s_hy = sem("t_h_updated")
        s_hm = sem("t_experts_in")
        s_gl = sem("t_experts_gelu")
        s_en = sem("t_encoded")
        s_xe = sem("t_encoding_written")
        s_lgp = sem("t_route_logits_product")
        s_r = sem("t_route_steps")
        s_rq = sem("t_route_chosen")
        s_rx = sem("t_route_exponentials")
        s_tr = sem("t_route_turned")
        s_oh = sem("t_route_copied")
        s_mk = sem("t_mask_product")
        s_gm = sem("t_experts_masked")
        s_o = sem("t_out_product")
        s_oa = sem("t_out_by_scalar")
        s_ov = sem("t_out_by_vector")
        s_out = [sem("t_out_stored_even"), sem("t_out_stored_odd")]

        block = ctx.enter_context(nc.Block())

        @block.sync
        def _(sp):
            for dst, src in loads:
                sp.dma_start(dst[...] if not isinstance(dst, bass.AP) else dst, src).then_inc(s_w, 16)
            sp.wait_ge(s_set, 1)
            with sp.Fori(0, B) as b:
                with sp.Fori(0, J3) as s:
                    it = b * J3 + s
                    sp.wait_ge(s_pj, mark(it, DC, 0))
                    for par in range(2):
                        rows = TR3 + 1 - par
                        src = bass.AP(t2.tensor, b * (E * T2ROWS * S2) + s * (TR3 * 2 * S2) + par * S2,
                                      [[T2ROWS * S2, E], [2 * S2, rows], [1, S2]])
                        sp.dma_start(x3[64 * par:64 * par + 64, 0:rows, 1:S2 + 1], src).then_inc(s_x, 16)

        @block.gpsimd
        def _(pool):
            tt = nc.gpsimd.tensor_tensor
            lead(pool, s_v, s_dg)
            pool.memset(x3[:, :, :], 0.0).then_inc(s_set, 1)
            pool.wait_ge(s_w, 16 * len(loads))
            pool.wait_ge(s_pd, 2)
            with pool.Fori(0, B) as b:
                with pool.Fori(0, J3) as s:
                    it = b * J3 + s
                    for dc in range(DC):
                        blk = it * DC + dc
                        pool.wait_ge(s_ba, mark(it, N, N))
                        pool.wait_ge(s_bv, mark(it, N, N))
                        for q in range(Q):
                            ns = slice(4 * q, 4 * q + 4)
                            pool.wait_ge(s_ns, blk * Q + (q + 1))
                            tt(v[:, ns, :], bcb[:, ns, :], xn[:, dc:dc + 1, :].to_broadcast([128, 4, T]),
                               ALU.mult).then_inc(s_v, 1)
                            tt(dg[:, ns, :], ident[:, :].unsqueeze(1).to_broadcast([128, 4, 128]),
                               ai[:, dc, ns].unsqueeze(2)
                               .to_broadcast([128, 4, 128]), ALU.mult).then_inc(s_dg, 1)

        @block.tensor
        def _(pe):
            mm = nc.tensor.matmul
            lead(pe, s_pj, *s_mean, *s_var, s_z, s_bc, s_bp, s_ns, s_hm, s_en, s_lgp, s_tr, s_mk, s_o)
            pe.wait_ge(s_w, 16 * len(loads))
            pe.wait_ge(s_pd, 2)

            def norm(it, k, ready):
                for dc in range(DC):
                    ready(dc)
                    last = mm(bank(6), jm[:, :], h[:, dc, :], start=(dc == 0), stop=(dc == DC - 1))
                last.then_inc(s_mean[k], 1)
                for dc in range(DC):
                    pe.wait_ge(s_sq[k], mark(it, DC, dc + 1))
                    last = mm(bank(7), jm[:, :], sq[:, dc, :], start=(dc == 0), stop=(dc == DC - 1))
                last.then_inc(s_var[k], 1)

            with pe.Fori(0, B) as b:
                with pe.Fori(0, J3) as s:
                    it = b * J3 + s
                    pe.wait_ge(s_oa, mark(it, NCH, 0))
                    pe.wait_ge(s_ov, mark(it, NCH, 0))
                    pe.wait_ge(s_x, (it + 1) * 32)
                    for dc in range(DC):
                        cols = slice(128 * dc, 128 * dc + 128)
                        for j in range(3):
                            mm(bank(dc), wpa[:, j, cols], x3[:, 0:TR3, j:j + 2 * S3 - 1:2], start=(j == 0), stop=False)
                        for j in range(3):
                            last = mm(bank(dc), wpb[:, j, cols], x3[0:64, 1:TR3 + 1, j:j + 2 * S3 - 1:2],
                                      start=False, stop=(j == 2))
                        last.then_inc(s_pj, 1)
                    norm(it, 0, lambda dc: pe.wait_ge(s_hw, mark(it, DC, dc + 1)))
                    for dc in range(DC):
                        pe.wait_ge(s_xn[0], mark(it, DC, dc + 1))
                        last = mm(bank(1, T, 2 * N), wbc[:, dc, :], xn[:, dc, :], start=(dc == 0), stop=(dc == DC - 1))
                    last.then_inc(s_bc, 1)
                    for dc in range(DC):
                        last = mm(bank(0), wd[:, dc:dc + 1].to_broadcast([128, 128]), xn[:, dc, :],
                                  start=(dc == 0), stop=(dc == DC - 1))
                    last.then_inc(s_z, 1)
                    pe.wait_ge(s_bcs, mark(it, 1, 1))
                    for n in range(2 * N):
                        if n >= 4:
                            pe.wait_ge((s_ba, s_bv)[n % 2], mark(it, N, (n - 4) // 2 + 1))
                        mm(bank(2 + n % 4), ident[0:2 * N, n:n + 1].to_broadcast([2 * N, 128]), bcs[:, :],
                           start=True, stop=True).then_inc(s_bp, 1)
                    for dc in range(DC):
                        blk = it * DC + dc
                        for q in range(Q):
                            if q == 0:
                                pe.wait_ge(s_hy, mark(blk, 1, 0))
                                pe.wait_ge(s_zs, mark(it, 1, 1))
                            pe.wait_ge(s_dg, mark(blk, Q, q + 1))
                            pe.wait_ge(s_cm, mark(blk, Q, q + 1))
                            for n in range(4 * q, 4 * q + 4):
                                last = mm(bank(0), dg[:, n, :], v[:, n, :], start=(n == 0), stop=(n == N - 1))
                            last.then_inc(s_ns, 1)
                    norm(it, 1, lambda dc: pe.wait_ge(s_hy, mark(it, DC, DC)))
                    for m in range(MT):
                        for dc in range(DC):
                            if m == 0:
                                pe.wait_ge(s_xn[1], mark(it, DC, dc + 1))
                            last = mm(bank(m), w1[:, dc, 128 * m:128 * m + 128], xn[:, dc, :],
                                      start=(dc == 0), stop=(dc == DC - 1))
                        last.then_inc(s_hm, 1)
                        if m == 0:
                            for dc in range(DC):
                                last = mm(bank(4, T, NR), enc[:, dc, :], xn[:, dc, :],
                                          start=(dc == 0), stop=(dc == DC - 1))
                            last.then_inc(s_en, 1)
                    pe.wait_ge(s_xe, mark(it, 1, 1))
                    for ch in range(NCH):
                        last = mm(ps[0:CH, 5, NX * ch:NX * ch + NX], xe[:, ch * CH:ch * CH + CH], sw[:, :],
                                  start=True, stop=True)
                    last.then_inc(s_lgp, 1)
                    pe.wait_ge(s_r, mark(it, 8, 8))
                    for ch in range(NCH):
                        last = mm(ps[0:NX, 6, ch * CH:ch * CH + CH], eq[:, ch, :], ident[0:CH, 0:CH],
                                  start=True, stop=True)
                    last.then_inc(s_tr, 1)
                    pe.wait_ge(s_oh, mark(it, 1, 1))
                    for m in range(MT):
                        pe.wait_ge(s_gl, mark(it, MT, m + 1))
                        mm(bank(m), sel8[:, m, :], oh8[:, :], start=True, stop=True).then_inc(s_mk, 1)
                    pe.wait_ge(s_gm, mark(it, MT, MT))
                    for ch in range(NCH):
                        cs = slice(ch * CH, ch * CH + CH)
                        for half in range(2):
                            o = 4 + 2 * (ch % 2) + half if ch < 2 else 2 * (ch % 2) + half
                            lo = half * (D // 2)
                            for m in range(MT):
                                mm(ps[0:CH, o, 0:D // 2], gm[:, m, cs], w2[:, m, lo:lo + D // 2],
                                   start=(m == 0), stop=False)
                            mm(ps[0:CH, o, 0:D // 2], oh8[:, cs], b2[:, lo:lo + D // 2], start=False, stop=False)
                            for k in range(DC // 2):
                                last = mm(ps[0:CH, o, 128 * k:128 * k + 128], h[:, half * (DC // 2) + k, cs],
                                          ident[:, :], start=False, stop=(k == DC // 2 - 1))
                        last.then_inc(s_o, 1)

        @block.scalar
        def _(act):
            fn = nc.scalar.activation
            lead(act, s_hw, *s_sq, *s_ln, *s_rs, s_bcs, s_ba, s_ab, s_ea, s_l1, s_a, s_gl, s_xe, s_rx, s_oa, *s_out)
            act.wait_ge(s_w, 16 * len(loads))
            act.wait_ge(s_pd, 2)

            def norm(it, k):
                for dc in range(DC):
                    act.wait_ge(s_xc[k], mark(it, DC, dc + 1))
                    fn(sq[:, dc, :], xn[:, dc, :], ACT.Square).then_inc(s_sq[k], 1)
                act.wait_ge(s_var[k], mark(it, 1, 1))
                fn(rs[:, :], bank(7), ACT.Ln, bias=eps[:, :]).then_inc(s_ln[k], 1)
                act.wait_ge(s_ln[k], mark(it, 1, 1))
                fn(rs[:, :], rs[:, :], ACT.Exp, scale=-0.5).then_inc(s_rs[k], 1)

            def softplus(blk, dc):
                fn(sp_[:, :], zs[:, :], ACT.Abs, bias=pd[:, dc:dc + 1]).then_inc(s_ab, 1)
                act.wait_ge(s_ab, mark(blk, 1, 1))
                fn(sp_[:, :], sp_[:, :], ACT.Exp, scale=-1.0).then_inc(s_ea, 1)
                act.wait_ge(s_ea, mark(blk, 1, 1))
                fn(sp_[:, :], sp_[:, :], ACT.Ln, bias=1.0).then_inc(s_l1, 1)

            with act.Fori(0, B) as b:
                with act.Fori(0, J3) as s:
                    it = b * J3 + s
                    for dc in range(DC):
                        act.wait_ge(s_pj, mark(it, DC, dc + 1))
                        fn(h[:, dc, :], bank(dc), ACT.Identity, bias=pbias[:, dc:dc + 1]).then_inc(s_hw, 1)
                    norm(it, 0)
                    act.wait_ge(s_bc, mark(it, 1, 1))
                    fn(bcs[:, :], bank(1, T, 2 * N), ACT.Identity, bias=bbc[:, :]).then_inc(s_bcs, 1)
                    for n in range(0, 2 * N, 2):
                        act.wait_ge(s_bp, mark(it, 2 * N, n + 1))
                        fn(bcb[:, n, :], bank(2 + n % 4), ACT.Copy).then_inc(s_ba, 1)
                    for dc in range(DC):
                        blk = it * DC + dc
                        act.wait_ge(s_zs, mark(it, 1, 1))
                        act.wait_ge(s_dl, mark(blk, 1, 0))
                        softplus(blk, dc)
                        act.wait_ge(s_dl, mark(blk, 1, 1))
                        for n in range(N):
                            q = n // 4
                            if n % 4 == 0:
                                act.wait_ge(s_cm, mark(blk, Q, q - 1))
                            fn(a[:, q % 2, n % 4, :], delta[:, :], ACT.Exp,
                               scale=aa[:, dc, n:n + 1]).then_inc(s_a, 1)
                    norm(it, 1)
                    for m in range(MT):
                        act.wait_ge(s_hm, mark(it, MT, m + 1))
                        fn(gm[:, m, :], bank(m), ACT.Gelu, bias=b1[:, m:m + 1]).then_inc(s_gl, 1)
                        if m == 0:
                            act.wait_ge(s_en, mark(it, 1, 1))
                            fn(xe[:, :], bank(4, T, NR), ACT.Identity, bias=encb[:, :]).then_inc(s_xe, 1)
                    act.wait_ge(s_r, mark(it, 8, 3))
                    fn(ex[:, :, :], lg[:, :, :], ACT.Exp).then_inc(s_rx, 1)
                    for ch in range(NCH):
                        act.wait_ge(s_o, mark(it, NCH, ch + 1))
                        act.wait_ge(s_out[ch % 2], mark(it, 32, 16 * (ch // 2)))
                        o = 4 + 2 * (ch % 2) if ch < 2 else 2 * (ch % 2)
                        fn(ot[:, ch % 2, 0:D // 2], ps[0:CH, o, 0:D // 2], ACT.Copy).then_inc(s_oa, 1)
                        act.wait_ge(s_oa, mark(it, NCH, ch + 1))
                        act.wait_ge(s_ov, mark(it, NCH, ch + 1))
                        dst = bass.AP(out.tensor, b * (L * D) + s * (T * D) + ch * CH * D, [[D, CH], [1, D]])
                        act.dma_start(dst, ot[:, ch % 2, :]).then_inc(s_out[ch % 2], 16)
            for k in range(2):
                act.wait_ge(s_out[k], mark(B * J3, 32, 0))

        @block.vector
        def _(dve):
            tt = nc.vector.tensor_tensor
            ts = nc.vector.tensor_scalar
            cp = nc.vector.tensor_copy
            lead(dve, *s_xc, *s_xn, s_zs, s_bv, s_mx, s_dl, s_wt, s_sc, s_st, s_cm, s_hy, s_r, s_rq, s_oh, s_gm, s_ov)
            dve.wait_ge(s_w, 16 * len(loads))
            nc.vector.reciprocal(ai[:, :, :], aa[:, :, :]).then_inc(s_pd, 1)
            ts(pd[:, :], pd[:, :], bd[:, :], None, ALU.add).then_inc(s_pd, 1)
            dve.wait_ge(s_pd, 2)

            def norm(it, k):
                dve.wait_ge(s_mean[k], mark(it, 1, 1))
                for dc in range(DC):
                    tt(xn[:, dc, :], h[:, dc, :], bank(6), ALU.subtract).then_inc(s_xc[k], 1)
                dve.wait_ge(s_rs[k], mark(it, 1, 1))
                for dc in range(DC):
                    tt(xn[:, dc, :], xn[:, dc, :], rs[:, :], ALU.mult).then_inc(s_xn[k], 1)

            def over(a2):
                return a2.unsqueeze(2).to_broadcast([CH, NCH, NX])

            with dve.Fori(0, B) as b:
                dve.wait_ge(s_st, mark(b, J3 * DC * Q, 0))
                dve.memset(st[:, :, :], 0.0).then_inc(s_stz, 1)
                with dve.Fori(0, J3) as s:
                    it = b * J3 + s
                    norm(it, 0)
                    dve.wait_ge(s_z, mark(it, 1, 1))
                    cp(zs[:, :], bank(0)).then_inc(s_zs, 1)
                    for n in range(1, 2 * N, 2):
                        dve.wait_ge(s_bp, mark(it, 2 * N, n + 1))
                        cp(bcb[:, n, :], bank(2 + n % 4)).then_inc(s_bv, 1)
                    for dc in range(DC):
                        blk = it * DC + dc
                        dve.wait_ge(s_stz, b + 1)
                        dve.wait_ge(s_zs, mark(it, 1, 1))
                        ts(mx[:, :], zs[:, :], pd[:, dc:dc + 1], 0.0, ALU.add, ALU.max).then_inc(s_mx, 1)
                        dve.wait_ge(s_mx, mark(blk, 1, 1))
                        dve.wait_ge(s_l1, mark(blk, 1, 1))
                        dve.wait_ge(s_a, mark(blk, N, 0))
                        tt(delta[:, :], mx[:, :], sp_[:, :], ALU.add).then_inc(s_dl, 1)
                        for q in range(Q):
                            dve.wait_ge(s_v, mark(blk, Q, q + 1))
                            for k in range(4):
                                n = 4 * q + k
                                dve.wait_ge(s_a, mark(blk, N, n + 1))
                                nc.vector.scalar_tensor_tensor(v[:, n, :], a[:, q % 2, k, :], aa[:, dc, n:n + 1],
                                                               v[:, n, :], ALU.subtract, ALU.mult).then_inc(s_wt, 1)
                            if q == 0:
                                dve.wait_ge(s_st, mark(blk, Q, 0))
                            for k in range(4):
                                n = 4 * q + k
                                dve.wait_ge(s_wt, mark(blk, N, n + 1))
                                nc.vector.tensor_tensor_scan(a[:, q % 2, k, :], a[:, q % 2, k, :], v[:, n, :],
                                                             st[:, dc, n:n + 1], ALU.mult,
                                                             ALU.add).then_inc(s_sc, 1)
                            dve.wait_ge(s_sc, mark(blk, N, 4 * q + 4))
                            cp(st[:, dc, 4 * q:4 * q + 4], a[:, q % 2, :, T - 1]).then_inc(s_st, 1)
                            tt(v[:, 4 * q:4 * q + 4, :], a[:, q % 2], bcb[:, N + 4 * q:N + 4 * q + 4, :],
                               ALU.mult).then_inc(s_cm, 1)
                        dve.wait_ge(s_ns, mark(blk, Q, Q))
                        tt(h[:, dc, :], h[:, dc, :], bank(0), ALU.add).then_inc(s_hy, 1)
                    norm(it, 1)
                    dve.wait_ge(s_lgp, mark(it, 1, 1))
                    tt(lg[:, :, :], ps[0:CH, 5, 0:NCH * NX].rearrange("p (h e) -> p h e", e=NX), swb[:, :, :],
                       ALU.add).then_inc(s_r, 1)
                    dve.wait_ge(s_r, mark(it, 8, 1))
                    nc.vector.reduce_max(m1[:, :], lg[:, :, :], mybir.AxisListType.X).then_inc(s_r, 1)
                    dve.wait_ge(s_r, mark(it, 8, 2))
                    tt(lg[:, :, :], lg[:, :, :], over(m1[:, :]), ALU.subtract).then_inc(s_r, 1)
                    dve.wait_ge(s_r, mark(it, 8, 3))
                    nc.vector.scalar_tensor_tensor(eq[:, :, :], lg[:, :, :], 0.0, desc[:, :, :], ALU.is_equal,
                                                   ALU.mult).then_inc(s_r, 1)
                    dve.wait_ge(s_r, mark(it, 8, 4))
                    nc.vector.reduce_max(m1[:, :], eq[:, :, :], mybir.AxisListType.X).then_inc(s_r, 1)
                    dve.wait_ge(s_rx, mark(it, 1, 1))
                    nc.vector.reduce_sum(sm[:, :], ex[:, :, :], mybir.AxisListType.X).then_inc(s_r, 1)
                    dve.wait_ge(s_r, mark(it, 8, 6))
                    tt(eq[:, :, :], eq[:, :, :], over(m1[:, :]), ALU.is_equal).then_inc(s_rq, 1)
                    nc.vector.reciprocal(sm[:, :], sm[:, :]).then_inc(s_r, 1)
                    dve.wait_ge(s_r, mark(it, 8, 7))
                    dve.wait_ge(s_rq, mark(it, 1, 1))
                    tt(eq[:, :, :], eq[:, :, :], over(sm[:, :]), ALU.mult).then_inc(s_r, 1)
                    dve.wait_ge(s_tr, mark(it, 1, 1))
                    cp(oh8[:, :], bank(6, T, NX)).then_inc(s_oh, 1)
                    for m in range(MT):
                        dve.wait_ge(s_mk, mark(it, MT, m + 1))
                        tt(gm[:, m, :], gm[:, m, :], bank(m), ALU.mult).then_inc(s_gm, 1)
                    for ch in range(NCH):
                        dve.wait_ge(s_o, mark(it, NCH, ch + 1))
                        dve.wait_ge(s_out[ch % 2], mark(it, 32, 16 * (ch // 2)))
                        o = 4 + 2 * (ch % 2) + 1 if ch < 2 else 2 * (ch % 2) + 1
                        cp(ot[:, ch % 2, D // 2:D], ps[0:CH, o, 0:D // 2]).then_inc(s_ov, 1)


def build(nc, w, c, out):
    t1 = nc.dram_tensor("tokens1", (B, E, T1ROWS, IMG), F32, kind="Internal").ap()
    t2 = nc.dram_tensor("tokens2", (B, E, T2ROWS, S2), F32, kind="Internal").ap()
    h_spill = nc.dram_tensor("h_spill", (B * J1 * U, 128, T), F32, kind="Internal").ap()
    vq_spill = nc.dram_tensor("vq_spill", (B * J2 * U, 96, T), F32, kind="Internal").ap()
    stages = (lambda sem: performer1(nc, sem, w["x"], w, c, t1, h_spill),
              lambda sem: performer2(nc, sem, w, c, t1, vq_spill, t2),
              lambda sem: tail(nc, sem, w, c, t2, out))
    for stage in stages:
        sems = []

        def sem(name):
            sems.append(nc.alloc_semaphore(name))
            return sems[-1]

        stage(sem)
        nc.clear_and_free_semaphores(sems)
        nc.all_engine_barrier()


def shape_constants():
    f = np.float32
    c = {}
    c["ident"] = np.eye(128, dtype=f)
    g32 = np.arange(128) // 32
    r32 = np.arange(128) % 32
    same = g32[:, None] == g32[None, :]
    c["bd32"] = same.astype(f)
    c["srep"] = (r32[:, None] == r32[None, :]).astype(f)
    inside = same & (r32 < F1)[:, None] & (r32 < F1)[None, :]
    c["cen1"] = (np.eye(128) * (r32 <= F1) - inside / F1).astype(f)
    c["mean27"] = (inside / F1).astype(f)
    g64 = np.arange(128) // 64
    c["jb64"] = ((g64[:, None] == g64[None, :]) / E).astype(f)
    pm = np.zeros((128, 2, 2, 64), f)
    nh = np.zeros((128, 2, 128), f)
    for g in range(G):
        pm[32 * g:32 * g + 32, g // 2, g % 2] = 1
        nh[64 * (g % 2):64 * (g % 2) + 64, g // 2, 32 * g:32 * g + 32] = -0.5
    c["pmask"], c["nh"] = pm, nh
    c["eps1"] = np.where(r32 == F1, 1.0, LN_EPS).astype(f)[:, None]
    c["eps64"] = np.full((128, 1), LN_EPS, f)
    c["ic64"] = np.concatenate([np.eye(E), np.eye(E) - 1.0 / E], 1).astype(f)
    c["e27col"] = (r32 == F1).astype(f)[:, None]
    c["e27"] = c["e27col"].T.copy()
    c["ones576"] = np.full((128, 128), 1.0 / (9 * E), f)
    i32 = np.arange(32)
    c["sel2"] = np.zeros((128, 64), f)
    c["sel2"][:64, 32:] = c["sel2"][64:, :32] = -0.5
    c["seli"] = np.zeros((128, 64), f)
    c["seli"][64 + np.arange(64), np.arange(64)] = 1
    c["selk"] = np.zeros((64, 32), f)
    c["selk"][32 + i32, i32] = 1
    c["j64"] = np.full((64, 128), 1.0 / E, f)
    c["c64"] = (np.eye(64) - 1.0 / E).astype(f)
    c["c64pad"] = np.pad(c["c64"], ((0, 0), (0, 64)))
    c["i64pad"] = np.eye(64, 128, dtype=f)
    c["last65"] = (np.arange(65) == 64).astype(f)[:, None]
    c["jm768"] = np.full((128, 128), 1.0 / D, f)
    c["sel8"] = (np.arange(NX * NR).reshape(1, MT, 128) // NR == np.arange(NX)[:, None, None]).astype(f)
    c["desc"] = np.tile(np.arange(NX, 0, -1, dtype=f), (CH, NCH, 1))
    return c


def by_parity(a):
    a = np.moveaxis(a, -3, 0)
    a = np.moveaxis(a, (-2, -1), (0, 2))
    return a[0:2].reshape((2 * E,) + a.shape[2:]), a[2]


def layouts(a):
    f = np.float32
    w = {}
    xp = np.zeros((B, 3, XROWS, XP), f)
    xp[:, :, 1:IMG + 1, 1:IMG + 1] = a["x"]
    w["x"] = xp
    t = {k[len("L0_tok_"):]: v for k, v in a.items() if k.startswith("L0_tok_")}
    gain = np.zeros((32, 32), f)
    gain[np.arange(F1), np.arange(F1)] = t["p1_n1_g"]
    gain[:F1, F1] = t["p1_n1_b"]
    gain[F1, F1] = 1
    w["gain1"] = np.tile(gain, (1, G))
    wt = np.zeros((32, 192), f)
    wt[:F1] = t["p1_kqv_w"].T
    wt[F1] = t["p1_kqv_b"]
    w["wt1"] = wt
    w["pb1"] = t["p1_proj_b"][None]
    w["pw1"] = t["p1_proj_w"]
    w["pwt1"] = t["p1_proj_w"].T
    w["wfeat1"] = t["p1_w"].T
    for name in ("m1", "m2"):
        bd = np.zeros((128, 128), f)
        bd[:64, :64] = bd[64:, 64:] = t[f"p1_{name}_w"].T
        w[f"{name}bd1"] = bd
    for name, key in (("g21", "n2_g"), ("b21", "n2_b"), ("m1b1", "m1_b"), ("m2b1", "m2_b")):
        w[name] = np.tile(t["p1_" + key], 2)[:, None]
    taps = t["p2_kqv_w"].reshape(192, E, 3, 3)
    w["wa2"], w["wb2"] = by_parity(taps)
    w["wn2"] = taps[:128].reshape(2, E, E, 3, 3).transpose(1, 0, 4, 3, 2).reshape(E, 2, 9 * E)
    w["ga2"], w["gb2"] = by_parity(t["p2_n1_g"].reshape(E, 3, 3))
    w["ba2"], w["bb2"] = by_parity(t["p2_n1_b"].reshape(E, 3, 3))
    w["wfeat2"] = t["p2_w"].T
    w["wsel2"] = np.zeros((128, 64), f)
    w["wsel2"][:64, 32:] = w["wsel2"][64:, :32] = t["p2_w"].T
    w["kqb2"], w["vb2"] = t["p2_kqv_b"][:128, None], t["p2_kqv_b"][128:, None]
    w["pb2"], w["pw2"], w["pwt2"] = t["p2_proj_b"][:, None], t["p2_proj_w"], t["p2_proj_w"].T
    w["m1t2"], w["m2t2"] = (np.pad(t[f"p2_{k}_w"].T, ((0, 0), (0, 64))) for k in ("m1", "m2"))
    w["g22"], w["b22"] = t["p2_n2_g"][:, None], t["p2_n2_b"][:, None]
    w["m1b2"], w["m2b2"] = t["p2_m1_b"][:, None], t["p2_m2_b"][:, None]


    def chunks(m):
        return m.reshape((-1, 128) + m.shape[1:]).swapaxes(0, 1)

    w["wpa"], w["wpb"] = by_parity(t["proj_w"].reshape(D, E, 3, 3))
    w["pbias"] = chunks(t["proj_b"])
    s = {k[len("L0_attn_"):]: v for k, v in a.items() if k.startswith("L0_attn_")}
    w["wbc"] = chunks(np.concatenate([s["W_B"], s["W_C"]], 1))
    w["bbc"] = np.concatenate([s["b_B"], s["b_C"]])[:, None]
    w["wd"] = chunks(s["W_D"][:, 0])
    w["pd"] = np.pad(chunks(s["p_Delta"]), ((0, 0), (0, 1)))
    w["bd"] = np.tile(s["b_D"], 128)[:, None]
    w["aa"] = chunks(s["A"])
    r = {k[len("L0_ffn_"):]: v for k, v in a.items() if k.startswith("L0_ffn_")}
    w["enc"], w["encb"] = chunks(r["enc_w"]), r["enc_b"][:, None]
    w["sw"], w["swb"] = r["sw_w"], np.tile(r["sw_b"], (CH, NCH, 1))
    w["w1"] = chunks(r["w1"].transpose(1, 0, 2).reshape(D, NX * NR))
    w["b1"] = chunks(r["b1"].reshape(-1))
    w["w2"] = chunks(r["w2"].reshape(NX * NR, D))
    w["b2"] = r["b2"]
    return w


def kernel(**inputs):
    import concourse.bacc as bacc
    from concourse.bass_utils import run_bass_kernel_spmd

    nc = bacc.Bacc("TRN2", target_bir_lowering=False, num_devices=1)
    arrays, w, c = {}, {}, {}
    host = layouts({k: np.asarray(v) for k, v in inputs.items()})
    for group, into in ((host, w), (shape_constants(), c)):
        for name, a in group.items():
            a = np.ascontiguousarray(a)
            arrays["in_" + name] = a
            into[name] = nc.dram_tensor("in_" + name, a.shape, F32, kind="ExternalInput").ap()
    out = nc.dram_tensor("out", (B, 3136, 768), F32, kind="ExternalOutput").ap()
    build(nc, w, c, out)
    r = run_bass_kernel_spmd(nc, [arrays], core_ids=[0])
    return r.results[0]["out"]
```

```python
from contextlib import ExitStack

import numpy as np

import concourse.bass as bass
from concourse import mybir

F32 = mybir.dt.float32
BF16 = mybir.dt.bfloat16
ALU = mybir.AluOpType
ACT = mybir.ActivationFunctionType

B = 4
IMG = 224
G = 4
F1 = 27
E = 64
M = 32
XP = IMG + 2
XROWS = XP + 1
T = 448
CH = 112
NCH = T // CH
U = 4
R1 = T // IMG
GROWS = IMG // G
J1 = GROWS // (R1 * U)
LN_EPS = 1e-5
D_EPS = 1e-8
T1ROWS = IMG + 2


def one_pass(it, u=0):
    return it * U + u + 1 + U


def last_turn(it, u=0):
    return it * U + u + 1


def before(it, per=U):
    return it * per + U


def lead(eng, *sems):
    for s in sems:
        eng.sem_inc(s, U)


def performer1(nc, sem, x, w, c, t1, h_spill):
    with ExitStack() as ctx:
        def sb(name, shape):
            return ctx.enter_context(nc.sbuf_tensor(name, shape, F32))

        ps = ctx.enter_context(nc.psum_tensor("ps1", [128, 8, 512], F32))

        def bank(k, n=T, rows=128):
            return ps[0:rows, k, 0:n]

        def banks(k):
            return ps[:, k:k + 2, 0:T]

        ident = sb("ident", [128, 128])
        bd32 = sb("bd32", [128, 128])
        srep = sb("srep", [128, 128])
        cen1 = sb("cen1", [128, 128])
        mean27 = sb("mean27", [128, 128])
        jb64 = sb("jb64", [128, 128])
        pmask = sb("pmask", [128, 2, 2, 64])
        nh = sb("nh", [128, 2, 128])
        eps1 = sb("eps1", [128, 1])
        eps64 = sb("eps64", [128, 1])
        ic64 = sb("ic64", [64, 128])
        e27 = sb("e27", [1, 128])
        gain1 = sb("gain1", [32, 128])
        wt1 = sb("wt1", [32, 192])
        pb1 = sb("pb1", [1, 64])
        pw1 = sb("pw1", [64, 64])
        pwr1 = sb("pwr1", [64, 128])
        wfeat = sb("wfeat", [64, 32])
        m1bd = sb("m1bd", [128, 128])
        m2bd = sb("m2bd", [128, 128])
        g2 = sb("g2", [128, 1])
        b2 = sb("b2", [128, 1])
        m1b = sb("m1b", [128, 1])
        m2b = sb("m2b", [128, 1])
        w1r = sb("w1r", [128, 192])
        w1t = sb("w1t", [64, 3, 128])
        wvyt = sb("wvyt", [64, 128])
        wkb = sb("wkb", [128, 2, 2, 64])
        wqb = sb("wqb", [128, 2, 2, 64])
        wvyb = sb("wvyb", [128, 2, 2, 64])
        wvycb = sb("wvycb", [128, 2, 2, 64])
        wwk = sb("wwk", [128, 4, 32])
        wwq = sb("wwq", [128, 4, 32])
        p1x = sb("p1x", [128, 129])
        m1g = sb("m1g", [128, 128])
        m1bias = sb("m1bias", [128, 1])
        khacc = sb("khacc", [128, 128])
        khm = sb("khm", [128, 128])
        t1s = sb("t1s", [128, 128])
        t2s = sb("t2s", [128, 129])
        myb = sb("myb", [128, 2, 2, 64])
        mycb = sb("mycb", [128, 2, 2, 64])
        dwb = sb("dwb", [128, 128])
        zero = sb("zero", [128, B * E // 128, IMG])
        xt = sb("xt", [128, R1 * U * XP])
        sq = sb("sq", [128, U, T])
        rs = sb("rs", [128, U, T])
        h = sb("h", [128, U, T])
        ksq = sb("ksq", [128, U, 2, T])
        kp = sb("kp", [CH, U, NCH, 128])
        ht = sb("ht", [CH, U, NCH, 128])
        hb = sb("hb", [128, U, T])
        qsq = sb("qsq", [128, U, 2, T])
        qp = sb("qp", [128, U, T])
        qpn = sb("qpn", [128, U, T])
        yc = sb("yc", [128, U, 2, T])
        ycs = sb("ycs", [128, U, 2, T])
        rs2 = sb("rs2", [128, U, 2, T])
        gl = sb("gl", [128, U, 2, T])
        ob = sb("ob", [128, U, 2, T])

        loads = [(ident, c["ident"]), (bd32, c["bd32"]), (srep, c["srep"]), (cen1, c["cen1"]),
                 (mean27, c["mean27"]), (jb64, c["jb64"]), (pmask, c["pmask"]), (nh, c["nh"]),
                 (eps1, c["eps1"]), (eps64, c["eps64"]), (ic64, c["ic64"]), (e27, c["e27"]),
                 (gain1, w["gain1"]), (wt1, w["wt1"]), (pb1, w["pb1"]), (pw1, w["pw1"]),
                 (pwr1[:, 0:64], w["pwt1"]), (wfeat, w["wfeat1"]), (m1bd, w["m1bd1"]),
                 (m2bd, w["m2bd1"]), (g2, w["g21"]), (b2, w["b21"]), (m1b, w["m1b1"]),
                 (m2b, w["m2b1"]), (p1x[:, 128:129], c["e27col"])]

        s_w = sem("p1_weights_loaded")
        s_ones = sem("p1_ones_set")
        s_prep_mm = sem("p1_prep_products")
        s_prep = sem("p1_prep_copied")
        s_x = sem("p1_x_loaded")
        s_cen = sem("p1_centred")
        s_sq = sem("p1_squared")
        s_var = sem("p1_variance")
        s_ln = sem("p1_log_variance")
        s_rs = sem("p1_inverse_deviation")
        s_h = sem("p1_h_written")
        s_hst = sem("p1_h_stored")
        s_k = sem("p1_k_product")
        s_ksq = sem("p1_k_squared")
        s_tok = sem("p1_token_major")
        s_kp = sem("p1_kp_written")
        s_ht = sem("p1_ht_written")
        s_kh = sem("p1_kh_summed")
        s_khadd = sem("p1_kh_added")
        s_khm = sem("p1_kh_masked")
        s_khz = sem("p1_kh_cleared")
        s_t1 = sem("p1_t1_product")
        s_t1s = sem("p1_t1_copied")
        s_t2 = sem("p1_t2_product")
        s_t2s = sem("p1_t2_scaled")
        s_yw = sem("p1_y_weights")
        s_hl = [sem(f"p1_h_loaded_{u}") for u in range(U)]
        s_q = sem("p1_q_product")
        s_qsq = sem("p1_q_squared")
        s_lq = sem("p1_q_logits")
        s_qp = sem("p1_qp_written")
        s_d = sem("p1_denominator")
        s_de = sem("p1_denominator_guarded")
        s_dr = sem("p1_denominator_inverse")
        s_qpn = sem("p1_qp_normalised")
        s_yc = sem("p1_y_centred")
        s_ycb = sem("p1_y_copied")
        s_ycs = sem("p1_y_squared")
        s_var2 = sem("p1_y_variance")
        s_ln2 = sem("p1_y_log_variance")
        s_rs2 = sem("p1_y_inverse_deviation")
        s_h2 = sem("p1_h2_written")
        s_m1 = sem("p1_mlp_in")
        s_gl = sem("p1_gelu_written")
        s_o = sem("p1_out_product")
        s_ob = sem("p1_out_written")
        s_t1st = sem("p1_out_stored")
        s_zero = sem("p1_zero_set")

        block = ctx.enter_context(nc.Block())

        @block.sync
        def _(sp):
            lead(sp, s_hst)
            for dst, src in loads:
                sp.dma_start(dst[...] if not isinstance(dst, bass.AP) else dst, src).then_inc(s_w, 16)
            sp.wait_ge(s_ones, 1)
            with sp.Fori(0, B) as b:
                with sp.Fori(0, J1) as j:
                    it = b * J1 + j
                    sp.wait_ge(s_cen, before(it))
                    for g in range(G):
                        for ch in range(3):
                            row = GROWS * g + j * (R1 * U)
                            src = bass.AP(x.tensor, (b * 3 + ch) * (XROWS * XP) + row * XP,
                                          [[XP, 3], [1, 3], [1, R1 * U * XP]])
                            sp.dma_start(xt[32 * g + 9 * ch:32 * g + 9 * ch + 9, :], src).then_inc(s_x, 16)
                    for u in range(U):
                        sp.wait_ge(s_h, one_pass(it, u))
                        sp.dma_start(h_spill[it * U + u], h[:, u, :]).then_inc(s_hst, 16)
                with sp.Fori(0, J1) as j:
                    it = b * J1 + j
                    sp.wait_ge(s_hst, before(b + 1, J1 * U * 16))
                    for u in range(U):
                        sp.wait_ge(s_o, last_turn(it, u))
                        sp.dma_start(hb[:, u, :], h_spill[it * U + u]).then_inc(s_hl[u], 16)

        @block.gpsimd
        def _(pool):
            pool.memset(xt[:, :], 1.0).then_inc(s_ones, 1)
            pool.memset(zero[:, :, :], 0.0).then_inc(s_zero, 1)
            pool.wait_ge(s_zero, 1)
            pool.dma_start(bass.AP(t1.tensor, 0, [[T1ROWS * IMG, B * E], [1, IMG]]), zero[:, :, :]).then_inc(s_t1st, 16)
            with pool.Fori(0, B) as b:
                with pool.Fori(0, J1) as j:
                    it = b * J1 + j
                    for u in range(U):
                        pool.wait_ge(s_ob, one_pass(it, u))
                        for p in range(2):
                            for gl_ in range(2):
                                row = 1 + GROWS * (2 * p + gl_) + R1 * u + j * (R1 * U)
                                dst = bass.AP(t1.tensor, b * (E * T1ROWS * IMG) + row * IMG,
                                              [[T1ROWS * IMG, E], [1, T]])
                                pool.dma_start(dst, ob[64 * gl_:64 * gl_ + 64, u, p, :]).then_inc(s_t1st, 16)
            pool.wait_ge(s_t1st, 16 + B * J1 * U * 4 * 16)

        @block.tensor
        def _(pe):
            mm = nc.tensor.matmul
            lead(pe, s_cen, s_var, s_k, s_tok, s_q, s_lq, s_d, s_yc, s_var2, s_m1, s_o)
            pe.wait_ge(s_w, 16 * len(loads))
            mm(bank(0, 192), gain1[:, :], wt1[:, :], start=True, stop=True)
            for k in range(3):
                mm(ps[0:64, 1, 128 * k:128 * k + 128], wt1[:, 64 * k:64 * k + 64], gain1[:, :], start=True, stop=True)
            mm(bank(2, 128, 64), wt1[:, 128:192], gain1[:, :], start=True, stop=False)
            mm(bank(2, 128, 64), pb1[:, :], e27[:, :], start=False, stop=True)
            mm(bank(7, 1), m1bd[:, :], b2[:, :], start=True, stop=True)
            mm(bank(3, 64, 64), pw1[:, :], ic64[:, 64:128], start=True, stop=True).then_inc(s_prep_mm, 1)
            pe.wait_ge(s_prep, 4)
            mm(ps[:, 4, 0:32], w1t[:, 0, :], wfeat[:, :], start=True, stop=True)
            mm(ps[:, 4, 32:64], w1t[:, 1, :], wfeat[:, :], start=True, stop=True)
            mm(bank(5, 128), wvyt[:, :], ic64[:, :], start=True, stop=True)
            mm(bank(6, 128), w1t[:, 2, :], pwr1[:, :], start=True, stop=True).then_inc(s_prep_mm, 1)
            pe.wait_ge(s_prep, 17)
            with pe.Fori(0, B) as b:
                with pe.Fori(0, J1) as j:
                    it = b * J1 + j
                    pe.wait_ge(s_khadd, before(it, 1))
                    pe.wait_ge(s_ob, before(b, J1 * U))
                    pe.wait_ge(s_x, (it + 1) * (16 * G * 3))
                    for u in range(U):
                        rows = xt[:, u * R1 * XP:(u + 1) * R1 * XP].rearrange("p (r c) -> p r c", c=XP)
                        mm(ps[:, u, 0:T], cen1[:, :], rows[:, :, 0:IMG], start=True, stop=True).then_inc(s_cen, 1)
                    for u in range(U):
                        pe.wait_ge(s_sq, one_pass(it, u))
                        mm(bank(4 + u), mean27[:, :], sq[:, u, :], start=True, stop=True).then_inc(s_var, 1)
                    for u in range(U):
                        if u == 0:
                            pe.wait_ge(s_h, one_pass(it, U - 1))
                        for p in range(2):
                            last = mm(bank(2 * u + p), wkb[:, p], h[:, u, :], start=True, stop=True)
                        last.then_inc(s_k, 1)
                    for u in range(U):
                        pe.wait_ge(s_ksq, one_pass(it, u))
                        for ch in range(NCH):
                            cs = slice(ch * CH, ch * CH + CH)
                            o = ps[0:CH, 2 * u, 128 * ch:128 * ch + 128]
                            mm(o, h[:, u, cs], wwk[:, :, :], start=True, stop=False)
                            mm(o, ksq[:, u, 0, cs], nh[:, 0, :], start=False, stop=False)
                            mm(o, ksq[:, u, 1, cs], nh[:, 1, :], start=False, stop=True)
                        for ch in range(NCH):
                            cs = slice(ch * CH, ch * CH + CH)
                            last = mm(ps[0:CH, 2 * u + 1, 128 * ch:128 * ch + 128], h[:, u, cs], ident[:, :],
                                      start=True, stop=True)
                        last.then_inc(s_tok, 1)
                    for u in range(U):
                        pe.wait_ge(s_kp, one_pass(it, u))
                        pe.wait_ge(s_ht, one_pass(it, u))
                        for ch in range(NCH):
                            last = mm(bank(0, 128), kp[:, u, ch, :], ht[:, u, ch, :],
                                      start=(u == 0 and ch == 0), stop=(u == U - 1 and ch == NCH - 1))
                    last.then_inc(s_kh, 1)
                pe.wait_ge(s_khm, b + 1)
                mm(bank(1, 128), khm[:, :], srep[:, :], start=True, stop=True).then_inc(s_t1, 1)
                pe.wait_ge(s_t1s, b + 1)
                mm(bank(2, 129), t1s[:, :], p1x[:, :], start=True, stop=True).then_inc(s_t2, 1)
                with pe.Fori(0, J1) as j:
                    it = b * J1 + j
                    pe.wait_ge(s_yw, 5 * (b + 1))
                    for u in range(U):
                        pe.wait_ge(s_ob, last_turn(it, u))
                        pe.wait_ge(s_hl[u], (it + 1) * 16)
                        for p in range(2):
                            last = mm(bank(2 * u + p), wqb[:, p], hb[:, u, :], start=True, stop=True)
                        last.then_inc(s_q, 1)
                    for u in range(U):
                        pe.wait_ge(s_qsq, one_pass(it, u))
                        mm(bank(u), wwq[:, :, :], hb[:, u, :], start=True, stop=False)
                        mm(bank(u), nh[:, 0, :], qsq[:, u, 0, :], start=False, stop=False)
                        mm(bank(u), nh[:, 1, :], qsq[:, u, 1, :], start=False, stop=True).then_inc(s_lq, 1)
                    for u in range(U):
                        pe.wait_ge(s_qp, one_pass(it, u))
                        mm(bank(4 + u), dwb[:, :], qp[:, u, :], start=True, stop=True).then_inc(s_d, 1)
                    for u in range(U):
                        pe.wait_ge(s_qpn, one_pass(it, u if u < 2 else U - 1))
                        for p in range(2):
                            mm(bank(2 * u + p), mycb[:, p], qpn[:, u, :], start=True, stop=False)
                            last = mm(bank(2 * u + p), wvycb[:, p], hb[:, u, :], start=False, stop=True)
                        last.then_inc(s_yc, 1)
                    for u in range(U):
                        pe.wait_ge(s_ycs, one_pass(it, u))
                        for p in range(2):
                            last = mm(bank(2 * u + p), jb64[:, :], ycs[:, u, p, :], start=True, stop=True)
                        last.then_inc(s_var2, 1)
                    for u in range(U):
                        pe.wait_ge(s_h2, one_pass(it, u))
                        for p in range(2):
                            last = mm(bank(2 * u + p), m1g[:, :], yc[:, u, p, :], start=True, stop=True)
                        last.then_inc(s_m1, 1)
                    for u in range(U):
                        pe.wait_ge(s_gl, one_pass(it, u))
                        for p in range(2):
                            mm(bank(2 * u + p), myb[:, p], qpn[:, u, :], start=True, stop=False)
                            mm(bank(2 * u + p), wvyb[:, p], hb[:, u, :], start=False, stop=False)
                            last = mm(bank(2 * u + p), m2bd[:, :], gl[:, u, p, :], start=False, stop=True)
                        last.then_inc(s_o, 1)

        @block.scalar
        def _(act):
            fn = nc.scalar.activation
            lead(act, s_sq, s_ln, s_rs, s_ksq, s_kp, s_qsq, s_qp, s_ycs, s_ln2, s_rs2, s_gl)
            act.wait_ge(s_w, 16 * len(loads))
            act.wait_ge(s_prep, 17)
            with act.Fori(0, B) as b:
                with act.Fori(0, J1) as j:
                    it = b * J1 + j
                    for u in range(U):
                        act.wait_ge(s_cen, one_pass(it, u))
                        fn(sq[:, u, :], bank(u), ACT.Square).then_inc(s_sq, 1)
                    for u in range(U):
                        act.wait_ge(s_var, one_pass(it, u))
                        fn(rs[:, u, :], bank(4 + u), ACT.Ln, bias=eps1[:, :]).then_inc(s_ln, 1)
                    for u in range(U):
                        act.wait_ge(s_ln, one_pass(it, u))
                        fn(rs[:, u, :], rs[:, u, :], ACT.Exp, scale=-0.5).then_inc(s_rs, 1)
                    for u in range(U):
                        act.wait_ge(s_k, one_pass(it, u))
                        fn(ksq[:, u], banks(2 * u), ACT.Square).then_inc(s_ksq, 1)
                    for u in range(U):
                        act.wait_ge(s_tok, one_pass(it, u))
                        fn(kp[:, u], ps[0:CH, 2 * u, :], ACT.Exp).then_inc(s_kp, 1)
                with act.Fori(0, J1) as j:
                    it = b * J1 + j
                    for u in range(U):
                        act.wait_ge(s_q, one_pass(it, u))
                        fn(qsq[:, u], banks(2 * u), ACT.Square).then_inc(s_qsq, 1)
                    for u in range(U):
                        act.wait_ge(s_lq, one_pass(it, u))
                        fn(qp[:, u, :], bank(u), ACT.Exp).then_inc(s_qp, 1)
                    for u in range(U):
                        act.wait_ge(s_ycb, one_pass(it, u))
                        fn(ycs[:, u], yc[:, u], ACT.Square).then_inc(s_ycs, 1)
                    for u in range(U):
                        act.wait_ge(s_var2, one_pass(it, u))
                        fn(rs2[:, u], banks(2 * u), ACT.Ln, bias=eps64[:, :]).then_inc(s_ln2, 1)
                    for u in range(U):
                        act.wait_ge(s_ln2, one_pass(it, u))
                        fn(rs2[:, u], rs2[:, u], ACT.Exp, scale=-0.5).then_inc(s_rs2, 1)
                    for u in range(U):
                        act.wait_ge(s_m1, one_pass(it, u))
                        fn(gl[:, u], banks(2 * u), ACT.Gelu, bias=m1bias[:, :]).then_inc(s_gl, 1)

        @block.vector
        def _(dve):
            tt = nc.vector.tensor_tensor
            cp = nc.vector.tensor_copy

            def spread(a):
                return a.unsqueeze(1).to_broadcast([128, 2, 64])

            lead(dve, s_h, s_ht, s_khadd, s_de, s_dr, s_qpn, s_ycb, s_h2, s_ob)
            dve.memset(khacc[:, :], 0.0).then_inc(s_khz, 1)
            dve.wait_ge(s_w, 16 * len(loads))
            dve.wait_ge(s_prep_mm, 1)
            cp(w1r[:, :], bank(0, 192)).then_inc(s_prep, 1)
            cp(w1t[:, :, :], ps[0:64, 1, 0:384]).then_inc(s_prep, 1)
            cp(wvyt[:, :], bank(2, 128, 64)).then_inc(s_prep, 1)
            cp(pwr1[:, 64:128], bank(3, 64, 64)).then_inc(s_prep, 1)
            dve.wait_ge(s_prep, 4)
            for p in range(2):
                tt(wkb[:, p], spread(w1r[:, 0:64]), pmask[:, p], ALU.mult).then_inc(s_prep, 1)
                tt(wqb[:, p], spread(w1r[:, 64:128]), pmask[:, p], ALU.mult).then_inc(s_prep, 1)
            dve.wait_ge(s_prep_mm, 2)
            for p in range(2):
                tt(wvyb[:, p], spread(ps[:, 5, 0:64]), pmask[:, p], ALU.mult).then_inc(s_prep, 1)
                tt(wvycb[:, p], spread(ps[:, 5, 64:128]), pmask[:, p], ALU.mult).then_inc(s_prep, 1)
            for dst, lo in ((wwk, 0), (wwq, 32)):
                tt(dst[:, :, :], ps[:, 4, lo:lo + 32].unsqueeze(1).to_broadcast([128, 4, 32]),
                   bd32[:, :].rearrange("p (g m) -> p g m", g=4), ALU.mult).then_inc(s_prep, 1)
            cp(p1x[:, 0:128], bank(6, 128)).then_inc(s_prep, 1)
            nc.vector.tensor_scalar(m1g[:, :], m1bd[:, :], g2[:, :], None, ALU.mult).then_inc(s_prep, 1)
            tt(m1bias[:, :], bank(7, 1), m1b[:, :], ALU.add).then_inc(s_prep, 1)
            with dve.Fori(0, B) as b:
                with dve.Fori(0, J1) as j:
                    it = b * J1 + j
                    dve.wait_ge(s_khz, b + 1)
                    for u in range(U):
                        dve.wait_ge(s_rs, one_pass(it, u))
                        if u == 0:
                            dve.wait_ge(s_hst, before(it, U * 16))
                        tt(h[:, u, :], bank(u), rs[:, u, :], ALU.mult).then_inc(s_h, 1)
                    for u in range(U):
                        dve.wait_ge(s_tok, one_pass(it, u))
                        cp(ht[:, u], ps[0:CH, 2 * u + 1, :]).then_inc(s_ht, 1)
                    dve.wait_ge(s_kh, it + 1)
                    dve.wait_ge(s_khadd, before(it, 1))
                    tt(khacc[:, :], khacc[:, :], bank(0, 128), ALU.add).then_inc(s_khadd, 1)
                dve.wait_ge(s_khadd, before(b + 1, J1))
                tt(khm[:, :], khacc[:, :], bd32[:, :], ALU.mult).then_inc(s_khm, 1)
                dve.wait_ge(s_khm, b + 1)
                dve.memset(khacc[:, :], 0.0).then_inc(s_khz, 1)
                dve.wait_ge(s_t1, b + 1)
                cp(t1s[:, :], bank(1, 128)).then_inc(s_t1s, 1)
                dve.wait_ge(s_t2, b + 1)
                nc.vector.tensor_scalar(t2s[:, :], bank(2, 129), 1.0 / M, None, ALU.mult).then_inc(s_t2s, 1)
                dve.wait_ge(s_t2s, b + 1)
                for p in range(2):
                    tt(myb[:, p], spread(t2s[:, 0:64]), pmask[:, p], ALU.mult).then_inc(s_yw, 1)
                    tt(mycb[:, p], spread(t2s[:, 64:128]), pmask[:, p], ALU.mult).then_inc(s_yw, 1)
                nc.vector.tensor_scalar(dwb[:, :], bd32[:, :], t2s[:, 128:129], None, ALU.mult).then_inc(s_yw, 1)
                with dve.Fori(0, J1) as j:
                    it = b * J1 + j
                    for u in range(U):
                        dve.wait_ge(s_d, one_pass(it, u))
                        nc.vector.tensor_scalar(qpn[:, u, :], bank(4 + u), D_EPS, None, ALU.add).then_inc(s_de, 1)
                        dve.wait_ge(s_de, one_pass(it, u))
                        nc.vector.reciprocal(qpn[:, u, :], qpn[:, u, :]).then_inc(s_dr, 1)
                        dve.wait_ge(s_dr, one_pass(it, u))
                        tt(qpn[:, u, :], qp[:, u, :], qpn[:, u, :], ALU.mult).then_inc(s_qpn, 1)
                    for u in range(U):
                        dve.wait_ge(s_yc, one_pass(it, u))
                        cp(yc[:, u], banks(2 * u)).then_inc(s_ycb, 1)
                    for u in range(U):
                        dve.wait_ge(s_rs2, one_pass(it, u))
                        tt(yc[:, u], yc[:, u], rs2[:, u], ALU.mult).then_inc(s_h2, 1)
                    for u in range(U):
                        dve.wait_ge(s_o, one_pass(it, u))
                        if u == 0:
                            dve.wait_ge(s_t1st, it * (U * 4 * 16) + 16)
                        nc.vector.tensor_scalar(ob[:, u], banks(2 * u), m2b[:, :], None, ALU.add).then_inc(s_ob, 1)


S2 = IMG // 2
TR2 = T // S2
J2 = S2 // (TR2 * U)
T2ROWS = S2 + 2


def performer2(nc, sem, w, c, t1, vq_spill, t2):
    with ExitStack() as ctx:
        def sb(name, shape):
            return ctx.enter_context(nc.sbuf_tensor(name, shape, F32))

        ps = ctx.enter_context(nc.psum_tensor("ps2", [128, 8, 512], F32))

        def bank(k, n=T, rows=128):
            return ps[0:rows, k, 0:n]

        ident = sb("ident2", [128, 128])
        ones576 = sb("ones576", [128, 128])
        sel2 = sb("sel2", [128, 64])
        seli = sb("seli", [128, 64])
        selk = sb("selk", [64, 32])
        j64 = sb("j64", [64, 128])
        c64 = sb("c64", [64, 64])
        eps64 = sb("eps64b", [128, 1])
        wa = sb("wa", [128, 3, 256])
        wb = sb("wb", [64, 3, 256])
        wn = sb("wn", [64, 2, 576])
        ga = sb("ga", [128, 3])
        gb = sb("gb", [64, 3])
        ba = sb("ba", [128, 3])
        bb = sb("bb", [64, 3])
        wfeat = sb("wfeat2", [64, 32])
        wsel = sb("wsel2", [128, 64])
        kqb = sb("kqb2", [128, 1])
        vb = sb("vb2", [64, 1])
        pb = sb("pb2", [64, 1])
        pw = sb("pw2", [64, 64])
        prj = sb("prj2", [64, 128])
        m1 = sb("m1t2", [64, 128])
        m2 = sb("m2t2", [64, 128])
        g2 = sb("g22", [64, 1])
        b2 = sb("b22", [64, 1])
        m1b = sb("m1b2", [64, 1])
        m2b = sb("m2b2", [64, 1])
        bkq = sb("bkq", [128, 1])
        bvp = sb("bvp", [64, 1])
        iv = sb("iv", [64, 65])
        by = sb("by", [64, 1])
        bo = sb("bo", [64, 1])
        blq = sb("blq", [64, 1])
        rr = sb("rr", [65, 129])
        m1g = sb("m1g2", [64, 128])
        m1bias = sb("m1bias2", [64, 1])
        kvacc = sb("kvacc", [65, 96])
        dw = sb("dw2", [96, 96])
        ycw = sb("ycw", [96, 128])
        yw = sb("yw", [96, 128])
        ones32 = sb("ones32", [96, 32])
        kps = sb("kps", [96, 1])
        xt = sb("xt2", [128, U, TR2 + 1, XP])
        xs = sb("xs2", [128, U, TR2 + 1, XP])
        cs = sb("cs2", [128, U, TR2 + 1, S2])
        css = sb("css2", [128, U, TR2 + 1, S2])
        ms = sb("ms2", [128, U, T])
        rs = sb("rsa2", [128, U, T])
        kq = sb("kq2", [128, U, T])
        vl = sb("vl2", [128, U, T])
        kpq = sb("kpq2", [64, U, T])
        vt = sb("vt2", [CH, U, NCH, 97])
        vq = sb("vq2", [96, U, T])
        dn = sb("dn2", [96, U, T])
        yc = sb("yc2", [64, U, T])
        ycs = sb("ycs2", [64, U, T])
        rs2 = sb("rs22", [64, U, T])
        gl = sb("gl2", [64, U, T])
        ob = sb("ob2", [64, U, T])

        loads = [(ident, c["ident"]), (ones576, c["ones576"]), (sel2, c["sel2"]), (seli, c["seli"]),
                 (selk, c["selk"]), (j64, c["j64"]), (c64, c["c64"]), (eps64, c["eps64"]),
                 (wa[:, :, 0:192], w["wa2"]), (wb[:, :, 0:192], w["wb2"]), (wn, w["wn2"]), (ga, w["ga2"]),
                 (gb, w["gb2"]), (ba, w["ba2"]), (bb, w["bb2"]), (wfeat, w["wfeat2"]), (wsel, w["wsel2"]),
                 (kqb, w["kqb2"]), (vb, w["vb2"]), (pb, w["pb2"]), (pw, w["pw2"]), (prj[:, 0:64], w["pwt2"]),
                 (m1, w["m1t2"]), (m2, w["m2t2"]), (g2, w["g22"]), (b2, w["b22"]), (m1b, w["m1b2"]),
                 (m2b, w["m2b2"]), (iv[:, 0:64], c["ident"][0:64, 0:64]), (ycw[0:64, :], c["c64pad"]),
                 (yw[0:64, :], c["i64pad"]), (rr[0:65, 128:129], c["last65"])]

        s_w = sem("p2_weights_loaded")
        s_set = sem("p2_buffers_set")
        s_pm = sem("p2_prep_products")
        s_pd = sem("p2_prep_written")
        s_x = [sem(f"p2_x_loaded_{u}") for u in range(U)]
        s_xs = sem("p2_x_squared")
        s_cs = sem("p2_column_sums")
        s_css = sem("p2_column_sums_of_squares")
        s_c1 = sem("p2_column_pairs_added")
        s_st = sem("p2_statistics")
        s_kq = sem("p2_kq_product")
        s_vl = sem("p2_vl_product")
        s_ms = sem("p2_mean_squared")
        s_va = sem("p2_variance")
        s_lv = sem("p2_log_variance")
        s_rs = sem("p2_inverse_deviation")
        s_kqn = sem("p2_kq_normalised")
        s_kqs = sem("p2_kq_squared")
        s_vln = sem("p2_vl_normalised")
        s_lg = sem("p2_logits")
        s_kpq = sem("p2_kpq_written")
        s_tr = sem("p2_transposed")
        s_vt = sem("p2_vt_written")
        s_kv = sem("p2_kv_product")
        s_kva = sem("p2_kv_added")
        s_vst = sem("p2_v_and_q_stored")
        s_mp = sem("p2_matrix_product")
        s_yw = sem("p2_y_weights")
        s_kps = sem("p2_kp_sum_scaled")
        s_kvz = sem("p2_kv_cleared")
        s_vql = [sem(f"p2_v_and_q_loaded_{u}") for u in range(U)]
        s_d = sem("p2_denominator")
        s_de = sem("p2_denominator_guarded")
        s_dr = sem("p2_denominator_inverse")
        s_qn = sem("p2_qp_normalised")
        s_yc = sem("p2_y_centred")
        s_ycb = sem("p2_y_copied")
        s_ycs = sem("p2_y_squared")
        s_v2 = sem("p2_y_variance")
        s_l2 = sem("p2_y_log_variance")
        s_r2 = sem("p2_y_inverse_deviation")
        s_h2 = sem("p2_h2_written")
        s_m1 = sem("p2_mlp_in")
        s_gl = sem("p2_gelu_written")
        s_o = sem("p2_out_product")
        s_ob = sem("p2_out_written")
        s_t2 = sem("p2_out_stored")
        s_zero = sem("p2_zero_set")

        block = ctx.enter_context(nc.Block())

        @block.sync
        def _(sp):
            for dst, src in loads:
                sp.dma_start(dst[...] if not isinstance(dst, bass.AP) else dst, src).then_inc(s_w, 16)
            sp.wait_ge(s_set, 3)
            with sp.Fori(0, B) as b:
                with sp.Fori(0, J2) as j:
                    it = b * J2 + j
                    for u in range(U):
                        sp.wait_ge(s_vl, last_turn(it, u))
                        sp.wait_ge(s_css, last_turn(it, u))
                        for par in range(2):
                            rows = TR2 + 1 - par
                            src = bass.AP(t1.tensor, b * (E * T1ROWS * IMG) + j * (U * TR2 * 2 * IMG)
                                          + (u * TR2 * 2 + par) * IMG,
                                          [[T1ROWS * IMG, E], [2 * IMG, rows], [1, IMG]])
                            sp.dma_start(xt[64 * par:64 * par + 64, u, 0:rows, 1:IMG + 1], src).then_inc(s_x[u], 16)
                with sp.Fori(0, J2) as j:
                    it = b * J2 + j
                    sp.wait_ge(s_vst, before(b + 1, J2 * U * 32))
                    for u in range(U):
                        sp.wait_ge(s_o, last_turn(it, u))
                        sp.dma_start(vq[:, u, :], vq_spill[it * U + u]).then_inc(s_vql[u], 16)

        @block.gpsimd
        def _(pool):
            lead(pool, s_c1, s_cs, s_css)
            pool.memset(ob[:, 0, :], 0.0).then_inc(s_zero, 1)
            pool.wait_ge(s_zero, 1)
            for b in range(B):
                pool.dma_start(bass.AP(t2.tensor, b * E * T2ROWS * S2, [[T2ROWS * S2, E], [1, S2]]),
                               ob[:, 0, 0:S2]).then_inc(s_t2, 16)
            pool.memset(xt[:, :, :, :], 0.0).then_inc(s_set, 1)
            pool.memset(vt[:, :, :, :], 1.0).then_inc(s_set, 1)
            pool.memset(ones32[:, :], 1.0).then_inc(s_set, 1)
            add = nc.gpsimd.tensor_tensor
            with pool.Fori(0, B) as b:
                with pool.Fori(0, J2) as j:
                    it = b * J2 + j
                    for u in range(U):
                        for src, dst, s_src, s_dst, at in ((xt, cs, s_x[u], s_cs, (it + 1) * 32),
                                                           (xs, css, s_xs, s_css, one_pass(it, u))):
                            first = 1 if s_dst is s_cs else 2
                            pool.wait_ge(s_src, at)
                            a = src[:, u, :, 0:2 * S2].rearrange("p r (c two) -> p r c two", two=2)
                            add(dst[:, u], a[:, :, :, 0], a[:, :, :, 1], ALU.add).then_inc(s_c1, 1)
                            pool.wait_ge(s_c1, it * (2 * U) + 2 * u + first + U)
                            a = src[:, u, :, 2:2 * S2 + 2].rearrange("p r (c two) -> p r c two", two=2)
                            add(dst[:, u], dst[:, u], a[:, :, :, 0], ALU.add).then_inc(s_dst, 1)
                with pool.Fori(0, J2) as j:
                    it = b * J2 + j
                    for u in range(U):
                        pool.wait_ge(s_ob, one_pass(it, u))
                        dst = bass.AP(t2.tensor, b * (E * T2ROWS * S2) + j * (U * TR2 * S2) + (1 + u * TR2) * S2,
                                      [[T2ROWS * S2, E], [1, T]])
                        pool.dma_start(dst, ob[:, u, :]).then_inc(s_t2, 16)
            pool.wait_ge(s_t2, 16 * B + B * J2 * U * 16)

        @block.tensor
        def _(pe):
            mm = nc.tensor.matmul
            lead(pe, s_st, s_kq, s_vl, s_lg, s_tr, s_kv, s_d, s_yc, s_v2, s_m1, s_o)
            pe.wait_ge(s_w, 16 * len(loads))
            for j in range(3):
                for k, lo in ((1, 0), (0, 32)):
                    mm(ps[:, 0, 64 * j + lo:64 * j + lo + 32], wn[:, k, 192 * j:192 * j + 128], wfeat[:, :],
                       start=True, stop=True)
                    mm(ps[0:64, 1, 64 * j + lo:64 * j + lo + 32], wn[:, k, 192 * j + 128:192 * j + 192],
                       wfeat[:, :], start=True, stop=True)
            for j in range(3):
                mm(bank(2, 1), wa[:, j, 0:128], ba[:, j:j + 1], start=(j == 0), stop=False)
            for j in range(3):
                mm(bank(2, 1), wb[:, j, 0:128], bb[:, j:j + 1], start=False, stop=(j == 2))
            for j in range(3):
                mm(bank(3, 1, 64), wa[:, j, 128:192], ba[:, j:j + 1], start=(j == 0), stop=False)
            for j in range(3):
                mm(bank(3, 1, 64), wb[:, j, 128:192], bb[:, j:j + 1], start=False, stop=(j == 2))
            mm(bank(7, 1), m1[:, :], b2[:, :], start=True, stop=True)
            mm(bank(6, 64, 64), pw[:, :], c64[:, :], start=True, stop=True).then_inc(s_pm, 1)
            pe.wait_ge(s_pd, 11)
            for j in range(3):
                mm(bank(4, 256), ones576[:, :], wa[:, j, :], start=(j == 0), stop=False)
            for j in range(3):
                mm(bank(4, 256), ones576[0:64, :], wb[:, j, :], start=False, stop=(j == 2))
            mm(bank(5, 1, 64), wsel[:, :], bkq[:, :], start=True, stop=True)
            mm(bank(0, 1, 64), c64[:, :], bvp[:, :], start=True, stop=True)
            mm(bank(1, 128, 65), iv[:, :], prj[:, :], start=True, stop=True).then_inc(s_pm, 1)
            pe.wait_ge(s_pd, 19)

            def taps(o, view, cols):
                for j in range(3):
                    mm(o, wa[:, j, cols], view(0, 128, j), start=(j == 0), stop=False)
                for j in range(3):
                    last = mm(o, wb[:, j, cols], view(1, 64, j), start=False, stop=(j == 2))
                return last

            def pixels(u):
                return lambda r, n, j: xt[0:n, u, r:r + TR2, j:j + 2 * S2 - 1:2]

            def statistics(it, u):
                base = 4 * (u % 2)
                pe.wait_ge(s_css, one_pass(it, u))
                pe.wait_ge(s_cs, one_pass(it, u))
                for k, a in ((2, cs), (3, css)):
                    o = bank(base + k)
                    mm(o, ones576[:, :], a[:, u, 0:TR2, :], start=True, stop=False)
                    last = mm(o, ones576[0:64, :], a[0:64, u, 1:TR2 + 1, :], start=False, stop=True)
                last.then_inc(s_st, 1)

            def conv_kq(it, u):
                taps(bank(4 * (u % 2)), pixels(u), slice(0, 128)).then_inc(s_kq, 1)

            def conv_vl(it, u):
                if u < 2:
                    pe.wait_ge(s_kva, before(it))
                else:
                    pe.wait_ge(s_kva, one_pass(it, u - 2))
                taps(bank(4 * (u % 2) + 1), pixels(u), slice(128, 256)).then_inc(s_vl, 1)

            def logits(it, u):
                o = bank(4 * (u % 2) + 2, T, 64)
                pe.wait_ge(s_vln, one_pass(it, u))
                mm(o, seli[:, :], vl[:, u, :], start=True, stop=False)
                pe.wait_ge(s_kqs, one_pass(it, u))
                mm(o, sel2[:, :], kq[:, u, :], start=False, stop=True).then_inc(s_lg, 1)

            def transposes(it, u):
                pe.wait_ge(s_kpq, one_pass(it, u))
                for ch in range(NCH):
                    cols = slice(ch * CH, ch * CH + CH)
                    o = 4 * (u % 2) + 3
                    mm(ps[0:CH, o, 96 * ch:96 * ch + 32], kpq[:, u, cols], selk[:, :], start=True, stop=True)
                    last = mm(ps[0:CH, o, 96 * ch + 32:96 * ch + 96], vl[0:64, u, cols], ident[0:64, 0:64],
                              start=True, stop=True)
                last.then_inc(s_tr, 1)

            def keys_values(it, u):
                pe.wait_ge(s_vt, one_pass(it, u))
                for ch in range(NCH):
                    last = mm(bank(4 * (u % 2) + 1, 32, 65), vt[:, u, ch, 32:97], vt[:, u, ch, 0:32],
                              start=(ch == 0), stop=(ch == NCH - 1))
                last.then_inc(s_kv, 1)

            with pe.Fori(0, B) as b:
                with pe.Fori(0, J2) as j:
                    it = b * J2 + j
                    pe.wait_ge(s_kpq, before(it))
                    pe.wait_ge(s_vt, before(it))
                    pe.wait_ge(s_ob, before(b, J2 * U))
                    for u in range(U + 1):
                        if u < U:
                            statistics(it, u)
                        if u > 0:
                            logits(it, u - 1)
                        if u < U:
                            conv_kq(it, u)
                        if u > 0:
                            transposes(it, u - 1)
                        if u < U:
                            conv_vl(it, u)
                        if u > 0:
                            keys_values(it, u - 1)
                pe.wait_ge(s_kva, before(b + 1, J2 * U))
                mm(bank(0, 129, 96), kvacc[:, :], rr[:, :], start=True, stop=True).then_inc(s_mp, 1)
                with pe.Fori(0, J2) as j:
                    it = b * J2 + j
                    pe.wait_ge(s_yw, 3 * (b + 1))
                    for u in range(U):
                        pe.wait_ge(s_ob, last_turn(it, u))
                        pe.wait_ge(s_vql[u], (it + 1) * 16)
                        mm(bank(u, T, 96), dw[:, :], vq[:, u, :], start=True, stop=True).then_inc(s_d, 1)
                    for u in range(U):
                        pe.wait_ge(s_qn, one_pass(it, u))
                        mm(bank(4 + u), ycw[:, :], vq[:, u, :], start=True, stop=True).then_inc(s_yc, 1)
                    for u in range(U):
                        pe.wait_ge(s_ycs, one_pass(it, u))
                        mm(bank(u), j64[:, :], ycs[:, u, :], start=True, stop=True).then_inc(s_v2, 1)
                    for u in range(U):
                        pe.wait_ge(s_h2, one_pass(it, u))
                        mm(bank(4 + u), m1g[:, :], yc[:, u, :], start=True, stop=True).then_inc(s_m1, 1)
                    for u in range(U):
                        pe.wait_ge(s_gl, one_pass(it, u))
                        mm(bank(u), m2[:, :], gl[:, u, :], start=True, stop=False)
                        mm(bank(u), yw[:, :], vq[:, u, :], start=False, stop=True).then_inc(s_o, 1)

        @block.scalar
        def _(act):
            fn = nc.scalar.activation
            lead(act, s_xs, s_ms, s_lv, s_rs, s_kqs, s_kpq, s_ycs, s_l2, s_r2, s_gl, s_vst)
            act.wait_ge(s_w, 16 * len(loads))
            act.wait_ge(s_pd, 19)

            def squares(it, u):
                act.wait_ge(s_x[u], (it + 1) * 32)
                act.wait_ge(s_css, last_turn(it, u))
                fn(xs[:, u], xt[:, u], ACT.Square).then_inc(s_xs, 1)

            with act.Fori(0, B) as b:
                with act.Fori(0, J2) as j:
                    it = b * J2 + j
                    squares(it, 0)
                    for u in range(U):
                        base = 4 * (u % 2)
                        if u + 1 < U:
                            squares(it, u + 1)
                        act.wait_ge(s_st, one_pass(it, u))
                        fn(ms[:, u, :], bank(base + 2), ACT.Square).then_inc(s_ms, 1)
                        act.wait_ge(s_va, one_pass(it, u))
                        fn(rs[:, u, :], ms[:, u, :], ACT.Ln, bias=eps64[:, :]).then_inc(s_lv, 1)
                        act.wait_ge(s_lv, one_pass(it, u))
                        fn(rs[:, u, :], rs[:, u, :], ACT.Exp, scale=-0.5).then_inc(s_rs, 1)
                        act.wait_ge(s_kqn, one_pass(it, u))
                        fn(kq[:, u, :], kq[:, u, :], ACT.Square, bias=bkq[:, :]).then_inc(s_kqs, 1)
                        act.wait_ge(s_lg, one_pass(it, u))
                        fn(kpq[:, u, :], bank(base + 2, T, 64), ACT.Exp, bias=blq[:, :]).then_inc(s_kpq, 1)
                        act.wait_ge(s_kpq, one_pass(it, u))
                        act.dma_start(vq_spill[it * U + u, 0:64], vl[0:64, u, :]).then_inc(s_vst, 16)
                        act.dma_start(vq_spill[it * U + u, 64:96], kpq[0:32, u, :]).then_inc(s_vst, 16)
                with act.Fori(0, J2) as j:
                    it = b * J2 + j
                    for u in range(U):
                        act.wait_ge(s_ycb, one_pass(it, u))
                        fn(ycs[:, u, :], yc[:, u, :], ACT.Square).then_inc(s_ycs, 1)
                    for u in range(U):
                        act.wait_ge(s_v2, one_pass(it, u))
                        fn(rs2[:, u, :], bank(u, T, 64), ACT.Ln, bias=eps64[0:64, :]).then_inc(s_l2, 1)
                    for u in range(U):
                        act.wait_ge(s_l2, one_pass(it, u))
                        fn(rs2[:, u, :], rs2[:, u, :], ACT.Exp, scale=-0.5).then_inc(s_r2, 1)
                    for u in range(U):
                        act.wait_ge(s_m1, one_pass(it, u))
                        fn(gl[:, u, :], bank(4 + u, T, 64), ACT.Gelu, bias=m1bias[:, :]).then_inc(s_gl, 1)

        @block.vector
        def _(dve):
            tt = nc.vector.tensor_tensor
            ts = nc.vector.tensor_scalar
            cp = nc.vector.tensor_copy
            lead(dve, s_va, s_kqn, s_vln, s_vt, s_kva, s_de, s_dr, s_qn, s_ycb, s_h2, s_ob)
            dve.memset(kvacc[:, :], 0.0).then_inc(s_kvz, 1)
            dve.memset(ycw[64:96, 64:128], 0.0).then_inc(s_pd, 1)
            dve.memset(yw[64:96, 64:128], 0.0).then_inc(s_pd, 1)
            dve.memset(dw[:, :], 0.0).then_inc(s_pd, 1)
            dve.wait_ge(s_w, 16 * len(loads))
            dve.wait_ge(s_pm, 1)
            cp(wa[:, :, 192:256], ps[:, 0, 0:192].rearrange("p (j m) -> p j m", j=3)).then_inc(s_pd, 1)
            cp(wb[:, :, 192:256], ps[0:64, 1, 0:192].rearrange("p (j m) -> p j m", j=3)).then_inc(s_pd, 1)
            tt(bkq[:, :], bank(2, 1), kqb[:, :], ALU.add).then_inc(s_pd, 1)
            tt(iv[:, 64:65], bank(3, 1, 64), vb[:, :], ALU.add).then_inc(s_pd, 1)
            dve.wait_ge(s_pd, 7)
            tt(wa[:, :, :], wa[:, :, :], ga[:, :].unsqueeze(2).to_broadcast([128, 3, 256]), ALU.mult).then_inc(s_pd, 1)
            tt(wb[:, :, :], wb[:, :, :], gb[:, :].unsqueeze(2).to_broadcast([64, 3, 256]), ALU.mult).then_inc(s_pd, 1)
            tt(bvp[:, :], iv[:, 64:65], pb[:, :], ALU.add).then_inc(s_pd, 1)
            cp(prj[:, 64:128], bank(6, 64, 64)).then_inc(s_pd, 1)
            dve.wait_ge(s_pd, 11)
            dve.wait_ge(s_pm, 2)
            tt(wa[:, :, :], wa[:, :, :], bank(4, 256).unsqueeze(1).to_broadcast([128, 3, 256]),
               ALU.subtract).then_inc(s_pd, 1)
            tt(wb[:, :, :], wb[:, :, :], bank(4, 256, 64).unsqueeze(1).to_broadcast([64, 3, 256]),
               ALU.subtract).then_inc(s_pd, 1)
            cp(blq[:, :], bank(5, 1, 64)).then_inc(s_pd, 1)
            cp(by[:, :], bank(0, 1, 64)).then_inc(s_pd, 1)
            tt(bo[:, :], bvp[:, :], m2b[:, :], ALU.add).then_inc(s_pd, 1)
            cp(rr[:, 0:128], bank(1, 128, 65)).then_inc(s_pd, 1)
            ts(m1g[:, :], m1[:, :], g2[:, :], None, ALU.mult).then_inc(s_pd, 1)
            tt(m1bias[:, :], bank(7, 1, 64), m1b[:, :], ALU.add).then_inc(s_pd, 1)
            with dve.Fori(0, B) as b:
                with dve.Fori(0, J2) as j:
                    it = b * J2 + j
                    dve.wait_ge(s_kvz, b + 1)
                    for u in range(U):
                        base = 4 * (u % 2)
                        dve.wait_ge(s_ms, one_pass(it, u))
                        tt(ms[:, u, :], bank(base + 3), ms[:, u, :], ALU.subtract).then_inc(s_va, 1)
                        if u > 0:
                            dve.wait_ge(s_tr, one_pass(it, u - 1))
                            cp(vt[:, u - 1, :, 0:96], ps[0:CH, 4 * ((u - 1) % 2) + 3, 0:96 * NCH]
                               .rearrange("p (h n) -> p h n", h=NCH)).then_inc(s_vt, 1)
                        dve.wait_ge(s_rs, one_pass(it, u))
                        dve.wait_ge(s_kq, one_pass(it, u))
                        tt(kq[:, u, :], bank(base), rs[:, u, :], ALU.mult).then_inc(s_kqn, 1)
                        dve.wait_ge(s_vl, one_pass(it, u))
                        if u == 0:
                            dve.wait_ge(s_vst, before(it, U * 32))
                        tt(vl[:, u, :], bank(base + 1), rs[:, u, :], ALU.mult).then_inc(s_vln, 1)
                        if u > 0:
                            dve.wait_ge(s_kv, one_pass(it, u - 1))
                            dve.wait_ge(s_kva, one_pass(it, u - 1) - 1)
                            tt(kvacc[:, 64:96], kvacc[:, 64:96], bank(4 * ((u - 1) % 2) + 1, 32, 65),
                               ALU.add).then_inc(s_kva, 1)
                    u = U - 1
                    dve.wait_ge(s_tr, one_pass(it, u))
                    cp(vt[:, u, :, 0:96], ps[0:CH, 4 * (u % 2) + 3, 0:96 * NCH]
                       .rearrange("p (h n) -> p h n", h=NCH)).then_inc(s_vt, 1)
                    dve.wait_ge(s_kv, one_pass(it, u))
                    dve.wait_ge(s_kva, one_pass(it, u) - 1)
                    tt(kvacc[:, 64:96], kvacc[:, 64:96], bank(4 * (u % 2) + 1, 32, 65), ALU.add).then_inc(s_kva, 1)
                dve.wait_ge(s_mp, b + 1)
                ts(ycw[64:96, 0:64], ps[64:96, 0, 64:128], 1.0 / M, None, ALU.mult).then_inc(s_yw, 1)
                ts(yw[64:96, 0:64], ps[64:96, 0, 0:64], 1.0 / M, None, ALU.mult).then_inc(s_yw, 1)
                ts(kps[64:96, :], ps[64:96, 0, 128:129], 1.0 / M, None, ALU.mult).then_inc(s_kps, 1)
                dve.wait_ge(s_kps, b + 1)
                ts(dw[64:96, 64:96], ones32[64:96, :], kps[64:96, :], None, ALU.mult).then_inc(s_yw, 1)
                dve.memset(kvacc[:, 64:96], 0.0).then_inc(s_kvz, 1)
                with dve.Fori(0, J2) as j:
                    it = b * J2 + j
                    for u in range(U):
                        dve.wait_ge(s_d, one_pass(it, u))
                        ts(dn[64:96, u, :], ps[64:96, u, 0:T], D_EPS, None, ALU.add).then_inc(s_de, 1)
                        dve.wait_ge(s_de, one_pass(it, u))
                        nc.vector.reciprocal(dn[64:96, u, :], dn[64:96, u, :]).then_inc(s_dr, 1)
                        dve.wait_ge(s_dr, one_pass(it, u))
                        tt(vq[64:96, u, :], vq[64:96, u, :], dn[64:96, u, :], ALU.mult).then_inc(s_qn, 1)
                    for u in range(U):
                        dve.wait_ge(s_yc, one_pass(it, u))
                        ts(yc[:, u, :], bank(4 + u, T, 64), by[:, :], None, ALU.add).then_inc(s_ycb, 1)
                    for u in range(U):
                        dve.wait_ge(s_r2, one_pass(it, u))
                        tt(yc[:, u, :], yc[:, u, :], rs2[:, u, :], ALU.mult).then_inc(s_h2, 1)
                    for u in range(U):
                        dve.wait_ge(s_o, one_pass(it, u))
                        if u == 0:
                            dve.wait_ge(s_t2, it * (U * 16) + 16 * B)
                        ts(ob[:, u, :], bank(u, T, 64), bo[:, :], None, ALU.add).then_inc(s_ob, 1)


S3 = S2 // 2
L = S3 * S3
TR3 = T // S3
J3 = S3 // TR3
D = 768
DC = D // 128
N = 16
Q = N // 4
NX = 8
NR = 64
MT = NX * NR // 128
STEPS = Q * DC
LAG = 2


START = 8


def mark(it, per, k):
    return it * per + (START + k)


def begin(eng, *sems):
    for s in sems:
        eng.sem_inc(s, START)


def tail(nc, sem, w, c, t2, out):
    with ExitStack() as ctx:
        def sb(name, shape, dt=F32):
            return ctx.enter_context(nc.sbuf_tensor(name, shape, dt))

        ps = ctx.enter_context(nc.psum_tensor("ps3", [128, 8, 512], F32))

        def bank(k, n=T, rows=128):
            return ps[0:rows, k, 0:n]

        ident = sb("ident3", [128, 128])
        jm = sb("jm768", [128, 128])
        sel8 = sb("sel8", [NX, MT, 128])
        desc = sb("desc", [CH, NCH, NX])
        eps = sb("eps3", [128, 1])
        selbc = sb("selbc", [128, 2 * N])
        selbf = sb("selbf", [128, 2 * N], BF16)
        wpa = sb("wpa", [128, 3, D])
        wpb = sb("wpb", [64, 3, D])
        pbias = sb("pbias", [128, DC])
        wbcz = sb("wbcz", [128, DC, 128])
        bbcz = sb("bbcz", [128, 1])
        pd = sb("pd", [128, DC + 1])
        bd = sb("bd", [128, 1])
        aa = sb("aa", [128, DC, N])
        ai = sb("ai", [128, DC, N])
        enc = sb("enc", [128, DC, NR])
        encb = sb("encb", [NR, 1])
        sw = sb("sw", [NR, NX])
        swb = sb("swb", [CH, NCH, NX])
        w1 = sb("w1", [128, DC, NX * NR])
        b1 = sb("b1", [128, MT])
        w2 = sb("w2", [128, MT, D])
        b2 = sb("b2x", [NX, D])
        x3 = sb("x3", [128, TR3 + 1, S2 + 2])
        h = sb("h3", [128, 2, DC, T])
        xn = sb("xn3", [128, 2, DC, T])
        sq = sb("sq3", [128, 3, T])
        rs = sb("rs3", [128, T])
        bcs = sb("bcs", [128, T])
        split = sb("bc_split", [128, T], BF16)
        zs = sb("zs", [128, T])
        mx = sb("mx", [128, T])
        rest = mx
        delta = sb("delta", [128, DC, T])
        bcb = sb("bcb", [128, 2, 8, T])
        v = sb("v3", [128, 3, 4, T])
        a = sb("a3", [128, 2, 4, T])
        dg = sb("dg3", [128, 3, 4, 128])
        st = sb("st3", [128, 2, DC, N])
        lg = sb("lg", [CH, NCH, NX])
        ex = sb("ex", [CH, NCH, NX])
        eq = sb("eq", [CH, NCH, NX])
        m1 = sb("mx8", [CH, NCH])
        sm = sb("sm8", [CH, NCH])
        gm = sb("gm", [128, MT, T])
        ot = sb("ot", [CH, 2, D])
        xe = rs[0:NR, :]
        oh8 = bcs[0:NX, :]

        loads = [(ident, c["ident"]), (jm, c["jm768"]), (sel8, c["sel8"]), (desc, c["desc"]), (eps, c["eps64"]),
                 (selbc, c["selbc"]),
                 (wpa, w["wpa"]), (wpb, w["wpb"]), (pbias, w["pbias"]), (wbcz, w["wbcz"]), (bbcz, w["bbcz"]),
                 (pd, w["pd"]), (bd, w["bd"]), (aa, w["aa"]), (enc, w["enc"]), (encb, w["encb"]),
                 (sw, w["sw"]), (swb, w["swb"]), (w1, w["w1"]), (b1, w["b1"]), (w2, w["w2"]), (b2, w["b2"])]

        s_w = sem("t_weights_loaded")
        s_set = sem("t_buffers_set")
        s_pd = sem("t_constants_made")
        s_x = sem("t_x_loaded")
        s_pj = sem("t_projected")
        s_hw = sem("t_h_written")
        s_mean = [sem("t_mean_1"), sem("t_mean_2")]
        s_xc = [sem("t_centred_1"), sem("t_centred_2")]
        s_sq = [sem("t_squared_1"), sem("t_squared_2")]
        s_var = [sem("t_variance_1"), sem("t_variance_2")]
        s_ln = [sem("t_log_variance_1"), sem("t_log_variance_2")]
        s_rs = [sem("t_inverse_deviation_1"), sem("t_inverse_deviation_2")]
        s_xn = [sem("t_normalised_1"), sem("t_normalised_2")]
        s_z = sem("t_z_product")
        s_bc = sem("t_bc_product")
        s_zs = sem("t_z_copied")
        s_bcs = sem("t_bc_written")
        s_part = sem("t_bc_parts_written")
        s_bp = sem("t_bc_spread_product")
        s_ba = sem("t_bc_spread_written")
        s_ab = sem("t_delta_magnitude")
        s_ea = sem("t_delta_exponential")
        s_l1 = sem("t_delta_logarithm")
        s_mx = sem("t_delta_positive_part")
        s_dl = sem("t_delta_written")
        s_v = sem("t_v_written")
        s_dg = sem("t_diagonals_written")
        s_a = sem("t_decay_written")
        s_wt = sem("t_v_weighted")
        s_sc = sem("t_states_scanned")
        s_st = sem("t_last_states_kept")
        s_stz = sem("t_first_states_cleared")
        s_cm = sem("t_states_times_c")
        s_ns = sem("t_states_summed")
        s_hy = sem("t_h_updated")
        s_hm = sem("t_experts_in_product")
        s_he = sem("t_experts_in_written")
        s_gl = sem("t_experts_gelu")
        s_en = sem("t_encoded")
        s_xe = sem("t_encoding_written")
        s_lgp = sem("t_route_logits_product")
        s_r = sem("t_route_steps")
        s_rq = sem("t_route_chosen")
        s_rx = sem("t_route_exponentials")
        s_tr = sem("t_route_turned")
        s_oh = sem("t_route_copied")
        s_mk = sem("t_mask_product")
        s_gm = sem("t_experts_masked")
        s_o = sem("t_out_product")
        s_oa = sem("t_out_written")
        s_out = [sem("t_out_stored_even"), sem("t_out_stored_odd")]

        front_read = ([(s_hw, DC, dc + 1) for dc in range(DC)]
                      + [(s_xc[0], DC, DC), (s_ln[0], 1, 1), (s_bcs, 1, 1), (s_zs, 1, 1)])
        mlp_read = ([(s_xc[1], DC, DC), (s_ln[1], 1, 1), (s_xe, 1, 1), (s_he, MT, 1), (s_r, 8, 1)]
                    + [(s_he, MT, m + 1) for m in range(1, MT)] + [(s_oh, 1, 1)]
                    + [(s_gm, MT, m + 1) for m in range(MT)] + [(s_oa, 2 * NCH, i + 1) for i in range(2 * NCH)])
        F_MEAN, F_VAR, F_BC, F_Z = DC, DC + 1, DC + 2, DC + 3
        X_MEAN, X_VAR, X_ENC, X_LOG, X_TURN, X_MASK = 0, 1, 2, 4, 8, 9
        X_OUT = X_MASK + MT

        def x_in(m):
            return 3 if m == 0 else 4 + m

        def front_bank(u, i):
            return 6 + i % 2 if u == 0 else 6

        def mlp_bank(u, i):
            return 6 + i % 2 if u == 1 or i >= X_OUT else 6

        out_slot = (18, 19, 19, 20, 21, 21, 22, 23)

        def spread_rows(k, u):
            q, j = divmod(k, DC)
            if j >= 4 or (q == Q - 1 and u == 1):
                return ()
            on, q = (1, 0) if q == Q - 1 else (0, q + 1)
            return [(on, 8 * q + 2 * j), (on, 8 * q + 2 * j + 1)]

        block = ctx.enter_context(nc.Block())

        @block.sync
        def _(sp):
            for dst, src in loads:
                sp.dma_start(dst[...] if not isinstance(dst, bass.AP) else dst, src).then_inc(s_w, 16)
            sp.wait_ge(s_set, 1)
            with sp.Fori(0, B // 2) as bp:
                with sp.Fori(0, J3) as s:
                    for u in range(2):
                        it = (bp * J3 + s) * 2 + u
                        sp.wait_ge(s_pj, mark(it, DC, 0))
                        for par in range(2):
                            rows = TR3 + 1 - par
                            src = bass.AP(t2.tensor, (bp * 2 + u) * (E * T2ROWS * S2) + s * (TR3 * 2 * S2) + par * S2,
                                          [[T2ROWS * S2, E], [2 * S2, rows], [1, S2]])
                            sp.dma_start(x3[64 * par:64 * par + 64, 0:rows, 1:S2 + 1], src).then_inc(s_x, 16)

        @block.gpsimd
        def _(pool):
            tt = nc.gpsimd.tensor_tensor

            def normalise(it, u, k):
                pool.wait_ge(s_rs[k], mark(it, 1, 1))
                for dc in range(DC):
                    tt(xn[:, u, dc, :], xn[:, u, dc, :], rs[:, :], ALU.mult).then_inc(s_xn[k], 1)

            def front(it, u, k):
                if k == 16:
                    normalise(it, u, 0)

            def mlp(it, u, k):
                if k == 9:
                    normalise(it, u, 1)

            def step(it, u, k):
                q, dc = divmod(k, DC)
                if dc == 0:
                    pool.wait_ge(s_ba, mark(it, 2 * N, 8 * q + 4))
                if q == 0:
                    pool.wait_ge(s_xn[0], mark(it, DC, dc + 1))
                pool.wait_ge(s_ns, mark(it, STEPS, k - 2))
                tt(v[:, k % 3], bcb[:, q % 2, 0:4, :], xn[:, u, dc:dc + 1, :].to_broadcast([128, 4, T]),
                   ALU.mult).then_inc(s_v, 1)
                tt(dg[:, k % 3], ident[:, :].unsqueeze(1).to_broadcast([128, 4, 128]),
                   ai[:, dc, 4 * q:4 * q + 4].unsqueeze(2).to_broadcast([128, 4, 128]), ALU.mult).then_inc(s_dg, 1)

            begin(pool, *s_xn, s_v, s_dg)
            pool.memset(x3[:, :, :], 0.0).then_inc(s_set, 1)
            pool.wait_ge(s_w, 16 * len(loads))
            pool.wait_ge(s_pd, 3)
            with pool.Fori(0, B // 2) as bp:
                with pool.Fori(0, J3) as s:
                    it = (bp * J3 + s) * 2
                    for k in range(STEPS):
                        front(it, 0, k)
                    for k in range(STEPS):
                        step(it, 0, k)
                        front(it + 1, 1, k)
                    for k in range(STEPS):
                        step(it + 1, 1, k)
                        mlp(it, 0, k)
                    for k in range(STEPS):
                        mlp(it + 1, 1, k)

        @block.tensor
        def _(pe):
            mm = nc.tensor.matmul

            def mean(it, u, k, into):
                for dc in range(DC):
                    last = mm(into, jm[:, :], h[:, u, dc, :], start=(dc == 0), stop=(dc == DC - 1))
                last.then_inc(s_mean[k], 1)

            def variance(it, k, into, chunks):
                for dc in chunks:
                    pe.wait_ge(s_sq[k], mark(it, DC, dc + 1))
                    mm(into, jm[:, :], sq[:, dc % 3, :], start=(dc == 0), stop=(dc == DC - 1)).then_inc(s_var[k], 1)

            def over_chunks(into, weights, u):
                for dc in range(DC):
                    last = mm(into, weights(dc), xn[:, u, dc, :], start=(dc == 0), stop=(dc == DC - 1))
                return last

            def front_free(it, u, i):
                back = 2 if u == 0 else 1
                if i >= back:
                    s, per, k = front_read[i - back]
                    pe.wait_ge(s, mark(it, per, k))
                elif u == 0:
                    pe.wait_ge(s_oa, mark(it, 2 * NCH, 0))
                else:
                    pe.wait_ge(s_bcs, mark(it, 1, 0))
                return front_bank(u, i)

            def front(it, u, k):
                if k < DC:
                    o = front_free(it, u, k)
                    cols = slice(128 * k, 128 * k + 128)
                    if k == 0:
                        pe.wait_ge(s_x, (it + 1) * 32)
                    for j in range(3):
                        mm(bank(o), wpa[:, j, cols], x3[:, 0:TR3, j:j + 2 * S3 - 1:2], start=(j == 0), stop=False)
                    for j in range(3):
                        last = mm(bank(o), wpb[:, j, cols], x3[0:64, 1:TR3 + 1, j:j + 2 * S3 - 1:2],
                                  start=False, stop=(j == 2))
                    last.then_inc(s_pj, 1)
                if k == 7:
                    o = front_free(it, u, F_MEAN)
                    pe.wait_ge(s_hw, mark(it, DC, DC))
                    mean(it, u, 0, bank(o))
                if k == 10:
                    variance(it, 0, bank(front_free(it, u, F_VAR)), range(0, 3))
                if k == 11:
                    variance(it, 0, bank(front_bank(u, F_VAR)), range(3, DC))
                if k == 14:
                    o = front_free(it, u, F_BC)
                    pe.wait_ge(s_xn[0], mark(it, DC, DC))
                    over_chunks(bank(o), lambda dc: wbcz[:, dc, :], u).then_inc(s_bc, 1)
                if k == 15:
                    o = front_free(it, u, F_Z)
                    pe.wait_ge(s_bcs, mark(it, 1, 1))
                    mm(bank(o), ident[:, 96:97].to_broadcast([128, 128]), bcs[:, :], start=True,
                       stop=True).then_inc(s_z, 1)

            def spread(it, r):
                n = (r % 8) // 4 * N + r // 8 * 4 + r % 4
                if r == 0:
                    pe.wait_ge(s_part, mark(it, 6, 6))
                    pe.wait_ge(s_zs, mark(it, 1, 1))
                pe.wait_ge(s_ba, mark(it, 2 * N, r))
                mm(bank(7), selbf[:, n:n + 1].to_broadcast([128, 128]), split[:, :], start=True,
                   stop=True).then_inc(s_bp, 1)

            def step(it, k):
                q, dc = divmod(k, DC)
                if q == 0:
                    pe.wait_ge(s_hy, mark(it, DC, dc + 1 - DC))
                pe.wait_ge(s_dg, mark(it, STEPS, k + 1))
                pe.wait_ge(s_cm, mark(it, STEPS, k + 1))
                for n in range(4):
                    last = mm(bank(dc), dg[:, k % 3, n, :], v[:, k % 3, n, :], start=(q == 0 and n == 0),
                              stop=(q == Q - 1 and n == 3))
                last.then_inc(s_ns, 1)

            def mlp_free(it, u, i):
                back = 2 if u == 1 or i >= X_OUT else 1
                if u == 0 and i == X_OUT:
                    pe.wait_ge(s_ba, mark(it + 1, 2 * N, 2 * N))
                elif i >= back:
                    s, per, k = mlp_read[i - back]
                    pe.wait_ge(s, mark(it, per, k))
                elif u == 1:
                    pe.wait_ge(s_oa, mark(it, 2 * NCH, 0))
                else:
                    pe.wait_ge(s_zs, mark(it + 1, 1, 1))
                return mlp_bank(u, i)

            def mlp(it, u, k):
                if k == 0:
                    o = mlp_free(it, u, X_MEAN)
                    pe.wait_ge(s_hy, mark(it, DC, DC))
                    mean(it, u, 1, bank(o))
                if k == 3:
                    variance(it, 1, bank(mlp_free(it, u, X_VAR)), range(0, 3))
                if k == 4:
                    variance(it, 1, bank(mlp_bank(u, X_VAR)), range(3, DC))
                if k == 7:
                    o = mlp_free(it, u, X_ENC)
                    pe.wait_ge(s_xn[1], mark(it, DC, DC))
                    over_chunks(bank(o, T, NR), lambda dc: enc[:, dc, :], u).then_inc(s_en, 1)
                if k in (8, 10, 11, 12):
                    m = max(k - 9, 0)
                    o = mlp_free(it, u, x_in(m))
                    over_chunks(bank(o), lambda dc: w1[:, dc, 128 * m:128 * m + 128], u).then_inc(s_hm, 1)
                if k == 9:
                    o = mlp_free(it, u, X_LOG)
                    pe.wait_ge(s_xe, mark(it, 1, 1))
                    for ch in range(NCH):
                        last = mm(ps[0:CH, o, NX * ch:NX * ch + NX], xe[:, ch * CH:ch * CH + CH], sw[:, :],
                                  start=True, stop=True)
                    last.then_inc(s_lgp, 1)
                if k == 13:
                    o = mlp_free(it, u, X_TURN)
                    pe.wait_ge(s_r, mark(it, 8, 8))
                    for ch in range(NCH):
                        last = mm(ps[0:NX, o, ch * CH:ch * CH + CH], eq[:, ch, :], ident[0:CH, 0:CH],
                                  start=True, stop=True)
                    last.then_inc(s_tr, 1)
                if 14 <= k < 14 + MT:
                    m = k - 14
                    o = mlp_free(it, u, X_MASK + m)
                    pe.wait_ge(s_oh, mark(it, 1, 1))
                    mm(bank(o), sel8[:, m, :], oh8[:, :], start=True, stop=True).then_inc(s_mk, 1)
                for i in range(2 * NCH):
                    if out_slot[i] != k:
                        continue
                    ch, half = divmod(i, 2)
                    cs, lo = slice(ch * CH, ch * CH + CH), half * (D // 2)
                    o = mlp_free(it, u, X_OUT + i)
                    pe.wait_ge(s_gm, mark(it, MT, MT))
                    for m in range(MT):
                        mm(ps[0:CH, o, 0:D // 2], gm[:, m, cs], w2[:, m, lo:lo + D // 2], start=(m == 0), stop=False)
                    mm(ps[0:CH, o, 0:D // 2], oh8[:, cs], b2[:, lo:lo + D // 2], start=False, stop=False)
                    for j in range(DC // 2):
                        last = mm(ps[0:CH, o, 128 * j:128 * j + 128], h[:, u, half * (DC // 2) + j, cs],
                                  ident[:, :], start=False, stop=(j == DC // 2 - 1))
                    last.then_inc(s_o, 1)

            begin(pe, s_pj, *s_mean, *s_var, s_z, s_bc, s_bp, s_ns, s_hm, s_en, s_lgp, s_tr, s_mk, s_o)
            pe.wait_ge(s_w, 16 * len(loads))
            pe.wait_ge(s_pd, 3)
            with pe.Fori(0, B // 2) as bp:
                with pe.Fori(0, J3) as s:
                    it = (bp * J3 + s) * 2
                    for k in range(STEPS):
                        front(it, 0, k)
                    for r in range(8):
                        spread(it, r)
                    for u in range(2):
                        for k in range(STEPS):
                            rows = spread_rows(k, u)
                            for on, r in rows[0:1]:
                                spread(it + u + on, r)
                            step(it + u, k)
                            for on, r in rows[1:2]:
                                spread(it + u + on, r)
                            if u == 0:
                                front(it + 1, 1, k)
                            else:
                                mlp(it, 0, k)
                    for k in range(STEPS):
                        mlp(it + 1, 1, k)

        @block.scalar
        def _(act):
            fn = nc.scalar.activation

            def squares(it, u, k, chunks):
                for dc in chunks:
                    act.wait_ge(s_xc[k], mark(it, DC, dc + 1))
                    if dc >= 3:
                        act.wait_ge(s_var[k], mark(it, DC, dc - 2))
                    fn(sq[:, dc % 3, :], xn[:, u, dc, :], ACT.Square).then_inc(s_sq[k], 1)

            def deviation(it, k, var):
                act.wait_ge(s_var[k], mark(it, DC, DC))
                fn(rs[:, :], bank(var), ACT.Ln, bias=eps[:, :]).then_inc(s_ln[k], 1)
                act.wait_ge(s_ln[k], mark(it, 1, 1))
                fn(rs[:, :], rs[:, :], ACT.Exp, scale=-0.5).then_inc(s_rs[k], 1)

            def front(it, u, k):
                dc = k - LAG
                if 0 <= dc < DC:
                    act.wait_ge(s_pj, mark(it, DC, dc + 1))
                    fn(h[:, u, dc, :], bank(front_bank(u, dc)), ACT.Identity,
                       bias=pbias[:, dc:dc + 1]).then_inc(s_hw, 1)
                if k == 10:
                    squares(it, u, 0, range(0, 3))
                if k == 12:
                    squares(it, u, 0, range(3, DC))
                if k == 13:
                    deviation(it, 0, front_bank(u, F_VAR))
                if k == 16:
                    act.wait_ge(s_bc, mark(it, 1, 1))
                    fn(bcs[:, :], bank(front_bank(u, F_BC)), ACT.Identity, bias=bbcz[:, :]).then_inc(s_bcs, 1)
                if k == 17:
                    act.wait_ge(s_z, mark(it, 1, 1))
                    fn(zs[:, :], bank(front_bank(u, F_Z)), ACT.Copy).then_inc(s_zs, 1)

            def spread(it, r):
                q = r // 8
                act.wait_ge(s_bp, mark(it, 2 * N, r + 1))
                if r % 8 < 4:
                    act.wait_ge(s_v, mark(it, STEPS, (q - 1) * DC))
                else:
                    act.wait_ge(s_cm, mark(it, STEPS, (q - 1) * DC))
                fn(bcb[:, q % 2, r % 8, :], bank(7), ACT.Copy).then_inc(s_ba, 1)

            def softplus(it):
                act.wait_ge(s_zs, mark(it, 1, 1))
                for dc in range(DC):
                    fn(delta[:, dc, :], zs[:, :], ACT.Abs, bias=pd[:, dc:dc + 1]).then_inc(s_ab, 1)
                act.wait_ge(s_ab, mark(it, DC, DC))
                fn(delta[:, :, :], delta[:, :, :], ACT.Exp, scale=-1.0).then_inc(s_ea, 1)
                act.wait_ge(s_ea, mark(it, 1, 1))
                fn(delta[:, :, :], delta[:, :, :], ACT.Ln, bias=1.0).then_inc(s_l1, 1)

            def step(it, k):
                q, dc = divmod(k, DC)
                if q == 0:
                    act.wait_ge(s_dl, mark(it, DC, dc + 1))
                act.wait_ge(s_cm, mark(it, STEPS, k - 1))
                for n in range(4):
                    fn(a[:, k % 2, n, :], delta[:, dc, :], ACT.Exp,
                       scale=aa[:, dc, 4 * q + n:4 * q + n + 1]).then_inc(s_a, 1)

            def mlp(it, b, s, u, k):
                if k == 3:
                    squares(it, u, 1, range(0, 3))
                if k == 5:
                    squares(it, u, 1, range(3, DC))
                if k == 6:
                    deviation(it, 1, mlp_bank(u, X_VAR))
                if k == 9:
                    act.wait_ge(s_en, mark(it, 1, 1))
                    fn(xe[:, :], bank(mlp_bank(u, X_ENC), T, NR), ACT.Identity, bias=encb[:, :]).then_inc(s_xe, 1)
                if k in (10, 12, 13, 14):
                    m = max(k - 11, 0)
                    act.wait_ge(s_hm, mark(it, MT, m + 1))
                    fn(gm[:, m, :], bank(mlp_bank(u, x_in(m))), ACT.Identity, bias=b1[:, m:m + 1]).then_inc(s_he, 1)
                if k == 12:
                    act.wait_ge(s_r, mark(it, 8, 3))
                    fn(ex[:, :, :], lg[:, :, :], ACT.Exp).then_inc(s_rx, 1)
                if k == 15:
                    act.wait_ge(s_he, mark(it, MT, MT))
                    fn(gm[:, :, :], gm[:, :, :], ACT.Gelu).then_inc(s_gl, 1)
                for i in range(2 * NCH):
                    if out_slot[i] != k - LAG:
                        continue
                    ch, half = divmod(i, 2)
                    act.wait_ge(s_o, mark(it, 2 * NCH, i + 1))
                    if half == 0:
                        act.wait_ge(s_out[ch % 2], mark(it, 32, 16 * (ch // 2)))
                    fn(ot[:, ch % 2, half * (D // 2):(half + 1) * (D // 2)],
                       ps[0:CH, mlp_bank(u, X_OUT + i), 0:D // 2], ACT.Copy).then_inc(s_oa, 1)
                    if half == 1:
                        act.wait_ge(s_oa, mark(it, 2 * NCH, i + 1))
                        dst = bass.AP(out.tensor, (b + u) * (L * D) + s * (T * D) + ch * CH * D, [[D, CH], [1, D]])
                        act.dma_start(dst, ot[:, ch % 2, :]).then_inc(s_out[ch % 2], 16)

            begin(act, s_hw, *s_sq, *s_ln, *s_rs, s_bcs, s_zs, s_ba, s_ab, s_ea, s_l1, s_a, s_he, s_gl, s_xe, s_rx,
                  s_oa, *s_out)
            act.wait_ge(s_w, 16 * len(loads))
            act.wait_ge(s_pd, 3)
            with act.Fori(0, B // 2) as bp:
                with act.Fori(0, J3) as s:
                    it = (bp * J3 + s) * 2
                    for k in range(STEPS + LAG):
                        front(it, 0, k)
                    for r in range(8):
                        spread(it, r)
                    for u in range(2):
                        softplus(it + u)
                        for k in range(STEPS + LAG):
                            if k < STEPS:
                                step(it + u, k)
                            if k >= LAG:
                                for on, r in spread_rows(k - LAG, u):
                                    spread(it + u + on, r)
                            if u == 0:
                                front(it + 1, 1, k)
                            else:
                                mlp(it, bp * 2, s, 0, k)
                    for k in range(STEPS + LAG):
                        mlp(it + 1, bp * 2, s, 1, k)
            for k in range(2):
                act.wait_ge(s_out[k], mark(B * J3, 32, 0))

        @block.vector
        def _(dve):
            tt = nc.vector.tensor_tensor
            ts = nc.vector.tensor_scalar
            cp = nc.vector.tensor_copy

            def centre(it, u, k, mean):
                dve.wait_ge(s_mean[k], mark(it, 1, 1))
                for dc in range(DC):
                    tt(xn[:, u, dc, :], h[:, u, dc, :], bank(mean), ALU.subtract).then_inc(s_xc[k], 1)

            def over(a2):
                return a2.unsqueeze(2).to_broadcast([CH, NCH, NX])

            def front(it, u, k):
                if k == 9:
                    centre(it, u, 0, front_bank(u, F_MEAN))
                if k == 16:
                    mid, low = slice(32, 64), slice(64, 96)
                    dve.wait_ge(s_bcs, mark(it, 1, 1))
                    dve.wait_ge(s_bp, mark(it, 2 * N, 0))
                    cp(split[:, :], bcs[:, :]).then_inc(s_part, 1)
                    dve.wait_ge(s_part, mark(it, 6, 1))
                    tt(rest[:, :], bcs[:, :], split[:, :], ALU.subtract).then_inc(s_part, 1)
                    dve.wait_ge(s_part, mark(it, 6, 2))
                    cp(split[mid, :], rest[mid, :]).then_inc(s_part, 1)
                    cp(split[low, :], rest[low, :]).then_inc(s_part, 1)
                    dve.wait_ge(s_part, mark(it, 6, 4))
                    tt(rest[low, :], rest[low, :], split[low, :], ALU.subtract).then_inc(s_part, 1)
                    dve.wait_ge(s_part, mark(it, 6, 5))
                    cp(split[low, :], rest[low, :]).then_inc(s_part, 1)

            def softplus(it):
                dve.wait_ge(s_zs, mark(it, 1, 1))
                dve.wait_ge(s_part, mark(it, 6, 6))
                for dc in range(DC):
                    dve.wait_ge(s_dl, mark(it, DC, dc))
                    ts(mx[:, :], zs[:, :], pd[:, dc:dc + 1], 0.0, ALU.add, ALU.max).then_inc(s_mx, 1)
                    dve.wait_ge(s_mx, mark(it, DC, dc + 1))
                    dve.wait_ge(s_l1, mark(it, 1, 1))
                    tt(delta[:, dc, :], mx[:, :], delta[:, dc, :], ALU.add).then_inc(s_dl, 1)

            def step(it, u, k):
                q, dc = divmod(k, DC)
                dve.wait_ge(s_v, mark(it, STEPS, k + 1))
                for n in range(4):
                    dve.wait_ge(s_a, mark(it, 4 * STEPS, 4 * k + n + 1))
                    nc.vector.scalar_tensor_tensor(v[:, k % 3, n, :], a[:, k % 2, n, :],
                                                   aa[:, dc, 4 * q + n:4 * q + n + 1], v[:, k % 3, n, :],
                                                   ALU.subtract, ALU.mult).then_inc(s_wt, 1)
                if k == 0:
                    dve.wait_ge(s_st, mark(it, STEPS, 0))
                for n in range(4):
                    dve.wait_ge(s_wt, mark(it, 4 * STEPS, 4 * k + n + 1))
                    nc.vector.tensor_tensor_scan(a[:, k % 2, n, :], a[:, k % 2, n, :], v[:, k % 3, n, :],
                                                 st[:, u, dc, 4 * q + n:4 * q + n + 1], ALU.mult,
                                                 ALU.add).then_inc(s_sc, 1)
                dve.wait_ge(s_sc, mark(it, 4 * STEPS, 4 * k + 4))
                cp(st[:, u, dc, 4 * q:4 * q + 4], a[:, k % 2, :, T - 1]).then_inc(s_st, 1)
                if dc == 0:
                    dve.wait_ge(s_ba, mark(it, 2 * N, 8 * q + 8))
                tt(v[:, k % 3], a[:, k % 2], bcb[:, q % 2, 4:8, :], ALU.mult).then_inc(s_cm, 1)

            def add_to_h(it, u, dc):
                dve.wait_ge(s_ns, mark(it, STEPS, STEPS - DC + dc + 1))
                tt(h[:, u, dc, :], h[:, u, dc, :], bank(dc), ALU.add).then_inc(s_hy, 1)

            def mlp(it, u, k):
                if k == 2:
                    centre(it, u, 1, mlp_bank(u, X_MEAN))
                if k == 11:
                    dve.wait_ge(s_lgp, mark(it, 1, 1))
                    tt(lg[:, :, :], ps[0:CH, mlp_bank(u, X_LOG), 0:NCH * NX].rearrange("p (h e) -> p h e", e=NX),
                       swb[:, :, :], ALU.add).then_inc(s_r, 1)
                    dve.wait_ge(s_r, mark(it, 8, 1))
                    nc.vector.reduce_max(m1[:, :], lg[:, :, :], mybir.AxisListType.X).then_inc(s_r, 1)
                    dve.wait_ge(s_r, mark(it, 8, 2))
                    tt(lg[:, :, :], lg[:, :, :], over(m1[:, :]), ALU.subtract).then_inc(s_r, 1)
                if k == 12:
                    dve.wait_ge(s_r, mark(it, 8, 3))
                    nc.vector.scalar_tensor_tensor(eq[:, :, :], lg[:, :, :], 0.0, desc[:, :, :], ALU.is_equal,
                                                   ALU.mult).then_inc(s_r, 1)
                    dve.wait_ge(s_r, mark(it, 8, 4))
                    nc.vector.reduce_max(m1[:, :], eq[:, :, :], mybir.AxisListType.X).then_inc(s_r, 1)
                    dve.wait_ge(s_rx, mark(it, 1, 1))
                    nc.vector.reduce_sum(sm[:, :], ex[:, :, :], mybir.AxisListType.X).then_inc(s_r, 1)
                    dve.wait_ge(s_r, mark(it, 8, 6))
                    tt(eq[:, :, :], eq[:, :, :], over(m1[:, :]), ALU.is_equal).then_inc(s_rq, 1)
                    nc.vector.reciprocal(sm[:, :], sm[:, :]).then_inc(s_r, 1)
                    dve.wait_ge(s_r, mark(it, 8, 7))
                    dve.wait_ge(s_rq, mark(it, 1, 1))
                    tt(eq[:, :, :], eq[:, :, :], over(sm[:, :]), ALU.mult).then_inc(s_r, 1)
                if k == 14:
                    dve.wait_ge(s_tr, mark(it, 1, 1))
                    cp(oh8[:, :], bank(mlp_bank(u, X_TURN), T, NX)).then_inc(s_oh, 1)
                if 15 <= k < 15 + MT:
                    m = k - 15
                    dve.wait_ge(s_gl, mark(it, 1, 1))
                    dve.wait_ge(s_mk, mark(it, MT, m + 1))
                    tt(gm[:, m, :], gm[:, m, :], bank(mlp_bank(u, X_MASK + m)), ALU.mult).then_inc(s_gm, 1)

            begin(dve, *s_xc, s_part, s_mx, s_dl, s_wt, s_sc, s_st, s_cm, s_hy, s_r, s_rq, s_oh, s_gm)
            dve.wait_ge(s_w, 16 * len(loads))
            nc.vector.reciprocal(ai[:, :, :], aa[:, :, :]).then_inc(s_pd, 1)
            ts(pd[:, :], pd[:, :], bd[:, :], None, ALU.add).then_inc(s_pd, 1)
            cp(selbf[:, :], selbc[:, :]).then_inc(s_pd, 1)
            dve.wait_ge(s_pd, 3)
            with dve.Fori(0, B // 2) as bp:
                dve.wait_ge(s_st, mark(bp, 2 * J3 * STEPS, 0))
                dve.memset(st[:, :, :, :], 0.0).then_inc(s_stz, 1)
                with dve.Fori(0, J3) as s:
                    it = (bp * J3 + s) * 2
                    dve.wait_ge(s_stz, bp + 1)
                    for k in range(STEPS):
                        front(it, 0, k)
                    for u in range(2):
                        softplus(it + u)
                        for k in range(STEPS):
                            step(it + u, u, k)
                            if k >= STEPS - DC + 2:
                                add_to_h(it + u, u, k - (STEPS - DC + 2))
                            if u == 0:
                                front(it + 1, 1, k)
                            else:
                                mlp(it, 0, k)
                        for dc in range(DC - 2, DC):
                            add_to_h(it + u, u, dc)
                    for k in range(STEPS):
                        mlp(it + 1, 1, k)


def build(nc, w, c, out):
    t1 = nc.dram_tensor("tokens1", (B, E, T1ROWS, IMG), F32, kind="Internal").ap()
    t2 = nc.dram_tensor("tokens2", (B, E, T2ROWS, S2), F32, kind="Internal").ap()
    h_spill = nc.dram_tensor("h_spill", (B * J1 * U, 128, T), F32, kind="Internal").ap()
    vq_spill = nc.dram_tensor("vq_spill", (B * J2 * U, 96, T), F32, kind="Internal").ap()
    stages = (lambda sem: performer1(nc, sem, w["x"], w, c, t1, h_spill),
              lambda sem: performer2(nc, sem, w, c, t1, vq_spill, t2),
              lambda sem: tail(nc, sem, w, c, t2, out))
    for stage in stages:
        sems = []

        def sem(name):
            sems.append(nc.alloc_semaphore(name))
            return sems[-1]

        stage(sem)
        nc.clear_and_free_semaphores(sems)
        nc.all_engine_barrier()


def shape_constants():
    f = np.float32
    c = {}
    c["ident"] = np.eye(128, dtype=f)
    g32 = np.arange(128) // 32
    r32 = np.arange(128) % 32
    same = g32[:, None] == g32[None, :]
    c["bd32"] = same.astype(f)
    c["srep"] = (r32[:, None] == r32[None, :]).astype(f)
    inside = same & (r32 < F1)[:, None] & (r32 < F1)[None, :]
    c["cen1"] = (np.eye(128) * (r32 <= F1) - inside / F1).astype(f)
    c["mean27"] = (inside / F1).astype(f)
    g64 = np.arange(128) // 64
    c["jb64"] = ((g64[:, None] == g64[None, :]) / E).astype(f)
    pm = np.zeros((128, 2, 2, 64), f)
    nh = np.zeros((128, 2, 128), f)
    for g in range(G):
        pm[32 * g:32 * g + 32, g // 2, g % 2] = 1
        nh[64 * (g % 2):64 * (g % 2) + 64, g // 2, 32 * g:32 * g + 32] = -0.5
    c["pmask"], c["nh"] = pm, nh
    c["eps1"] = np.where(r32 == F1, 1.0, LN_EPS).astype(f)[:, None]
    c["eps64"] = np.full((128, 1), LN_EPS, f)
    c["ic64"] = np.concatenate([np.eye(E), np.eye(E) - 1.0 / E], 1).astype(f)
    c["e27col"] = (r32 == F1).astype(f)[:, None]
    c["e27"] = c["e27col"].T.copy()
    c["ones576"] = np.full((128, 128), 1.0 / (9 * E), f)
    i32 = np.arange(32)
    c["sel2"] = np.zeros((128, 64), f)
    c["sel2"][:64, 32:] = c["sel2"][64:, :32] = -0.5
    c["seli"] = np.zeros((128, 64), f)
    c["seli"][64 + np.arange(64), np.arange(64)] = 1
    c["selk"] = np.zeros((64, 32), f)
    c["selk"][32 + i32, i32] = 1
    c["j64"] = np.full((64, 128), 1.0 / E, f)
    c["c64"] = (np.eye(64) - 1.0 / E).astype(f)
    c["c64pad"] = np.pad(c["c64"], ((0, 0), (0, 64)))
    c["i64pad"] = np.eye(64, 128, dtype=f)
    c["last65"] = (np.arange(65) == 64).astype(f)[:, None]
    c["jm768"] = np.full((128, 128), 1.0 / D, f)
    c["sel8"] = (np.arange(NX * NR).reshape(1, MT, 128) // NR == np.arange(NX)[:, None, None]).astype(f)
    c["selbc"] = np.zeros((128, 2 * N), f)
    c["selbc"][:96] = np.tile(np.eye(2 * N), (3, 1))
    c["desc"] = np.tile(np.arange(NX, 0, -1, dtype=f), (CH, NCH, 1))
    return c


def by_parity(a):
    a = np.moveaxis(a, -3, 0)
    a = np.moveaxis(a, (-2, -1), (0, 2))
    return a[0:2].reshape((2 * E,) + a.shape[2:]), a[2]


def layouts(a):
    f = np.float32
    w = {}
    xp = np.zeros((B, 3, XROWS, XP), f)
    xp[:, :, 1:IMG + 1, 1:IMG + 1] = a["x"]
    w["x"] = xp
    t = {k[len("L0_tok_"):]: v for k, v in a.items() if k.startswith("L0_tok_")}
    gain = np.zeros((32, 32), f)
    gain[np.arange(F1), np.arange(F1)] = t["p1_n1_g"]
    gain[:F1, F1] = t["p1_n1_b"]
    gain[F1, F1] = 1
    w["gain1"] = np.tile(gain, (1, G))
    wt = np.zeros((32, 192), f)
    wt[:F1] = t["p1_kqv_w"].T
    wt[F1] = t["p1_kqv_b"]
    w["wt1"] = wt
    w["pb1"] = t["p1_proj_b"][None]
    w["pw1"] = t["p1_proj_w"]
    w["pwt1"] = t["p1_proj_w"].T
    w["wfeat1"] = t["p1_w"].T
    for name in ("m1", "m2"):
        bd = np.zeros((128, 128), f)
        bd[:64, :64] = bd[64:, 64:] = t[f"p1_{name}_w"].T
        w[f"{name}bd1"] = bd
    for name, key in (("g21", "n2_g"), ("b21", "n2_b"), ("m1b1", "m1_b"), ("m2b1", "m2_b")):
        w[name] = np.tile(t["p1_" + key], 2)[:, None]
    taps = t["p2_kqv_w"].reshape(192, E, 3, 3)
    w["wa2"], w["wb2"] = by_parity(taps)
    w["wn2"] = taps[:128].reshape(2, E, E, 3, 3).transpose(1, 0, 4, 3, 2).reshape(E, 2, 9 * E)
    w["ga2"], w["gb2"] = by_parity(t["p2_n1_g"].reshape(E, 3, 3))
    w["ba2"], w["bb2"] = by_parity(t["p2_n1_b"].reshape(E, 3, 3))
    w["wfeat2"] = t["p2_w"].T
    w["wsel2"] = np.zeros((128, 64), f)
    w["wsel2"][:64, 32:] = w["wsel2"][64:, :32] = t["p2_w"].T
    w["kqb2"], w["vb2"] = t["p2_kqv_b"][:128, None], t["p2_kqv_b"][128:, None]
    w["pb2"], w["pw2"], w["pwt2"] = t["p2_proj_b"][:, None], t["p2_proj_w"], t["p2_proj_w"].T
    w["m1t2"], w["m2t2"] = (np.pad(t[f"p2_{k}_w"].T, ((0, 0), (0, 64))) for k in ("m1", "m2"))
    w["g22"], w["b22"] = t["p2_n2_g"][:, None], t["p2_n2_b"][:, None]
    w["m1b2"], w["m2b2"] = t["p2_m1_b"][:, None], t["p2_m2_b"][:, None]


    def chunks(m):
        return m.reshape((-1, 128) + m.shape[1:]).swapaxes(0, 1)

    w["wpa"], w["wpb"] = by_parity(t["proj_w"].reshape(D, E, 3, 3))
    w["pbias"] = chunks(t["proj_b"])
    s = {k[len("L0_attn_"):]: v for k, v in a.items() if k.startswith("L0_attn_")}
    w["wbcz"] = chunks(np.concatenate([s["W_B"], s["W_C"]] * 3 + [s["W_D"], np.zeros((D, 31), f)], 1))
    w["bbcz"] = np.concatenate([s["b_B"], s["b_C"]] * 3 + [np.zeros(32, f)])[:, None]
    w["pd"] = np.pad(chunks(s["p_Delta"]), ((0, 0), (0, 1)))
    w["bd"] = np.tile(s["b_D"], 128)[:, None]
    w["aa"] = chunks(s["A"])
    r = {k[len("L0_ffn_"):]: v for k, v in a.items() if k.startswith("L0_ffn_")}
    w["enc"], w["encb"] = chunks(r["enc_w"]), r["enc_b"][:, None]
    w["sw"], w["swb"] = r["sw_w"], np.tile(r["sw_b"], (CH, NCH, 1))
    w["w1"] = chunks(r["w1"].transpose(1, 0, 2).reshape(D, NX * NR))
    w["b1"] = chunks(r["b1"].reshape(-1))
    w["w2"] = chunks(r["w2"].reshape(NX * NR, D))
    w["b2"] = r["b2"]
    return w


def kernel(**inputs):
    import concourse.bacc as bacc
    from concourse.bass_utils import run_bass_kernel_spmd

    nc = bacc.Bacc("TRN2", target_bir_lowering=False, num_devices=1)
    arrays, w, c = {}, {}, {}
    host = layouts({k: np.asarray(v) for k, v in inputs.items()})
    for group, into in ((host, w), (shape_constants(), c)):
        for name, a in group.items():
            a = np.ascontiguousarray(a)
            arrays["in_" + name] = a
            into[name] = nc.dram_tensor("in_" + name, a.shape, F32, kind="ExternalInput").ap()
    out = nc.dram_tensor("out", (B, 3136, 768), F32, kind="ExternalOutput").ap()
    build(nc, w, c, out)
    r = run_bass_kernel_spmd(nc, [arrays], core_ids=[0])
    return r.results[0]["out"]
```
